# Optimizing a Trainium2 kernel written in Bass

```python
import numpy as np
import jax
import jax.numpy as jnp

def _softmax(x, axis=-1):
    return jax.nn.softmax(x, axis=axis)
def _gelu(x):
    return jax.nn.gelu(x, approximate=True)
def _silu(x):
    return jax.nn.silu(x)
def _sigmoid(x):
    return jax.nn.sigmoid(x)
def _layernorm(x, axis=-1, eps=1e-5):
    m = jnp.mean(x, axis=axis, keepdims=True)
    v = jnp.var(x, axis=axis, keepdims=True)
    return (x - m) / jnp.sqrt(v + eps)
def _scatter_add(tgt, idx, src, axis=0):
    return tgt.at[idx].add(src)
def _segment_sum(src, seg, n):
    return jax.ops.segment_sum(src, seg, n)

kernel_name = 'mk_adj_preln_d2_adj_512_d3a94c'

def setup_inputs(seed: int = 0):
    np.random.seed(seed)
    _w = jnp.asarray
    def _rec_inputs():
        import jax
        import jax.numpy as jnp
        _gk = jax.random.key(seed)
        x = -0.0002928 + 1 * jax.random.normal(jax.random.fold_in(_gk, 1), (128, 128, 512), jnp.float32)
        _a = jax.random.bernoulli(jax.random.fold_in(_gk, 2), 0.125, (128, 128, 128))
        _a = jnp.logical_or(_a, jnp.swapaxes(_a, -1, -2))
        adj = _a
        return x, adj
    x, adj = _rec_inputs()
    def _L0_gnn_setup():
        import jax, jax.numpy as jnp
        import numpy as np
        HEAD_NUM = 8
        THRESHOLD = 0.1
        NEG = -10000000000.0
        COS_EPS = 1e-08
        B, S, D = (8, 1024, 512)
        D_OUT = 512
        key = jax.random.key(seed)
        ks = jax.random.split(key, 12)
        embs = jax.random.normal(ks[0], (B, S, D), dtype=jnp.float32)
        lengths = jax.random.randint(ks[1], (B,), S // 2, S + 1)
        pad = jnp.arange(S)[None, :] >= lengths[:, None]
        score_mask = pad[:, :, None] | pad[:, None, :]
        sc = 1.0 / np.sqrt(D)
        mk = lambda k, shp: jax.random.normal(k, shp, dtype=jnp.float32) * sc
        return {'embs': embs, 'score_mask': score_mask, 'map_w': mk(ks[2], (D, D)), 'map_b': jnp.zeros((D,), jnp.float32), 'q_w': mk(ks[3], (D, D)), 'q_b': jnp.zeros((D,), jnp.float32), 'k_w': mk(ks[4], (D, D)), 'k_b': jnp.zeros((D,), jnp.float32), 'gcn_map_w': mk(ks[5], (D_OUT, D)), 'gcn_map_b': jnp.zeros((D_OUT,), jnp.float32), 'gcn_W': jax.random.normal(ks[6], (D_OUT // HEAD_NUM, D_OUT // HEAD_NUM), dtype=jnp.float32) * (1.0 / np.sqrt(D_OUT // HEAD_NUM))}
    _L0_gnn_all = _L0_gnn_setup()
    _L0_gnn_in = {k: v for k, v in _L0_gnn_all.items() if k in ('map_w', 'map_b', 'q_w', 'q_b', 'k_w', 'k_b', 'gcn_map_w', 'gcn_map_b', 'gcn_W', )}
    del _L0_gnn_all

    def _L1_gnn_setup():
        import jax, jax.numpy as jnp
        import numpy as np
        QUERY_DIM = 512
        HEADS = 4
        DIM_HEAD = 64
        INNER = HEADS * DIM_HEAD
        B, N = (4, 2048)
        key = jax.random.key(seed)
        ks = jax.random.split(key, 6)
        s = 1.0 / np.sqrt(QUERY_DIM)
        x = jax.random.normal(ks[0], (B, N, QUERY_DIM), dtype=jnp.float32)
        adjacency_mask = jax.random.randint(ks[1], (B, N, N), 0, 2) > 0
        Wq = jax.random.normal(ks[2], (QUERY_DIM, INNER), dtype=jnp.float32) * s
        Wk = jax.random.normal(ks[3], (QUERY_DIM, INNER), dtype=jnp.float32) * s
        Wv = jax.random.normal(ks[4], (QUERY_DIM, INNER), dtype=jnp.float32) * s
        Wo = jax.random.normal(ks[5], (INNER, QUERY_DIM), dtype=jnp.float32) * (1.0 / np.sqrt(INNER))
        bo = jnp.zeros((QUERY_DIM,), dtype=jnp.float32)
        return {'x': x, 'adjacency_mask': adjacency_mask, 'Wq': Wq, 'Wk': Wk, 'Wv': Wv, 'Wo': Wo, 'bo': bo}
    _L1_gnn_all = _L1_gnn_setup()
    _L1_gnn_in = {k: v for k, v in _L1_gnn_all.items() if k in ('Wq', 'Wk', 'Wv', 'Wo', 'bo', )}
    del _L1_gnn_all

    return {
        "x": x,
        "adj": adj,
        "L0_gnn_map_w": _L0_gnn_in["map_w"],
        "L0_gnn_map_b": _L0_gnn_in["map_b"],
        "L0_gnn_q_w": _L0_gnn_in["q_w"],
        "L0_gnn_q_b": _L0_gnn_in["q_b"],
        "L0_gnn_k_w": _L0_gnn_in["k_w"],
        "L0_gnn_k_b": _L0_gnn_in["k_b"],
        "L0_gnn_gcn_map_w": _L0_gnn_in["gcn_map_w"],
        "L0_gnn_gcn_map_b": _L0_gnn_in["gcn_map_b"],
        "L0_gnn_gcn_W": _L0_gnn_in["gcn_W"],
        "L1_gnn_Wq": _L1_gnn_in["Wq"],
        "L1_gnn_Wk": _L1_gnn_in["Wk"],
        "L1_gnn_Wv": _L1_gnn_in["Wv"],
        "L1_gnn_Wo": _L1_gnn_in["Wo"],
        "L1_gnn_bo": _L1_gnn_in["bo"],
    }

def reference(x, adj, L0_gnn_map_w, L0_gnn_map_b, L0_gnn_q_w, L0_gnn_q_b, L0_gnn_k_w, L0_gnn_k_b, L0_gnn_gcn_map_w, L0_gnn_gcn_map_b, L0_gnn_gcn_W, L1_gnn_Wq, L1_gnn_Wk, L1_gnn_Wv, L1_gnn_Wo, L1_gnn_bo):
    import jax
    import jax.numpy as jnp
    def _L0_gnn_ref(embs, score_mask, map_w, map_b, q_w, q_b, k_w, k_b, gcn_map_w, gcn_map_b, gcn_W):
        import jax, jax.numpy as jnp
        import numpy as np
        HEAD_NUM = 8
        THRESHOLD = 0.1
        NEG = -10000000000.0
        COS_EPS = 1e-08
        B, S, D = (8, 1024, 512)
        D_OUT = 512
        b, s, d = embs.shape
        h, dk = (HEAD_NUM, d // HEAD_NUM)
        sm = score_mask[:, None, :, :]
        keep = (~sm[..., 0:1]).astype(embs.dtype)
        m = embs @ map_w.T + map_b
        sem = m.reshape(b, s, h, dk).transpose(0, 2, 1, 3)
        norm = jnp.maximum(jnp.linalg.norm(sem, axis=-1, keepdims=True), COS_EPS)
        n = sem / norm
        cos = jnp.einsum('bhsd,bhtd->bhst', n, n)
        cos = cos * (~sm).astype(cos.dtype)
        cos_adj = (cos > THRESHOLD).astype(embs.dtype)
        q = (m @ q_w.T + q_b).reshape(b, s, h, dk).transpose(0, 2, 1, 3)
        k = (m @ k_w.T + k_b).reshape(b, s, h, dk).transpose(0, 2, 1, 3)
        scores = jnp.einsum('bhsd,bhtd->bhst', q, k) / jnp.sqrt(jnp.asarray(dk, embs.dtype))
        scores = jnp.where(sm, NEG, scores)
        p_attn = jax.nn.softmax(scores, axis=-1) * keep
        adj = cos_adj * p_attn
        hk = gcn_map_w.shape[0] // h
        sem_h = (embs @ gcn_map_w.T + gcn_map_b).reshape(b, s, h, hk).transpose(2, 0, 1, 3)
        adj_h = adj.transpose(1, 0, 2, 3)
        Ax = jnp.einsum('hbst,hbtd->hbsd', adj_h, sem_h)
        AxW = Ax @ gcn_W.T
        denom = adj_h.sum(-1, keepdims=True) + 1.0
        out = jax.nn.relu(AxW / denom)
        out = out.transpose(1, 2, 0, 3).reshape(b, s, h * hk)
        return out

    def _L1_gnn_ref(x, adjacency_mask, Wq, Wk, Wv, Wo, bo):
        import jax, jax.numpy as jnp
        import numpy as np
        QUERY_DIM = 512
        HEADS = 4
        DIM_HEAD = 64
        INNER = HEADS * DIM_HEAD
        B, N = (4, 2048)
        scale = DIM_HEAD ** (-0.5)

        def split_heads(t):
            b, n, _ = t.shape
            return t.reshape(b, n, HEADS, DIM_HEAD).transpose(0, 2, 1, 3)
        q = split_heads(x @ Wq)
        k = split_heads(x @ Wk)
        v = split_heads(x @ Wv)
        sim = jnp.einsum('bhid,bhjd->bhij', q, k) * scale
        neg = -jnp.finfo(sim.dtype).max
        sim = jnp.where(adjacency_mask[:, None, :, :], sim, neg)
        attn = jax.nn.softmax(sim, axis=-1)
        out = jnp.einsum('bhij,bhjd->bhid', attn, v)
        out = out.transpose(0, 2, 1, 3).reshape(x.shape[0], x.shape[1], INNER)
        return out @ Wo + bo

    h = jnp.maximum(_layernorm(x, axis=-1), 0.0)
    x = x + _L0_gnn_ref(h, adj, L0_gnn_map_w, L0_gnn_map_b, L0_gnn_q_w, L0_gnn_q_b, L0_gnn_k_w, L0_gnn_k_b, L0_gnn_gcn_map_w, L0_gnn_gcn_map_b, L0_gnn_gcn_W)
    h = jnp.maximum(_layernorm(x, axis=-1), 0.0)
    x = x + _L1_gnn_ref(h, adj, L1_gnn_Wq, L1_gnn_Wk, L1_gnn_Wv, L1_gnn_Wo, L1_gnn_bo)
    return x


_drawn_inputs = setup_inputs


def setup_inputs(seed=0):
    import zlib

    import numpy as np

    out = dict(_drawn_inputs(seed))
    spreads = {'L0_gnn_map_b': (0.0, 0.8),
     'L0_gnn_q_b': (0.0, 0.8),
     'L0_gnn_k_b': (0.0, 0.8),
     'L0_gnn_gcn_map_b': (0.0, 0.295),
     'L1_gnn_bo': (0.0, 0.1)}
    factors = {'L0_gnn_map_w': 6.078, 'L0_gnn_q_w': 7.426, 'L0_gnn_k_w': 7.44}
    for name, (base, spread) in spreads.items():
        noise = np.random.default_rng([zlib.crc32(name.encode()), seed]).standard_normal(out[name].shape)
        drawn = base * np.exp(spread * noise) if base else spread * noise
        out[name] = jnp.asarray(drawn.astype(out[name].dtype))
    for name, factor in factors.items():
        out[name] = (out[name] * factor).astype(out[name].dtype)
    return out
```

```python
from contextlib import ExitStack

import numpy as np

import concourse.bass as bass
from concourse import mybir
from concourse.alu_op_type import AluOpType as ALU

ACT = mybir.ActivationFunctionType
AX_X = mybir.AxisListType.X
F32 = mybir.dt.float32
F32R = mybir.dt.float32r
BF16 = mybir.dt.bfloat16
I32 = mybir.dt.int32
U8 = mybir.dt.uint8

P = 128
B, D = 128, 512
KT = D // P
QUAD = 4
GROUPS = B // QUAD
DH = 64
H0, H1 = 8, 4
PAIRS0, PAIRS1 = H0 // 2, H1 // 2
INNER = H1 * DH
HB = 4
VW = DH + 2
VROW = H0 * VW + 32
NV = 96
THRESHOLD = 0.1
SCALE = DH ** -0.5
LN_EPS = 1e-5
NORM_EPS2 = 1e-16
NEG0 = -1e10 / SCALE
NEG1 = -3.3895e38
RSQRT_SEED = 1597463007.0
NEWTON = 3
LN_OPS = 5 + 3 * NEWTON
NORM_OPS = 4 + 3 * NEWTON
BASE = 2


def count(n):
    return BASE + n


def wait_apart(eng, sem, n, passed):
    eng.wait_ge(sem, n)
    eng.sem_inc(passed, 1)


def rsqrt_steps(nc, link, y, v, a):
    link(nc.vector.tensor_scalar(y.bitcast(I32), v.bitcast(I32), -0.5, RSQRT_SEED, ALU.mult, ALU.add))
    for _ in range(NEWTON):
        link(nc.vector.scalar_tensor_tensor(a, y, -0.5, y, ALU.mult, ALU.mult))
        link(nc.vector.tensor_tensor(a, a, v, ALU.mult))
        link(nc.vector.scalar_tensor_tensor(y, a, 1.5, y, ALU.add, ALU.mult))


def layer_norm_stats(nc, dve, ln_chain, passed, first, x, st, rstd, nbias):
    done = [0]

    def link(ins):
        ins.then_inc(ln_chain, 1)
        done[0] += 1
        if done[0] == 1:
            wait_apart(dve, ln_chain, first + 1, passed)
        elif done[0] < LN_OPS:
            dve.wait_ge(ln_chain, first + done[0])

    stats, mv, var, a = st[:, 0:6], st[:, 6:8], st[:, 8:9], st[:, 9:10]
    link(nc.vector.bn_stats(stats, x))
    link(nc.vector.bn_aggr(mv, stats))
    link(nc.vector.tensor_scalar(var, mv[:, 1:2], LN_EPS, None, ALU.add))
    rsqrt_steps(nc, link, rstd, var, a)
    link(nc.vector.scalar_tensor_tensor(nbias, mv[:, 0:1], -1.0, rstd, ALU.mult, ALU.mult))
    assert done[0] == LN_OPS


def rounds(eng, body):
    with eng.Fori(0, GROUPS // 2 - 1) as i:
        body(i, 0, True, True)
        body(i, 1, True, True)
    body(GROUPS // 2 - 1, 0, True, False)
    body(GROUPS // 2 - 1, 1, False, False)


def split_products(pe, out, lhs_hi, lhs_lo, rhs_hi, rhs_lo, kts):
    last = None
    n = 0
    for kt in range(kts):
        for a, b in ((lhs_hi, rhs_hi), (lhs_hi, rhs_lo), (lhs_lo, rhs_hi)):
            last = pe.matmul(out, a(kt), b(kt), start=(n == 0), stop=(n == 3 * kts - 1))
            n += 1
    return last


def identities(nc, pool, ident, negi, neg, s_ident):
    nc.gpsimd.memset(ident[:], 0.0)
    nc.gpsimd.memset(negi[:], 0.0).then_inc(s_ident, 1)
    pool.wait_ge(s_ident, 1)
    nc.gpsimd.affine_select(out=ident[:], in_=ident[:], compare_op=ALU.not_equal, fill=1.0, base=0,
                            pattern=[[-1, P]], channel_multiplier=1)
    nc.gpsimd.affine_select(out=negi[:], in_=negi[:], compare_op=ALU.not_equal, fill=neg, base=0,
                            pattern=[[-1, P]], channel_multiplier=1).then_inc(s_ident, 1)


def layer0(nc, x, adj, map_w, map_wT, map_b, q_wT, q_b, k_wT, k_b, gmap_w, gmap_b, gcn_WT, x1):
    with ExitStack() as ctx:
        def sb(name, shape, dt=F32):
            return ctx.enter_context(nc.sbuf_tensor(name, shape, dt))

        def bank(name):
            return ctx.enter_context(nc.psum_tensor(name, [P, 512], F32))

        def sem(name):
            return ctx.enter_context(nc.semaphore(name))

        w_hi = {k: sb(f"w{k}_hi", [P, KT, D], F32R) for k in "qkmv"}
        w_lo = {k: sb(f"w{k}_lo", [P, KT, D], F32R) for k in "qkmv"}
        ident = sb("ident", [P, P])
        negi = sb("negi", [P, P], BF16)
        mb = sb("mb", [P, D])
        vb = sb("vb", [P, D])
        qb = sb("qb", [P, KT])
        kb = sb("kb", [P, KT])
        bcols = sb("bcols", [P, 4, KT])
        qk = sb("qk", [P, 2 * KT * D + 2 * KT * 2 * D])
        q_sb = qk[:, 0:2 * KT * D].rearrange("p (g b n) -> p g b n", g=2, b=KT)
        k_bd = qk[:, 2 * KT * D:].rearrange("p (g b s n) -> p g b s n", g=2, b=KT, s=2)
        raw = [qk[:, n * KT * D:(n + 1) * KT * D].rearrange("p (k n) -> p k n", k=KT) for n in range(5)]
        raw_mapT, raw_map, raw_q, raw_k, raw_g = raw
        gw_bd = qk[:, 5 * KT * D:5 * KT * D + P]
        gb_rows = qk[:, 5 * KT * D + P:5 * KT * D + P + KT * P].rearrange("p (k n) -> p k n", k=KT)
        hT_hi = sb("hT_hi", [P, KT, QUAD * P], F32R)
        hT_lo = sb("hT_lo", [P, KT, QUAD * P], F32R)
        xg = sb("xg", [P, QUAD, D])
        h = sb("h", [P, 2, D])
        ln_st = sb("ln_st", [P, QUAD, 12])
        m_sb = sb("m_sb", [P, QUAD, D])
        sq = sb("sq", [P, D])
        norm_st = sb("norm_st", [P, 3, H0])
        nT = sb("nT", [P, 2, KT, P])
        nT_bd = sb("nT_bd", [P, 2, KT, 2, P])
        v_sb = sb("v_sb", [P, QUAD + 1, VROW])
        mask_u8 = sb("mask_u8", [P, 2, QUAD, P], U8)
        mask = sb("mask", [P, 2, QUAD, P], BF16)
        keep = sb("keep", [P, 2, QUAD])
        negmax = sb("negmax", [P, 2, HB])
        zsum = sb("zsum", [P, 2, HB])
        probs = sb("probs", [P, HB, P])
        cprobs = sb("cprobs", [P, HB, P])
        cpT = sb("cpT", [P, HB, P])
        epi_st = sb("epi_st", [P, 3, HB])
        xres = sb("xres", [P, 2, D])
        o_sb = sb("o_sb", [P, 2, D])

        ps_s, ps_c, ps_pt, ps_av = bank("ps_s"), bank("ps_c"), bank("ps_pt"), bank("ps_av")
        ps_pj = [bank("ps_pj0"), bank("ps_pj1")]
        ps_th, ps_tn = bank("ps_th"), bank("ps_tn")

        raw_loaded, const_loaded, x_loaded = sem("raw_loaded"), sem("const_loaded"), sem("x_loaded")
        mask_loaded = [sem(f"mask_loaded{n}") for n in range(2)]
        xres_loaded = [sem(f"xres_loaded{n}") for n in range(2)]
        o_stored = [sem(f"o_stored{n}") for n in range(2)]
        s_ident, prep_zero, prep_mm, prep_hi, prep_lo, prep_bias, prep_done = (
            sem(n) for n in ("s_ident", "prep_zero", "prep_mm", "prep_hi", "prep_lo", "prep_bias", "prep_done"))
        th_ready, tn_ready, pj_ready, s_ready, c_ready, pt_ready, av_ready = pe_sems = [
            sem(n) for n in ("th_ready", "tn_ready", "pj_ready", "s_ready", "c_ready", "pt_ready", "av_ready")]
        relu_done, hhi_done, q_done, ka_done, sq_done, nT_done, exp_done, cpT_done = act_sems = [
            sem(n) for n in ("relu_done", "hhi_done", "q_done", "ka_done", "sq_done", "nT_done", "exp_done", "cpT_done")]
        ln_chain, norm_chain, epi_chain, hlo_done, kb_done, m_done, v_done, nbd_done, negmax_done, cp_done = dve_sems = [
            sem(n) for n in ("ln_chain", "norm_chain", "epi_chain", "hlo_done", "kb_done", "m_done", "v_done",
                             "nbd_done", "negmax_done", "cp_done")]
        passed_dve, passed_sp, passed_pool = sem("passed_dve"), sem("passed_sp"), sem("passed_pool")
        mask_ready, res_done = pool_sems = [sem("mask_ready"), sem("res_done")]
        EPI_OPS = 4

        xt = x.rearrange("(g j) p d -> g p j d", j=QUAD)
        adjt = adj.rearrange("(g j) p d -> g p j d", j=QUAD)
        x1t = x1.rearrange("(g j) p d -> g j p d", j=QUAD)
        xrt = x.rearrange("(g j) p d -> g j p d", j=QUAD)

        def vslot(par, j):
            return j if j < QUAD - 1 else j + par

        def tiles(t):
            return [t[:, kt, :] for kt in range(KT)]

        block = ctx.enter_context(nc.Block())

        @block.sync
        def _(sp):
            for dst, src in ((raw_mapT, map_wT), (raw_map, map_w), (raw_q, q_wT), (raw_k, k_wT), (raw_g, gmap_w)):
                sp.dma_start(dst, src.rearrange("(k p) n -> p k n", p=P)).then_inc(raw_loaded, 16)
            sp.dma_start(xg[:], xt[0]).then_inc(x_loaded, 16)
            for n in range(2):
                sp.dma_start(mask_u8[:, n], adjt[n]).then_inc(mask_loaded[n], 16)
            sp.dma_start(mb[:], map_b.partition_broadcast(P)).then_inc(const_loaded, 16)
            for n, b in enumerate((map_b, q_b, k_b, gmap_b)):
                with nc.allow_non_contiguous_dma("512 floats, once"):
                    sp.dma_start(bcols[:, n, :], b.rearrange("(k p) -> p k", p=P)).then_inc(const_loaded, 16)
            sp.wait_ge(prep_zero, 2)
            for n in range(2):
                sp.dma_start(gw_bd[DH * n:DH * n + DH, DH * n:DH * n + DH], gcn_WT).then_inc(const_loaded, 16)
            sp.wait_ge(relu_done, count(QUAD))
            sp.dma_start(xg[:], xt[1]).then_inc(x_loaded, 16)

            def body(pair, par, proj, ahead):
                t = 2 * pair + par
                if ahead:
                    wait_apart(sp, relu_done, count(QUAD * (t + 2)), passed_sp)
                    sp.dma_start(xg[:], xt[t + 2]).then_inc(x_loaded, 16)
                    wait_apart(sp, mask_ready, count(t + 1), passed_sp)
                    sp.dma_start(mask_u8[:, par], adjt[t + 2]).then_inc(mask_loaded[par], 16)

                def load_residual(j):
                    wait_apart(sp, res_done, count(QUAD * t + j - 1), passed_sp)
                    sp.dma_start(xres[:, j % 2], xrt[t, j]).then_inc(xres_loaded[j % 2], 16)

                load_residual(0)
                for j in range(QUAD):
                    if j + 1 < QUAD:
                        load_residual(j + 1)
                    wait_apart(sp, res_done, count(QUAD * t + j + 1), passed_sp)
                    sp.dma_start(x1t[t, j], o_sb[:, j % 2]).then_inc(o_stored[j % 2], 16)

            rounds(sp, body)
            for n in range(2):
                sp.wait_ge(o_stored[n], BASE + 16 * (B // 2))

        @block.gpsimd
        def _(pool):
            for s in (*pool_sems, *o_stored):
                pool.sem_inc(s, BASE)
            nc.gpsimd.memset(gw_bd, 0.0).then_inc(prep_zero, 1)
            identities(nc, pool, ident, negi, NEG0, s_ident)
            nc.gpsimd.memset(nT_bd[:], 0.0)
            nc.gpsimd.memset(v_sb[:], 1.0).then_inc(s_ident, 1)
            pool.wait_ge(s_ident, 3)
            pool.wait_ge(prep_mm, 2 * KT + KT + 2)
            pool.wait_ge(prep_lo, 4 * KT)
            nc.gpsimd.memset(k_bd[DH:P, :, :, 0, :], 0.0).then_inc(prep_done, 1)
            pool.wait_ge(prep_done, 2)

            def convert_mask(pair, par):
                t = 2 * pair + par
                pool.wait_ge(mask_loaded[par], 16 * (pair + 1))
                pool.wait_ge(s_ready, count(2 * QUAD * (t - 1)) if not isinstance(t, int) or t else BASE)
                wait_apart(pool, epi_chain, count(EPI_OPS * 2 * QUAD * (t - 1)) if not isinstance(t, int) or t else BASE, passed_pool)
                nc.gpsimd.tensor_scalar(keep[:, par, :], mask_u8[:, par, :, 0], -1.0, 1.0, ALU.mult, ALU.add)
                nc.gpsimd.tensor_copy(mask[:, par], mask_u8[:, par]).then_inc(mask_ready, 1)

            convert_mask(0, 0)

            def body(pair, par, proj, ahead):
                t = 2 * pair + par
                if proj:
                    convert_mask(pair + par, 1 - par)
                for j in range(QUAD):
                    pool.wait_ge(xres_loaded[j % 2], 16 * (2 * t + j // 2 + 1))
                    pool.wait_ge(epi_chain, count(EPI_OPS * (8 * t + 2 * j + 2)))
                    nc.gpsimd.tensor_tensor(o_sb[:, j % 2], o_sb[:, j % 2], xres[:, j % 2], ALU.add).then_inc(res_done, 1)

            rounds(pool, body)

        @block.scalar
        def _(act):
            for s in act_sems:
                act.sem_inc(s, BASE)
            for n, kind in enumerate(["q"] * KT + ["k"] * KT + ["v"] * KT):
                act.wait_ge(prep_mm, n + 1)
                nc.scalar.activation(w_hi[kind][:, n % KT, :], ps_pj[n % 2][:], ACT.Copy,
                                     scale=SCALE if kind == "q" else 1.0).then_inc(prep_hi, 1)
            act.wait_ge(raw_loaded, 16 * 5)
            nc.scalar.copy(w_hi["m"][:], raw_mapT).then_inc(prep_hi, 1)

            def relu(g, j):
                act.wait_ge(ln_chain, count(LN_OPS * (QUAD * g + j + 1)))
                act.wait_ge(th_ready, count(QUAD * g + j - 1))
                nc.scalar.activation(h[:, j % 2], xg[:, j], ACT.Relu, bias=ln_st[:, j, 11:12],
                                     scale=ln_st[:, j, 10:11]).then_inc(relu_done, 1)

            def hT_high(g, j):
                act.wait_ge(th_ready, count(QUAD * g + j + 1))
                nc.scalar.copy(hT_hi[:, :, j * P:(j + 1) * P],
                               ps_th[:].rearrange("p (k n) -> p k n", k=KT)).then_inc(hhi_done, 1)

            def q_copy(g, par, b):
                act.wait_ge(pj_ready, count(16 * g + 2 * b + 1))
                nc.scalar.activation(q_sb[:, par, b], ps_pj[0][:], ACT.Identity, bias=qb[:, b:b + 1]).then_inc(q_done, 1)

            def k_copy(g, par, b):
                act.wait_ge(pj_ready, count(16 * g + 2 * b + 2))
                nc.scalar.activation(k_bd[0:DH, par, b, 0], ps_pj[1][0:DH, :], ACT.Identity,
                                     bias=kb[0:DH, b:b + 1]).then_inc(ka_done, 1)

            def square(g, j):
                act.wait_ge(m_done, count(QUAD * g + j + 1))
                act.wait_ge(norm_chain, count(NORM_OPS * (QUAD * g + j - 1) + 1)
                            if not isinstance(g, int) or g or j else BASE)
                nc.scalar.activation(sq[:], m_sb[:, j], ACT.Square).then_inc(sq_done, 1)

            def nT_copy(g, j):
                act.wait_ge(tn_ready, count(QUAD * g + j + 1))
                nc.scalar.copy(nT[:, j % 2], ps_tn[:].rearrange("p (k n) -> p k n", k=KT)).then_inc(nT_done, 1)

            def exps(t, u):
                n = 8 * t + u
                act.wait_ge(negmax_done, count(n + 1))
                act.wait_ge(cp_done, count(n))
                act.wait_ge(epi_chain, count(EPI_OPS * (n - 1))
                            if not isinstance(n, int) or n else BASE)
                for hh in range(HB):
                    last = nc.scalar.activation(probs[:, hh], ps_s[:, hh * P:(hh + 1) * P], ACT.Exp,
                                                bias=negmax[:, u % 2, hh:hh + 1],
                                                accum_out=zsum[:, u % 2, hh:hh + 1])
                last.then_inc(exp_done, 1)

            def cpT_copy(t, u):
                n = 8 * t + u
                act.wait_ge(pt_ready, count(n + 1))
                act.wait_ge(av_ready, count(n))
                nc.scalar.copy(cpT[:], ps_pt[:].rearrange("p (h n) -> p h n", h=HB)).then_inc(cpT_done, 1)

            for j in range(QUAD):
                relu(0, j)
                hT_high(0, j)
            act.wait_ge(prep_bias, 7)
            act.wait_ge(prep_done, 2)
            for b in range(KT):
                q_copy(0, 0, b)
                k_copy(0, 0, b)
            for j in range(QUAD):
                relu(1, j)
                hT_high(1, j)
            square(0, 0)
            square(0, 1)
            nT_copy(0, 0)
            exps(0, 0)

            def body(pair, par, proj, ahead):
                t = 2 * pair + par
                for u in range(8):
                    if proj and u < KT:
                        q_copy(t + 1, 1 - par, u)
                    cpT_copy(t, u)
                    if ahead and u in (2, 3, 5, 6):
                        relu(t + 2, (2, 3, 5, 6).index(u))
                    if u < 2:
                        square(t, 2 + u)
                    if proj and u in (5, 7):
                        square(t + 1, u // 6)
                    if u in (1, 3, 5):
                        nT_copy(t, (u + 1) // 2)
                    if proj and u == 7:
                        nT_copy(t + 1, 0)
                    if proj and u < KT:
                        k_copy(t + 1, 1 - par, u)
                    if ahead and u >= 4:
                        hT_high(t + 2, u - 4)
                    if u < 7 or proj:
                        exps(t + (u + 1) // 8, (u + 1) % 8)

            rounds(act, body)

        @block.vector
        def _(dve):
            for s in dve_sems:
                dve.sem_inc(s, BASE)

            nc.vector.memset(gb_rows, 0.0).then_inc(prep_zero, 1)
            for n, kind in enumerate(["q"] * KT + ["k"] * KT + ["v"] * KT):
                if n == 0:
                    dve.wait_ge(const_loaded, 16 * 7)
                    dve.wait_ge(prep_zero, 2)
                    for b in range(KT):
                        ins = nc.vector.tensor_scalar(gb_rows[:, b], gb_rows[:, b], bcols[:, 3, b:b + 1], None, ALU.add)
                    ins.then_inc(prep_bias, 1)
                dve.wait_ge(prep_hi, n + 1)
                nc.vector.scalar_tensor_tensor(w_lo[kind][:, n % KT, :], ps_pj[n % 2][:],
                                               SCALE if kind == "q" else 1.0,
                                               w_hi[kind][:, n % KT, :].bitcast(F32), ALU.mult,
                                               ALU.subtract).then_inc(prep_lo, 1)
            dve.wait_ge(prep_hi, 3 * KT + 1)
            for kt in range(KT):
                nc.vector.tensor_tensor(w_lo["m"][:, kt], raw_mapT[:, kt], w_hi["m"][:, kt].bitcast(F32),
                                        ALU.subtract).then_inc(prep_lo, 1)
            dve.wait_ge(prep_mm, 3 * KT + 2)
            nc.vector.tensor_tensor(qb[:], ps_th[:, 0:KT], bcols[:, 1], ALU.add).then_inc(prep_bias, 1)
            nc.vector.tensor_tensor(kb[:], ps_th[:, KT:2 * KT], bcols[:, 2], ALU.add).then_inc(prep_bias, 1)
            dve.wait_ge(prep_bias, 3)
            nc.vector.tensor_scalar(qb[:], qb[:], SCALE, None, ALU.mult).then_inc(prep_bias, 1)
            nc.vector.tensor_copy(vb[:], ps_tn[:]).then_inc(prep_bias, 1)
            dve.wait_ge(prep_bias, 5)
            dve.wait_ge(prep_lo, 4 * KT)
            dve.sem_inc(prep_bias, 2)
            nc.vector.memset(k_bd[0:DH, :, :, 1, :], 0.0).then_inc(prep_done, 1)

            def stats(g, j):
                dve.wait_ge(x_loaded, 16 * (g + 1))
                layer_norm_stats(nc, dve, ln_chain, passed_dve, count(LN_OPS * (QUAD * g + j)), xg[:, j], ln_st[:, j],
                                 ln_st[:, j, 10:11], ln_st[:, j, 11:12])

            def hT_low(g, j):
                dve.wait_ge(hhi_done, count(QUAD * g + j + 1))
                cols = slice(j * P, (j + 1) * P)
                nc.vector.tensor_tensor(hT_lo[:, :, cols], ps_th[:].rearrange("p (k n) -> p k n", k=KT),
                                        hT_hi[:, :, cols].bitcast(F32), ALU.subtract).then_inc(hlo_done, 1)

            def k_copy(g, par, b):
                dve.wait_ge(pj_ready, count(16 * g + 2 * b + 2))
                nc.vector.tensor_scalar(k_bd[DH:P, par, b, 1], ps_pj[1][DH:P, :], kb[DH:P, b:b + 1], None,
                                        ALU.add).then_inc(kb_done, 1)

            def m_copy(g, j):
                dve.wait_ge(pj_ready, count(16 * g + 8 + 2 * j + 1))
                nc.vector.tensor_tensor(m_sb[:, j], ps_pj[0][:], mb[:], ALU.add).then_inc(m_done, 1)

            def v_copy(g, par, j):
                dve.wait_ge(pj_ready, count(16 * g + 8 + 2 * j + 2))
                dst = v_sb[:, vslot(par, j), 0:H0 * VW].rearrange("p (h c) -> p h c", h=H0)[:, :, 0:DH]
                nc.vector.tensor_tensor(dst, ps_pj[1][:].rearrange("p (h c) -> p h c", h=H0),
                                        vb[:].rearrange("p (h c) -> p h c", h=H0), ALU.add).then_inc(v_done, 1)

            def normalise(g, j):
                first = count(NORM_OPS * (QUAD * g + j))
                done = [0]

                def link(ins):
                    ins.then_inc(norm_chain, 1)
                    done[0] += 1
                    if done[0] < NORM_OPS:
                        dve.wait_ge(norm_chain, first + done[0])

                n2, r, a = norm_st[:, 0], norm_st[:, 1], norm_st[:, 2]
                heads = m_sb[:, j].rearrange("p (h c) -> p h c", h=H0)
                dve.wait_ge(sq_done, count(QUAD * g + j + 1))
                link(nc.vector.tensor_reduce(n2, sq[:].rearrange("p (h c) -> p h c", h=H0), AX_X, ALU.add))
                link(nc.vector.tensor_scalar(n2, n2, NORM_EPS2, None, ALU.max))
                rsqrt_steps(nc, link, r, n2, a)
                link(nc.vector.tensor_tensor(heads, heads, r.unsqueeze(2).to_broadcast([P, H0, DH]), ALU.mult))
                assert done[0] == NORM_OPS

            def nT_blocks(g, j):
                dve.wait_ge(nT_done, count(QUAD * g + j + 1))
                nc.vector.tensor_copy(nT_bd[0:DH, j % 2, :, 0], nT[0:DH, j % 2])
                nc.vector.tensor_copy(nT_bd[DH:P, j % 2, :, 1], nT[DH:P, j % 2]).then_inc(nbd_done, 1)

            def row_max(t, u):
                dve.wait_ge(s_ready, count(8 * t + u + 1))
                nc.vector.tensor_reduce(negmax[:, u % 2], ps_s[:].rearrange("p (h n) -> p h n", h=HB), AX_X,
                                        ALU.max, negate=True).then_inc(negmax_done, 1)

            def select_similar(t, u):
                n = 8 * t + u
                dve.wait_ge(exp_done, count(n + 1))
                dve.wait_ge(c_ready, count(n + 1))
                dve.wait_ge(pt_ready, count(n))
                nc.vector.scalar_tensor_tensor(cprobs[:], ps_c[:].rearrange("p (h n) -> p h n", h=HB), THRESHOLD,
                                               probs[:], ALU.is_gt, ALU.mult).then_inc(cp_done, 1)

            def epilogue(t, par, u):
                n = 8 * t + u
                j, half = u // 2, u % 2
                first = count(EPI_OPS * n)
                av = ps_av[:].rearrange("p (h n) -> p h n", h=HB)
                den, rec, rk = epi_st[:, 0], epi_st[:, 1], epi_st[:, 2]
                dve.wait_ge(av_ready, count(n + 1))
                nc.vector.tensor_tensor(den, av[:, :, DH], zsum[:, u % 2], ALU.add).then_inc(epi_chain, 1)
                dve.wait_ge(epi_chain, first + 1)
                nc.vector.reciprocal(rec, den).then_inc(epi_chain, 1)
                dve.wait_ge(epi_chain, first + 2)
                nc.vector.tensor_scalar(rk, rec, keep[:, par, j:j + 1], None, ALU.mult).then_inc(epi_chain, 1)
                dve.wait_ge(epi_chain, first + 3)
                if half == 0:
                    dve.wait_ge(o_stored[j % 2], BASE + 16 * (2 * t + j // 2))
                dst = o_sb[:, j % 2, half * HB * DH:(half + 1) * HB * DH].rearrange("p (h c) -> p h c", h=HB)
                nc.vector.scalar_tensor_tensor(dst, av[:, :, 0:DH], 0.0, rk.unsqueeze(2).to_broadcast([P, HB, DH]),
                                               ALU.max, ALU.mult).then_inc(epi_chain, 1)

            for j in range(QUAD):
                stats(0, j)
                hT_low(0, j)
            for b in range(KT):
                k_copy(0, 0, b)
            for j in range(QUAD):
                m_copy(0, j)
                v_copy(0, 0, j)
                stats(1, j)
                hT_low(1, j)
            normalise(0, 0)
            normalise(0, 1)
            nT_blocks(0, 0)
            row_max(0, 0)

            def body(pair, par, proj, ahead):
                t = 2 * pair + par
                dve.wait_ge(mask_ready, count(t + 1))
                for u in range(8):
                    select_similar(t, u)
                    if ahead and u in (2, 3, 5, 6):
                        stats(t + 2, (2, 3, 5, 6).index(u))
                    if proj and u >= 4:
                        m_copy(t + 1, u - 4)
                    if u < 2:
                        normalise(t, 2 + u)
                    if proj and u in (5, 7):
                        normalise(t + 1, u // 6)
                    if u in (1, 3, 5):
                        nT_blocks(t, (u + 1) // 2)
                    if proj and u == 7:
                        nT_blocks(t + 1, 0)
                    if proj and u < KT:
                        k_copy(t + 1, 1 - par, u)
                    if proj and u >= 4:
                        v_copy(t + 1, 1 - par, u - 4)
                    epilogue(t, par, u)
                    if ahead and u >= 4:
                        hT_low(t + 2, u - 4)
                    if u < 7 or proj:
                        row_max(t + (u + 1) // 8, (u + 1) % 8)

            rounds(dve, body)

        @block.tensor
        def _(pe):
            for s in pe_sems:
                pe.sem_inc(s, BASE)
            pe.wait_ge(raw_loaded, 16 * 5)
            pe.wait_ge(const_loaded, 16 * 7)
            for n in range(3 * KT):
                if n >= 2:
                    pe.wait_ge(prep_lo, n - 1)
                out = ps_pj[n % 2]
                rows = slice((n % KT) * P, (n % KT + 1) * P)
                if n < 2 * KT:
                    rhs = raw_q if n < KT else raw_k
                    for mk in range(KT):
                        mm = nc.tensor.matmul(out[:], raw_map[:, mk, rows], rhs[:, mk, :], start=(mk == 0), stop=(mk == KT - 1))
                else:
                    for pr in range(PAIRS0):
                        mm = nc.tensor.matmul(out[:, pr * P:(pr + 1) * P], raw_g[:, pr, rows], gw_bd, start=True, stop=True)
                mm.then_inc(prep_mm, 1)
            for n in range(2 * KT):
                rhs = raw_q if n < KT else raw_k
                cols = slice((n % KT) * P, (n % KT + 1) * P)
                for mk in range(KT):
                    mm = nc.tensor.matmul(ps_th[:, n:n + 1], rhs[:, mk, cols], bcols[:, 0, mk:mk + 1], start=(mk == 0), stop=(mk == KT - 1))
            mm.then_inc(prep_mm, 1)
            pe.wait_ge(prep_bias, 1)
            for pr in range(PAIRS0):
                mm = nc.tensor.matmul(ps_tn[:, pr * P:(pr + 1) * P], gb_rows[:, pr, :], gw_bd, start=True, stop=True)
            mm.then_inc(prep_mm, 1)
            pe.wait_ge(s_ident, 3)
            pe.wait_ge(prep_bias, 5)
            pe.wait_ge(prep_lo, 4 * KT)
            pe.wait_ge(prep_done, 2)

            def h_transpose(g, j):
                pe.wait_ge(relu_done, count(QUAD * g + j + 1))
                pe.wait_ge(hlo_done, count(QUAD * g + j))
                for kt in range(KT):
                    mm = nc.tensor.transpose(ps_th[:, kt * P:(kt + 1) * P], h[:, j % 2, kt * P:(kt + 1) * P], ident[:])
                mm.then_inc(th_ready, 1)

            def n_transpose(g, j):
                pe.wait_ge(norm_chain, count(NORM_OPS * (QUAD * g + j + 1)))
                pe.wait_ge(nT_done, count(QUAD * g + j))
                for kt in range(KT):
                    mm = nc.tensor.transpose(ps_tn[:, kt * P:(kt + 1) * P], m_sb[:, j, kt * P:(kt + 1) * P], ident[:])
                mm.then_inc(tn_ready, 1)

            def by_channel(kind, b, out):
                cols = slice(b * P, (b + 1) * P)
                split_products(nc.tensor, out, lambda k: w_hi[kind][:, k, cols], lambda k: w_lo[kind][:, k, cols],
                               lambda k: hT_hi[:, k, :], lambda k: hT_lo[:, k, :], KT).then_inc(pj_ready, 1)

            def by_node(kind, j, out):
                cols = slice(j * P, (j + 1) * P)
                split_products(nc.tensor, out, lambda k: hT_hi[:, k, cols], lambda k: hT_lo[:, k, cols],
                               lambda k: w_hi[kind][:, k, :], lambda k: w_lo[kind][:, k, :], KT).then_inc(pj_ready, 1)

            def project_q(g, b):
                if b == 0:
                    pe.wait_ge(hlo_done, count(QUAD * g + QUAD))
                    pe.wait_ge(m_done, count(QUAD * g))
                else:
                    pe.wait_ge(q_done, count(QUAD * g + b))
                by_channel("q", b, ps_pj[0][:])

            def project_k(g, b):
                if b == 0:
                    pe.wait_ge(v_done, count(QUAD * g))
                else:
                    pe.wait_ge(ka_done, count(QUAD * g + b))
                    pe.wait_ge(kb_done, count(QUAD * g + b))
                by_channel("k", b, ps_pj[1][:])

            def project_m(g, j):
                if j == 0:
                    pe.wait_ge(q_done, count(QUAD * g + QUAD))
                else:
                    pe.wait_ge(m_done, count(QUAD * g + j))
                by_node("m", j, ps_pj[0][:])

            def project_v(g, j):
                if j == 0:
                    pe.wait_ge(ka_done, count(QUAD * g + QUAD))
                    pe.wait_ge(kb_done, count(QUAD * g + QUAD))
                else:
                    pe.wait_ge(v_done, count(QUAD * g + j))
                by_node("v", j, ps_pj[1][:])

            def scores(t, par, u):
                n = 8 * t + u
                j, half = u // 2, u % 2
                cols = slice(j * P, (j + 1) * P)
                if u == 0:
                    pe.wait_ge(q_done, count(QUAD * t + QUAD))
                    pe.wait_ge(ka_done, count(QUAD * t + QUAD))
                    pe.wait_ge(kb_done, count(QUAD * t + QUAD))
                    pe.wait_ge(mask_ready, count(t + 1))
                pe.wait_ge(exp_done, count(n))
                nc.tensor.matmul(ps_s[:].rearrange("p (h n) -> p h n", h=HB), negi[:],
                                 mask[:, par, j:j + 1, :].to_broadcast([P, HB, P]), start=True, stop=False)
                for pl in range(2):
                    pr = 2 * half + pl
                    mm = nc.tensor.matmul(ps_s[:, 2 * pl * P:2 * (pl + 1) * P].rearrange("p (h n) -> p h n", h=2), q_sb[:, par, pr, cols], k_bd[:, par, pr, :, cols],
                                          start=False, stop=(pl == 1))
                mm.then_inc(s_ready, 1)
                pe.wait_ge(cp_done, count(n))
                if half == 0:
                    pe.wait_ge(nbd_done, count(QUAD * t + j + 1))
                for pl in range(2):
                    pr = 2 * half + pl
                    mm = nc.tensor.matmul(ps_c[:, 2 * pl * P:2 * (pl + 1) * P].rearrange("p (h n) -> p h n", h=2), nT[:, j % 2, pr, :], nT_bd[:, j % 2, pr],
                                          start=True, stop=True)
                mm.then_inc(c_ready, 1)

            def prob_transpose(t, u):
                n = 8 * t + u
                pe.wait_ge(cp_done, count(n + 1))
                pe.wait_ge(cpT_done, count(n))
                for hh in range(HB):
                    mm = nc.tensor.transpose(ps_pt[:, hh * P:(hh + 1) * P], cprobs[:, hh], ident[:])
                mm.then_inc(pt_ready, 1)

            def weigh_values(t, par, u):
                n = 8 * t + u
                j, half = u // 2, u % 2
                pe.wait_ge(cpT_done, count(n + 1))
                pe.wait_ge(epi_chain, count(EPI_OPS * n))
                pe.wait_ge(v_done, count(QUAD * t + j + 1))
                for hh in range(HB):
                    hd = HB * half + hh
                    mm = nc.tensor.matmul(ps_av[:, hh * P:hh * P + NV], cpT[:, hh],
                                          v_sb[:, vslot(par, j), hd * VW:hd * VW + NV], start=True, stop=True)
                mm.then_inc(av_ready, 1)

            for j in range(QUAD):
                h_transpose(0, j)
            for b in range(KT):
                project_q(0, b)
                project_k(0, b)
            for j in range(QUAD):
                project_m(0, j)
                project_v(0, j)
                h_transpose(1, j)
            n_transpose(0, 0)
            scores(0, 0, 0)

            def body(pair, par, proj, ahead):
                t = 2 * pair + par
                for u in range(8):
                    if proj and u < KT:
                        project_q(t + 1, u)
                    if proj and u >= KT:
                        project_m(t + 1, u - KT)
                    prob_transpose(t, u)
                    if u in (1, 3, 5):
                        n_transpose(t, (u + 1) // 2)
                    if proj and u == 7:
                        n_transpose(t + 1, 0)
                    if proj and u < KT:
                        project_k(t + 1, u)
                    if proj and u >= KT:
                        project_v(t + 1, u - KT)
                    weigh_values(t, par, u)
                    if ahead and u >= 4:
                        h_transpose(t + 2, u - 4)
                    if u < 7:
                        scores(t, par, u + 1)
                    elif proj:
                        scores(t + 1, 1 - par, 0)

            rounds(pe, body)


def layer1(nc, x1, adj, wq, wk, wv, wo, bo, out):
    with ExitStack() as ctx:
        def sb(name, shape, dt=F32):
            return ctx.enter_context(nc.sbuf_tensor("l1_" + name, shape, dt))

        def bank(name):
            return ctx.enter_context(nc.psum_tensor("l1_" + name, [P, 512], F32))

        def sem(name):
            return ctx.enter_context(nc.semaphore("l1_" + name))

        widths = {"q": (KT, INNER), "k": (KT, INNER), "v": (KT, INNER), "o": (PAIRS1, D)}
        w_hi = {k: sb(f"w{k}_hi", [P, *s], F32R) for k, s in widths.items()}
        w_lo = {k: sb(f"w{k}_lo", [P, *s], F32R) for k, s in widths.items()}
        raw = {k: sb(f"w{k}_raw", [P, *s]) for k, s in widths.items()}
        ident = sb("ident", [P, P])
        negi = sb("negi", [P, P], BF16)
        bo_rows = sb("bo_rows", [P, D])
        q_sb = sb("q_sb", [P, 2, PAIRS1, QUAD * P])
        k_bd = sb("k_bd", [P, 2, PAIRS1, 2, QUAD * P])
        v_sb = sb("v_sb", [P, 2, QUAD, INNER])
        hT_hi = sb("hT_hi", [P, 2, KT, QUAD * P], F32R)
        hT_lo = sb("hT_lo", [P, 2, KT, QUAD * P], F32R)
        xg = sb("xg", [P, QUAD, D])
        h = sb("h", [P, 2, D])
        ln_st = sb("ln_st", [P, QUAD, 12])
        mask_u8 = sb("mask_u8", [P, 2, QUAD, P], U8)
        mask = sb("mask", [P, 2, QUAD, P], BF16)
        negmax = sb("negmax", [P, 2, HB])
        zsum = sb("zsum", [P, 2, HB])
        rec = sb("rec", [P, HB])
        probs = sb("probs", [P, HB, P])
        nprobs = sb("nprobs", [P, HB, P])
        npT = sb("npT", [P, HB, P])
        aT_hi = sb("aT_hi", [P, PAIRS1, P], F32R)
        aT_lo = sb("aT_lo", [P, PAIRS1, P], F32R)
        xres = sb("xres", [P, 2, D])
        o_sb = sb("o_sb", [P, 2, D])

        ps_s, ps_pt, ps_av, ps_o, ps_th = bank("ps_s"), bank("ps_pt"), bank("ps_av"), bank("ps_o"), bank("ps_th")
        ps_pj = [bank("ps_pj0"), bank("ps_pj1")]

        raw_loaded, bo_loaded, x_loaded = sem("raw_loaded"), sem("bo_loaded"), sem("x_loaded")
        mask_loaded = [sem(f"mask_loaded{n}") for n in range(2)]
        xres_loaded = [sem(f"xres_loaded{n}") for n in range(2)]
        o_stored = [sem(f"o_stored{n}") for n in range(2)]
        s_ident, prep_hi, prep_lo, prep_zero = sem("s_ident"), sem("prep_hi"), sem("prep_lo"), sem("prep_zero")
        th_ready, pj_ready, s_ready, pt_ready, av_ready, o_ready = pe_sems = [
            sem(n) for n in ("th_ready", "pj_ready", "s_ready", "pt_ready", "av_ready", "o_ready")]
        relu_done, hhi_done, q_done, ka_done, exp_done, npT_done, ahi_done = act_sems = [
            sem(n) for n in ("relu_done", "hhi_done", "q_done", "ka_done", "exp_done", "npT_done", "ahi_done")]
        ln_chain, hlo_done, kb_done, v_done, negmax_done, rec_done, np_done, alo_done, out_done = dve_sems = [
            sem(n) for n in ("ln_chain", "hlo_done", "kb_done", "v_done", "negmax_done", "rec_done", "np_done", "alo_done", "out_done")]
        passed_dve, passed_sp, passed_pool = sem("passed_dve"), sem("passed_sp"), sem("passed_pool")
        mask_ready, res_ready = pool_sems = [sem("mask_ready"), sem("res_ready")]

        xt = x1.rearrange("(g j) p d -> g p j d", j=QUAD)
        xrt = x1.rearrange("(g j) p d -> g j p d", j=QUAD)
        adjt = adj.rearrange("(g j) p d -> g p j d", j=QUAD)
        outt = out.rearrange("(g j) p d -> g j p d", j=QUAD)

        block = ctx.enter_context(nc.Block())

        @block.sync
        def _(sp):
            sp.dma_start(xg[:], xt[0]).then_inc(x_loaded, 16)
            for k, w in (("q", wq), ("k", wk), ("v", wv), ("o", wo)):
                sp.dma_start(raw[k][:], w.rearrange("(k p) n -> p k n", p=P)).then_inc(raw_loaded, 16)
            for n in range(2):
                sp.dma_start(mask_u8[:, n], adjt[n]).then_inc(mask_loaded[n], 16)
            sp.dma_start(bo_rows[:], bo.partition_broadcast(P)).then_inc(bo_loaded, 16)
            sp.wait_ge(relu_done, count(QUAD))
            sp.dma_start(xg[:], xt[1]).then_inc(x_loaded, 16)

            def body(pair, par, proj, ahead):
                t = 2 * pair + par
                if ahead:
                    wait_apart(sp, relu_done, count(QUAD * (t + 2)), passed_sp)
                    sp.dma_start(xg[:], xt[t + 2]).then_inc(x_loaded, 16)
                    wait_apart(sp, mask_ready, count(t + 1), passed_sp)
                    sp.dma_start(mask_u8[:, par], adjt[t + 2]).then_inc(mask_loaded[par], 16)

                def load_residual(j):
                    wait_apart(sp, out_done, count(QUAD * t + j - 1), passed_sp)
                    sp.dma_start(xres[:, j % 2], xrt[t, j]).then_inc(xres_loaded[j % 2], 16)

                load_residual(0)
                for j in range(QUAD):
                    if j + 1 < QUAD:
                        load_residual(j + 1)
                    wait_apart(sp, out_done, count(QUAD * t + j + 1), passed_sp)
                    sp.dma_start(outt[t, j], o_sb[:, j % 2]).then_inc(o_stored[j % 2], 16)

            rounds(sp, body)
            for n in range(2):
                sp.wait_ge(o_stored[n], BASE + 16 * (B // 2))

        @block.gpsimd
        def _(pool):
            for s in (*pool_sems, *o_stored):
                pool.sem_inc(s, BASE)
            identities(nc, pool, ident, negi, NEG1, s_ident)
            nc.gpsimd.memset(k_bd[:], 0.0).then_inc(prep_zero, 1)
            pool.wait_ge(bo_loaded, 16)

            def convert_mask(pair, par):
                t = 2 * pair + par
                pool.wait_ge(mask_loaded[par], 16 * (pair + 1))
                wait_apart(pool, s_ready, count(QUAD * (t - 1)) if not isinstance(t, int) or t else BASE, passed_pool)
                nc.gpsimd.tensor_scalar(mask[:, par], mask_u8[:, par], -1.0, 1.0, ALU.mult, ALU.add).then_inc(mask_ready, 1)

            convert_mask(0, 0)

            def body(pair, par, proj, ahead):
                t = 2 * pair + par
                if proj:
                    convert_mask(pair + par, 1 - par)
                for j in range(QUAD):
                    pool.wait_ge(xres_loaded[j % 2], 16 * (2 * t + j // 2 + 1))
                    nc.gpsimd.tensor_tensor(xres[:, j % 2], xres[:, j % 2], bo_rows[:], ALU.add).then_inc(res_ready, 1)

            rounds(pool, body)

        @block.scalar
        def _(act):
            for s in act_sems:
                act.sem_inc(s, BASE)
            act.wait_ge(raw_loaded, 16 * 4)
            for k in "qkvo":
                nc.scalar.activation(w_hi[k][:], raw[k][:], ACT.Copy, scale=SCALE if k == "q" else 1.0).then_inc(prep_hi, 1)

            def relu(g, j):
                act.wait_ge(ln_chain, count(LN_OPS * (QUAD * g + j + 1)))
                act.wait_ge(th_ready, count(QUAD * g + j - 1))
                nc.scalar.activation(h[:, j % 2], xg[:, j], ACT.Relu, bias=ln_st[:, j, 11:12],
                                     scale=ln_st[:, j, 10:11]).then_inc(relu_done, 1)

            def hT_high(g, par, j):
                act.wait_ge(th_ready, count(QUAD * g + j + 1))
                nc.scalar.copy(hT_hi[:, par, :, j * P:(j + 1) * P],
                               ps_th[:].rearrange("p (k n) -> p k n", k=KT)).then_inc(hhi_done, 1)

            def qk_copy(g, par, c):
                act.wait_ge(pj_ready, count(8 * g + 2 * c + 1))
                if c % 2 == 0:
                    nc.scalar.copy(q_sb[:, par, c // 2], ps_pj[0][:]).then_inc(q_done, 1)
                else:
                    nc.scalar.copy(k_bd[0:DH, par, c // 2, 0], ps_pj[0][0:DH, :]).then_inc(ka_done, 1)

            def exps(t, u):
                n = QUAD * t + u
                act.wait_ge(negmax_done, count(n + 1))
                act.wait_ge(np_done, count(n))
                for hh in range(HB):
                    last = nc.scalar.activation(probs[:, hh], ps_s[:, hh * P:(hh + 1) * P], ACT.Exp,
                                                bias=negmax[:, u % 2, hh:hh + 1],
                                                accum_out=zsum[:, u % 2, hh:hh + 1])
                last.then_inc(exp_done, 1)

            def npT_copy(t, u):
                n = QUAD * t + u
                act.wait_ge(pt_ready, count(n + 1))
                act.wait_ge(av_ready, count(n))
                nc.scalar.copy(npT[:], ps_pt[:].rearrange("p (h n) -> p h n", h=HB)).then_inc(npT_done, 1)

            def aT_high(t, u):
                n = QUAD * t + u
                act.wait_ge(av_ready, count(n + 1))
                act.wait_ge(o_ready, count(n))
                nc.scalar.copy(aT_hi[:], ps_av[:, 0:PAIRS1 * P].rearrange("p (k n) -> p k n", k=PAIRS1)).then_inc(ahi_done, 1)

            for g in range(2):
                for j in range(QUAD):
                    relu(g, j)
                    hT_high(g, g, j)
            act.wait_ge(prep_zero, 1)
            for c in range(QUAD):
                qk_copy(0, 0, c)
            exps(0, 0)

            def body(pair, par, proj, ahead):
                t = 2 * pair + par
                for u in range(QUAD):
                    if ahead:
                        relu(t + 2, u)
                    if proj:
                        qk_copy(t + 1, 1 - par, u)
                    npT_copy(t, u)
                    aT_high(t, u)
                    if ahead:
                        hT_high(t + 2, par, u)
                    if u < QUAD - 1 or proj:
                        exps(t + (u + 1) // QUAD, (u + 1) % QUAD)

            rounds(act, body)

        @block.vector
        def _(dve):
            for s in dve_sems:
                dve.sem_inc(s, BASE)
            for n, k in enumerate("qkvo"):
                dve.wait_ge(prep_hi, n + 1)
                nc.vector.scalar_tensor_tensor(w_lo[k][:], raw[k][:], SCALE if k == "q" else 1.0,
                                               w_hi[k][:].bitcast(F32), ALU.mult, ALU.subtract).then_inc(prep_lo, 1)

            def stats(g, j):
                dve.wait_ge(x_loaded, 16 * (g + 1))
                layer_norm_stats(nc, dve, ln_chain, passed_dve, count(LN_OPS * (QUAD * g + j)), xg[:, j], ln_st[:, j],
                                 ln_st[:, j, 10:11], ln_st[:, j, 11:12])

            def hT_low(g, par, j):
                dve.wait_ge(hhi_done, count(QUAD * g + j + 1))
                cols = slice(j * P, (j + 1) * P)
                nc.vector.tensor_tensor(hT_lo[:, par, :, cols], ps_th[:].rearrange("p (k n) -> p k n", k=KT),
                                        hT_hi[:, par, :, cols].bitcast(F32), ALU.subtract).then_inc(hlo_done, 1)

            def k_copy(g, par, c):
                dve.wait_ge(pj_ready, count(8 * g + 2 * c + 1))
                nc.vector.tensor_copy(k_bd[DH:P, par, c // 2, 1], ps_pj[0][DH:P, :]).then_inc(kb_done, 1)

            def v_copy(g, par, j):
                dve.wait_ge(pj_ready, count(8 * g + 2 * j + 2))
                nc.vector.tensor_copy(v_sb[:, par, j], ps_pj[1][:, 0:INNER]).then_inc(v_done, 1)

            def row_max(t, u):
                dve.wait_ge(s_ready, count(QUAD * t + u + 1))
                nc.vector.tensor_reduce(negmax[:, u % 2], ps_s[:].rearrange("p (h n) -> p h n", h=HB), AX_X,
                                        ALU.max, negate=True).then_inc(negmax_done, 1)

            def normalise(t, u):
                n = QUAD * t + u
                dve.wait_ge(exp_done, count(n + 1))
                nc.vector.reciprocal(rec[:], zsum[:, u % 2]).then_inc(rec_done, 1)
                dve.wait_ge(rec_done, count(n + 1))
                dve.wait_ge(pt_ready, count(n))
                nc.vector.tensor_tensor(nprobs[:], probs[:], rec[:].unsqueeze(2).to_broadcast([P, HB, P]),
                                        ALU.mult).then_inc(np_done, 1)

            def aT_low(t, u):
                n = QUAD * t + u
                dve.wait_ge(ahi_done, count(n + 1))
                nc.vector.tensor_tensor(aT_lo[:], ps_av[:, 0:PAIRS1 * P].rearrange("p (k n) -> p k n", k=PAIRS1),
                                        aT_hi[:].bitcast(F32), ALU.subtract).then_inc(alo_done, 1)

            def add_residual(t, u):
                dve.wait_ge(o_ready, count(QUAD * t + u + 1))
                dve.wait_ge(res_ready, count(QUAD * t + u + 1))
                dve.wait_ge(o_stored[u % 2], BASE + 16 * (2 * t + u // 2))
                nc.vector.tensor_tensor(o_sb[:, u % 2], ps_o[:], xres[:, u % 2], ALU.add).then_inc(out_done, 1)

            for g in range(2):
                for j in range(QUAD):
                    stats(g, j)
                    hT_low(g, g, j)
            dve.wait_ge(prep_zero, 1)
            for j in range(QUAD):
                if j % 2:
                    k_copy(0, 0, j)
                v_copy(0, 0, j)
            row_max(0, 0)

            def body(pair, par, proj, ahead):
                t = 2 * pair + par
                for u in range(QUAD):
                    normalise(t, u)
                    if ahead:
                        stats(t + 2, u)
                    if proj and u % 2:
                        k_copy(t + 1, 1 - par, u)
                    if proj:
                        v_copy(t + 1, 1 - par, u)
                    aT_low(t, u)
                    if ahead:
                        hT_low(t + 2, par, u)
                    if u < QUAD - 1 or proj:
                        row_max(t + (u + 1) // QUAD, (u + 1) % QUAD)
                    add_residual(t, u)

            rounds(dve, body)

        @block.tensor
        def _(pe):
            for s in pe_sems:
                pe.sem_inc(s, BASE)
            pe.wait_ge(s_ident, 2)
            pe.wait_ge(prep_lo, 4)
            pe.wait_ge(prep_zero, 1)

            def h_transpose(g, j):
                pe.wait_ge(relu_done, count(QUAD * g + j + 1))
                pe.wait_ge(hlo_done, count(QUAD * g + j))
                for kt in range(KT):
                    mm = nc.tensor.transpose(ps_th[:, kt * P:(kt + 1) * P], h[:, j % 2, kt * P:(kt + 1) * P], ident[:])
                mm.then_inc(th_ready, 1)

            def project_qk(g, par, c):
                if c == 0:
                    pe.wait_ge(hlo_done, count(QUAD * g + QUAD))
                if c % 2 == 0:
                    pe.wait_ge(ka_done, count(2 * g + c // 2))
                    pe.wait_ge(kb_done, count(2 * g + c // 2))
                else:
                    pe.wait_ge(q_done, count(2 * g + c // 2 + 1))
                kind = "qk"[c % 2]
                cols = slice((c // 2) * P, (c // 2 + 1) * P)
                split_products(nc.tensor, ps_pj[0][:], lambda k: w_hi[kind][:, k, cols], lambda k: w_lo[kind][:, k, cols],
                               lambda k: hT_hi[:, par, k, :], lambda k: hT_lo[:, par, k, :], KT).then_inc(pj_ready, 1)

            def project_v(g, par, j):
                pe.wait_ge(v_done, count(QUAD * g + j))
                cols = slice(j * P, (j + 1) * P)
                split_products(nc.tensor, ps_pj[1][:, 0:INNER], lambda k: hT_hi[:, par, k, cols], lambda k: hT_lo[:, par, k, cols],
                               lambda k: w_hi["v"][:, k, :], lambda k: w_lo["v"][:, k, :], KT).then_inc(pj_ready, 1)

            def scores(t, par, u):
                n = QUAD * t + u
                cols = slice(u * P, (u + 1) * P)
                if u == 0:
                    pe.wait_ge(q_done, count(2 * t + 2))
                    pe.wait_ge(ka_done, count(2 * t + 2))
                    pe.wait_ge(kb_done, count(2 * t + 2))
                    pe.wait_ge(mask_ready, count(t + 1))
                pe.wait_ge(exp_done, count(n))
                nc.tensor.matmul(ps_s[:].rearrange("p (h n) -> p h n", h=HB), negi[:],
                                 mask[:, par, u:u + 1, :].to_broadcast([P, HB, P]), start=True, stop=False)
                for pr in range(PAIRS1):
                    mm = nc.tensor.matmul(ps_s[:, 2 * pr * P:2 * (pr + 1) * P].rearrange("p (h n) -> p h n", h=2), q_sb[:, par, pr, cols], k_bd[:, par, pr, :, cols],
                                          start=False, stop=(pr == PAIRS1 - 1))
                mm.then_inc(s_ready, 1)

            def prob_transpose(t, u):
                n = QUAD * t + u
                pe.wait_ge(np_done, count(n + 1))
                pe.wait_ge(npT_done, count(n))
                for hh in range(HB):
                    mm = nc.tensor.transpose(ps_pt[:, hh * P:(hh + 1) * P], nprobs[:, hh], ident[:])
                mm.then_inc(pt_ready, 1)

            def weigh_values(t, par, u):
                n = QUAD * t + u
                pe.wait_ge(npT_done, count(n + 1))
                pe.wait_ge(alo_done, count(n))
                pe.wait_ge(v_done, count(n + 1))
                for hh in range(HB):
                    rows = slice(DH * (hh % 2), DH * (hh % 2) + DH)
                    mm = nc.tensor.matmul(ps_av[rows, (hh // 2) * P:(hh // 2 + 1) * P],
                                          v_sb[:, par, u, hh * DH:(hh + 1) * DH], npT[:, hh], start=True, stop=True)
                mm.then_inc(av_ready, 1)

            def project_out(t, u):
                n = QUAD * t + u
                pe.wait_ge(alo_done, count(n + 1))
                pe.wait_ge(out_done, count(n))
                split_products(nc.tensor, ps_o[:], lambda k: aT_hi[:, k, :], lambda k: aT_lo[:, k, :],
                               lambda k: w_hi["o"][:, k, :], lambda k: w_lo["o"][:, k, :], PAIRS1).then_inc(o_ready, 1)

            for g in range(2):
                for j in range(QUAD):
                    h_transpose(g, j)
            for c in range(QUAD):
                project_qk(0, 0, c)
                project_v(0, 0, c)
            scores(0, 0, 0)

            def body(pair, par, proj, ahead):
                t = 2 * pair + par
                for u in range(QUAD):
                    if proj:
                        project_qk(t + 1, 1 - par, u)
                    prob_transpose(t, u)
                    if proj:
                        project_v(t + 1, 1 - par, u)
                    weigh_values(t, par, u)
                    if ahead:
                        h_transpose(t + 2, u)
                    if u < QUAD - 1:
                        scores(t, par, u + 1)
                    elif proj:
                        scores(t + 1, 1 - par, 0)
                    project_out(t, u)

            rounds(pe, body)


def build(nc, ap):
    x1 = nc.dram_tensor("x1_scratch", (B, P, D), F32, kind="Internal").ap()
    layer0(nc, ap["x"], ap["adj"], ap["map_w"], ap["map_wT"], ap["map_b"], ap["q_wT"], ap["q_b"], ap["k_wT"], ap["k_b"],
           ap["gmap_w"], ap["gmap_b"], ap["gcn_WT"], x1)
    layer1(nc, x1, ap["adj"], ap["wq"], ap["wk"], ap["wv"], ap["wo"], ap["bo"], ap["out"])


def kernel(x, adj, L0_gnn_map_w, L0_gnn_map_b, L0_gnn_q_w, L0_gnn_q_b, L0_gnn_k_w, L0_gnn_k_b, L0_gnn_gcn_map_w,
           L0_gnn_gcn_map_b, L0_gnn_gcn_W, L1_gnn_Wq, L1_gnn_Wk, L1_gnn_Wv, L1_gnn_Wo, L1_gnn_bo):
    from concourse import bacc
    from concourse.bass_utils import run_bass_kernel_spmd

    arrays = {
        "x": x, "adj": adj, "map_w": L0_gnn_map_w, "map_wT": np.transpose(L0_gnn_map_w), "map_b": L0_gnn_map_b,
        "q_wT": np.transpose(L0_gnn_q_w), "q_b": L0_gnn_q_b, "k_wT": np.transpose(L0_gnn_k_w), "k_b": L0_gnn_k_b,
        "gmap_w": L0_gnn_gcn_map_w, "gmap_b": L0_gnn_gcn_map_b, "gcn_WT": np.transpose(L0_gnn_gcn_W),
        "wq": L1_gnn_Wq, "wk": L1_gnn_Wk, "wv": L1_gnn_Wv, "wo": L1_gnn_Wo, "bo": L1_gnn_bo,
    }
    arrays = {f"in_{k}": np.ascontiguousarray(a) for k, a in arrays.items()}
    nc = bacc.Bacc("TRN2", target_bir_lowering=False, num_devices=1)
    ap = {k[3:]: nc.dram_tensor(k, a.shape, mybir.dt.from_np(a.dtype), kind="ExternalInput").ap() for k, a in arrays.items()}
    ap["out"] = nc.dram_tensor("out", (B, P, D), F32, kind="ExternalOutput").ap()
    build(nc, ap)
    r = run_bass_kernel_spmd(nc, [arrays], core_ids=[0])
    return r.results[0]["out"]
```

```python
from contextlib import ExitStack

import numpy as np

import concourse.bass as bass
from concourse import mybir
from concourse.alu_op_type import AluOpType as ALU

ACT = mybir.ActivationFunctionType
AX_X = mybir.AxisListType.X
F32 = mybir.dt.float32
F32R = mybir.dt.float32r
BF16 = mybir.dt.bfloat16
I32 = mybir.dt.int32
U8 = mybir.dt.uint8

P = 128
B, D = 128, 512
KT = D // P
QUAD = 4
GROUPS = B // QUAD
DH = 64
H0, H1 = 8, 4
PAIRS0, PAIRS1 = H0 // 2, H1 // 2
INNER = H1 * DH
HB = 4
VW = DH + 2
VROW = H0 * VW + 32
NV = 96
THRESHOLD = 0.1
SCALE = DH ** -0.5
LN_EPS = 1e-5
NORM_EPS2 = 1e-16
NEG0 = -1e10 / SCALE
NEG1 = -3.3895e38
RSQRT_SEED = 1597463007.0
NEWTON = 3
EXCLUDED = 3e38
LN_OPS = 5 + 4 * NEWTON
NORM_OPS = 3 + 4 * NEWTON
BASE = 2


def count(n):
    return BASE + n


def wait_apart(eng, sem, n, passed):
    eng.wait_ge(sem, n)
    eng.sem_inc(passed, 1)


def exists(g):
    return not isinstance(g, int) or g < GROUPS


def chained(pool, sem, first, total, passed):
    done = [0]

    def link(ins, plain=False):
        ins.then_inc(sem, 1)
        done[0] += 1
        assert done[0] <= total
        if done[0] < total:
            if plain:
                wait_apart(pool, sem, first + done[0], passed)
            else:
                pool.wait_ge(sem, first + done[0])

    return link


def rsqrt_steps(nc, link, y, v, vh, a, minus_half, three_halves):
    tt = nc.gpsimd.tensor_tensor
    link(tt(vh, v, minus_half, ALU.mult), plain=True)
    link(nc.gpsimd.tensor_scalar(y.bitcast(I32), v.bitcast(I32), -0.5, RSQRT_SEED, ALU.mult, ALU.add))
    for _ in range(NEWTON):
        link(tt(a, y, y, ALU.mult))
        link(tt(a, a, vh, ALU.mult))
        link(tt(a, a, three_halves, ALU.add))
        link(tt(y, a, y, ALU.mult))


def row_stats(nc, dve, x, st, bn_done, first, passed):
    nc.vector.bn_stats(st[:, 0:6], x).then_inc(bn_done, 1)
    wait_apart(dve, bn_done, first + 1, passed)
    nc.vector.bn_aggr(st[:, 6:8], st[:, 0:6]).then_inc(bn_done, 1)


def layer_norm_factors(nc, pool, ln_chain, first, passed, st, consts):
    link = chained(pool, ln_chain, first, LN_OPS, passed)
    mean, var, vh, a = st[:, 6:7], st[:, 7:8], st[:, 8:9], st[:, 9:10]
    rstd, nbias = st[:, 10:11], st[:, 11:12]
    tt = nc.gpsimd.tensor_tensor
    link(tt(var, var, consts[:, 2, 0:1], ALU.add))
    rsqrt_steps(nc, link, rstd, var, vh, a, consts[:, 0, 0:1], consts[:, 1, 0:1])
    link(tt(nbias, mean, rstd, ALU.mult))
    link(tt(nbias, nbias, consts[:, 3, 0:1], ALU.mult))


def small_constants(nc, consts, sem):
    for n, value in enumerate((-0.5, 1.5, LN_EPS, -1.0)):
        ins = nc.gpsimd.memset(consts[:, n], value)
    ins.then_inc(sem, 1)


def rounds(eng, body, peeled=1):
    pairs = GROUPS // 2
    with eng.Fori(0, pairs - peeled) as i:
        body(i, 0, True, True)
        body(i, 1, True, True)
    for pair in range(pairs - peeled, pairs):
        last = pair == pairs - 1
        body(pair, 0, True, not last)
        body(pair, 1, not last, not last)


def split_products(pe, out, lhs_hi, lhs_lo, rhs_hi, rhs_lo, kts):
    last = None
    n = 0
    for kt in range(kts):
        for a, b in ((lhs_hi, rhs_hi), (lhs_hi, rhs_lo), (lhs_lo, rhs_hi)):
            last = pe.matmul(out, a(kt), b(kt), start=(n == 0), stop=(n == 3 * kts - 1))
            n += 1
    return last


def identities(nc, pool, ident, negi, neg, s_ident):
    nc.gpsimd.memset(ident[:], 0.0)
    nc.gpsimd.memset(negi[:], 0.0).then_inc(s_ident, 1)
    pool.wait_ge(s_ident, 1)
    nc.gpsimd.affine_select(out=ident[:], in_=ident[:], compare_op=ALU.not_equal, fill=1.0, base=0,
                            pattern=[[-1, P]], channel_multiplier=1)
    nc.gpsimd.affine_select(out=negi[:], in_=negi[:], compare_op=ALU.not_equal, fill=neg, base=0,
                            pattern=[[-1, P]], channel_multiplier=1).then_inc(s_ident, 1)


def layer0(nc, x, adj, map_w, map_wT, map_b, q_wT, q_b, k_wT, k_b, gmap_w, gmap_b, gcn_WT, x1):
    with ExitStack() as ctx:
        def sb(name, shape, dt=F32):
            return ctx.enter_context(nc.sbuf_tensor(name, shape, dt))

        def bank(name):
            return ctx.enter_context(nc.psum_tensor(name, [P, 512], F32))

        def sem(name):
            return ctx.enter_context(nc.semaphore(name))

        w_hi = {k: sb(f"w{k}_hi", [P, KT, D], F32R) for k in "qkmv"}
        w_lo = {k: sb(f"w{k}_lo", [P, KT, D], F32R) for k in "qkmv"}
        ident = sb("ident", [P, P])
        negi = sb("negi", [P, P], BF16)
        mb = sb("mb", [P, D])
        vb = sb("vb", [P, D])
        qb = sb("qb", [P, KT])
        kb = sb("kb", [P, KT])
        bcols = sb("bcols", [P, 4, KT])
        qk = sb("qk", [P, 2 * KT * D + 2 * KT * 2 * D])
        q_sb = qk[:, 0:2 * KT * D].rearrange("p (g b n) -> p g b n", g=2, b=KT)
        k_bd = qk[:, 2 * KT * D:].rearrange("p (g b s n) -> p g b s n", g=2, b=KT, s=2)
        raw = [qk[:, n * KT * D:(n + 1) * KT * D].rearrange("p (k n) -> p k n", k=KT) for n in range(5)]
        raw_mapT, raw_map, raw_q, raw_k, raw_g = raw
        gw_bd = qk[:, 5 * KT * D:5 * KT * D + P]
        gb_rows = qk[:, 5 * KT * D + P:5 * KT * D + P + KT * P].rearrange("p (k n) -> p k n", k=KT)
        hT_hi = sb("hT_hi", [P, KT, QUAD * P], F32R)
        hT_lo = sb("hT_lo", [P, KT, QUAD * P], F32R)
        xg = sb("xg", [P, QUAD, D])
        h = sb("h", [P, 2, D])
        ln_st = sb("ln_st", [P, QUAD, 12])
        m_sb = sb("m_sb", [P, QUAD, D])
        sq = sb("sq", [P, D])
        norm_st = sb("norm_st", [P, 4, H0])
        consts = sb("consts", [P, 4, H0])
        nT = sb("nT", [P, 2, KT, P])
        nT_bd = sb("nT_bd", [P, 2, KT, 2, P])
        v_sb = sb("v_sb", [P, QUAD + 1, VROW])
        mask_u8 = sb("mask_u8", [P, 2, QUAD, P], U8)
        mask = sb("mask", [P, 2, QUAD, P], BF16)
        bound = sb("bound", [P, 2, QUAD])
        negmax = sb("negmax", [P, 2, HB])
        zsum = sb("zsum", [P, 2, HB])
        probs = sb("probs", [P, HB, P])
        cprobs = sb("cprobs", [P, HB, P])
        cpT = sb("cpT", [P, HB, P])
        epi_st = sb("epi_st", [P, 2, HB])
        xres = sb("xres", [P, 2, D])
        o_sb = sb("o_sb", [P, 2, D])

        ps_s, ps_c, ps_pt, ps_av = bank("ps_s"), bank("ps_c"), bank("ps_pt"), bank("ps_av")
        ps_pj = [bank("ps_pj0"), bank("ps_pj1")]
        ps_th, ps_tn = bank("ps_th"), bank("ps_tn")

        raw_loaded, const_loaded, x_loaded = sem("raw_loaded"), sem("const_loaded"), sem("x_loaded")
        mask_loaded = [sem(f"mask_loaded{n}") for n in range(2)]
        xres_loaded = [sem(f"xres_loaded{n}") for n in range(2)]
        o_stored = [sem(f"o_stored{n}") for n in range(2)]
        s_ident, prep_zero, prep_mm, prep_hi, prep_lo, prep_bias, prep_done = (
            sem(n) for n in ("s_ident", "prep_zero", "prep_mm", "prep_hi", "prep_lo", "prep_bias", "prep_done"))
        th_ready, tn_ready, pj_ready, s_ready, c_ready, pt_ready, av_ready = pe_sems = [
            sem(n) for n in ("th_ready", "tn_ready", "pj_ready", "s_ready", "c_ready", "pt_ready", "av_ready")]
        relu_done, hhi_done, q_done, ka_done, sq_done, nT_done, exp_done, cpT_done = act_sems = [
            sem(n) for n in ("relu_done", "hhi_done", "q_done", "ka_done", "sq_done", "nT_done", "exp_done", "cpT_done")]
        bn_done, sum_done, n_done, epi_chain, hlo_done, kb_done, m_done, v_done, nbd_done, negmax_done, cp_done = dve_sems = [
            sem(n) for n in ("bn_done", "sum_done", "n_done", "epi_chain", "hlo_done", "kb_done", "m_done", "v_done",
                             "nbd_done", "negmax_done", "cp_done")]
        passed_dve, passed_sp, passed_pool = sem("passed_dve"), sem("passed_sp"), sem("passed_pool")
        mask_ready, res_done, ln_chain, norm_chain = pool_sems = [
            sem(n) for n in ("mask_ready", "res_done", "ln_chain", "norm_chain")]
        EPI_OPS = 3

        xt = x.rearrange("(g j) p d -> g p j d", j=QUAD)
        adjt = adj.rearrange("(g j) p d -> g p j d", j=QUAD)
        x1t = x1.rearrange("(g j) p d -> g j p d", j=QUAD)
        xrt = x.rearrange("(g j) p d -> g j p d", j=QUAD)

        def vslot(par, j):
            return j if j < QUAD - 1 else j + par

        def tiles(t):
            return [t[:, kt, :] for kt in range(KT)]

        block = ctx.enter_context(nc.Block())

        @block.sync
        def _(sp):
            for dst, src in ((raw_mapT, map_wT), (raw_map, map_w), (raw_q, q_wT), (raw_k, k_wT), (raw_g, gmap_w)):
                sp.dma_start(dst, src.rearrange("(k p) n -> p k n", p=P)).then_inc(raw_loaded, 16)
            sp.dma_start(xg[:], xt[0]).then_inc(x_loaded, 16)
            for n in range(2):
                sp.dma_start(mask_u8[:, n], adjt[n]).then_inc(mask_loaded[n], 16)
            sp.dma_start(mb[:], map_b.partition_broadcast(P)).then_inc(const_loaded, 16)
            for n, b in enumerate((map_b, q_b, k_b, gmap_b)):
                with nc.allow_non_contiguous_dma("512 floats, once"):
                    sp.dma_start(bcols[:, n, :], b.rearrange("(k p) -> p k", p=P)).then_inc(const_loaded, 16)
            sp.wait_ge(prep_zero, 2)
            for n in range(2):
                sp.dma_start(gw_bd[DH * n:DH * n + DH, DH * n:DH * n + DH], gcn_WT).then_inc(const_loaded, 16)
            sp.wait_ge(relu_done, count(QUAD))
            sp.dma_start(xg[:], xt[1]).then_inc(x_loaded, 16)

            def body(pair, par, proj, ahead):
                t = 2 * pair + par
                if ahead:
                    wait_apart(sp, relu_done, count(QUAD * (t + 2)), passed_sp)
                    sp.dma_start(xg[:], xt[t + 2]).then_inc(x_loaded, 16)
                    wait_apart(sp, mask_ready, count(t + 1), passed_sp)
                    sp.dma_start(mask_u8[:, par], adjt[t + 2]).then_inc(mask_loaded[par], 16)

                def load_residual(j):
                    wait_apart(sp, res_done, count(QUAD * t + j - 1), passed_sp)
                    sp.dma_start(xres[:, j % 2], xrt[t, j]).then_inc(xres_loaded[j % 2], 16)

                load_residual(0)
                for j in range(QUAD):
                    if j + 1 < QUAD:
                        load_residual(j + 1)
                    wait_apart(sp, res_done, count(QUAD * t + j + 1), passed_sp)
                    sp.dma_start(x1t[t, j], o_sb[:, j % 2]).then_inc(o_stored[j % 2], 16)

            rounds(sp, body)
            for n in range(2):
                sp.wait_ge(o_stored[n], BASE + 16 * (B // 2))

        @block.gpsimd
        def _(pool):
            for s in (*pool_sems, *o_stored):
                pool.sem_inc(s, BASE)
            nc.gpsimd.memset(gw_bd, 0.0).then_inc(prep_zero, 1)
            identities(nc, pool, ident, negi, NEG0, s_ident)
            nc.gpsimd.memset(nT_bd[:], 0.0)
            nc.gpsimd.memset(v_sb[:], 1.0).then_inc(s_ident, 1)
            small_constants(nc, consts, s_ident)
            pool.wait_ge(s_ident, 4)
            pool.wait_ge(prep_mm, 2 * KT + KT + 2)
            pool.wait_ge(prep_lo, 4 * KT)
            nc.gpsimd.memset(k_bd[DH:P, :, :, 0, :], 0.0).then_inc(prep_done, 1)
            pool.wait_ge(prep_done, 2)

            def convert_mask(pair, par):
                t = 2 * pair + par
                pool.wait_ge(mask_loaded[par], 16 * (pair + 1))
                pool.wait_ge(s_ready, count(2 * QUAD * (t - 1)) if not isinstance(t, int) or t else BASE)
                wait_apart(pool, epi_chain, count(EPI_OPS * 2 * QUAD * (t - 1)) if not isinstance(t, int) or t else BASE, passed_pool)
                nc.gpsimd.tensor_scalar(bound[:, par, :], mask_u8[:, par, :, 0], EXCLUDED, THRESHOLD, ALU.mult, ALU.add)
                nc.gpsimd.tensor_copy(mask[:, par], mask_u8[:, par]).then_inc(mask_ready, 1)

            def factors(g, j):
                pool.wait_ge(bn_done, count(2 * (QUAD * g + j + 1)))
                layer_norm_factors(nc, pool, ln_chain, count(LN_OPS * (QUAD * g + j)), passed_pool, ln_st[:, j], consts)

            def head_norms(g, j):
                wait_apart(pool, sum_done, count(QUAD * g + j + 1), passed_pool)
                n2, r, a, vh = (norm_st[:, n] for n in range(4))
                link = chained(pool, norm_chain, count(NORM_OPS * (QUAD * g + j)), NORM_OPS, passed_pool)
                link(nc.gpsimd.tensor_scalar(n2, n2, NORM_EPS2, None, ALU.max))
                rsqrt_steps(nc, link, r, n2, vh, a, consts[:, 0], consts[:, 1])

            def add_residual(t, j):
                pool.wait_ge(xres_loaded[j % 2], 16 * (2 * t + j // 2 + 1))
                pool.wait_ge(epi_chain, count(EPI_OPS * (8 * t + 2 * j + 2)))
                nc.gpsimd.tensor_tensor(o_sb[:, j % 2], o_sb[:, j % 2], xres[:, j % 2], ALU.add).then_inc(res_done, 1)

            convert_mask(0, 0)
            for g in range(2):
                for j in range(QUAD):
                    factors(g, j)
            for j in range(3):
                head_norms(0, j)

            def body(pair, par, proj, ahead):
                t = 2 * pair + par
                for u in range(8):
                    if u == 0:
                        head_norms(t, 3)
                    if proj and u == 0:
                        convert_mask(pair + par, 1 - par)
                    if proj and u in (5, 6, 7):
                        head_norms(t + 1, u - 5)
                    if ahead and u in (1, 2, 4, 5):
                        factors(t + 2, (1, 2, 4, 5).index(u))
                    if u % 2:
                        add_residual(t, u // 2)

            rounds(pool, body)

        @block.scalar
        def _(act):
            for s in act_sems:
                act.sem_inc(s, BASE)
            for n, kind in enumerate(["q"] * KT + ["k"] * KT + ["v"] * KT):
                act.wait_ge(prep_mm, n + 1)
                nc.scalar.activation(w_hi[kind][:, n % KT, :], ps_pj[n % 2][:], ACT.Copy,
                                     scale=SCALE if kind == "q" else 1.0).then_inc(prep_hi, 1)
            act.wait_ge(raw_loaded, 16 * 5)
            nc.scalar.copy(w_hi["m"][:], raw_mapT).then_inc(prep_hi, 1)

            def relu(g, j):
                act.wait_ge(ln_chain, count(LN_OPS * (QUAD * g + j + 1)))
                act.wait_ge(th_ready, count(QUAD * g + j - 1))
                nc.scalar.activation(h[:, j % 2], xg[:, j], ACT.Relu, bias=ln_st[:, j, 11:12],
                                     scale=ln_st[:, j, 10:11]).then_inc(relu_done, 1)

            def hT_high(g, j):
                act.wait_ge(th_ready, count(QUAD * g + j + 1))
                nc.scalar.copy(hT_hi[:, :, j * P:(j + 1) * P],
                               ps_th[:].rearrange("p (k n) -> p k n", k=KT)).then_inc(hhi_done, 1)

            def q_copy(g, par, b):
                act.wait_ge(pj_ready, count(16 * g + 2 * b + 1))
                nc.scalar.activation(q_sb[:, par, b], ps_pj[0][:], ACT.Identity, bias=qb[:, b:b + 1]).then_inc(q_done, 1)

            def k_copy(g, par, b):
                act.wait_ge(pj_ready, count(16 * g + 2 * b + 2))
                nc.scalar.activation(k_bd[0:DH, par, b, 0], ps_pj[1][0:DH, :], ACT.Identity,
                                     bias=kb[0:DH, b:b + 1]).then_inc(ka_done, 1)

            def square(g, j):
                act.wait_ge(m_done, count(QUAD * g + j + 1))
                act.wait_ge(sum_done, count(QUAD * g + j))
                nc.scalar.activation(sq[:], m_sb[:, j], ACT.Square).then_inc(sq_done, 1)

            def nT_copy(g, j):
                act.wait_ge(tn_ready, count(QUAD * g + j + 1))
                nc.scalar.copy(nT[:, j % 2], ps_tn[:].rearrange("p (k n) -> p k n", k=KT)).then_inc(nT_done, 1)

            def exps(t, u):
                n = 8 * t + u
                act.wait_ge(negmax_done, count(n + 1))
                act.wait_ge(cp_done, count(n))
                act.wait_ge(epi_chain, count(EPI_OPS * (n - 1))
                            if not isinstance(n, int) or n else BASE)
                for hh in range(HB):
                    last = nc.scalar.activation(probs[:, hh], ps_s[:, hh * P:(hh + 1) * P], ACT.Exp,
                                                bias=negmax[:, u % 2, hh:hh + 1],
                                                accum_out=zsum[:, u % 2, hh:hh + 1])
                last.then_inc(exp_done, 1)

            def cpT_copy(t, u):
                n = 8 * t + u
                act.wait_ge(pt_ready, count(n + 1))
                act.wait_ge(av_ready, count(n))
                nc.scalar.copy(cpT[:], ps_pt[:].rearrange("p (h n) -> p h n", h=HB)).then_inc(cpT_done, 1)

            for j in range(QUAD):
                relu(0, j)
                hT_high(0, j)
            act.wait_ge(prep_bias, 7)
            act.wait_ge(prep_done, 2)
            for b in range(KT):
                q_copy(0, 0, b)
                k_copy(0, 0, b)
            for j in range(QUAD):
                relu(1, j)
                hT_high(1, j)
            for j in range(3):
                square(0, j)
            nT_copy(0, 0)
            exps(0, 0)

            def body(pair, par, proj, ahead):
                t = 2 * pair + par
                for u in range(8):
                    if proj and u < KT:
                        q_copy(t + 1, 1 - par, u)
                    cpT_copy(t, u)
                    if ahead and u in (2, 3, 5, 6):
                        relu(t + 2, (2, 3, 5, 6).index(u))
                    if u == 0:
                        square(t, 3)
                    if proj and u in (5, 6, 7):
                        square(t + 1, u - 5)
                    if u in (1, 3, 5):
                        nT_copy(t, (u + 1) // 2)
                    if proj and u == 7:
                        nT_copy(t + 1, 0)
                    if proj and u < KT:
                        k_copy(t + 1, 1 - par, u)
                    if ahead and u >= 4:
                        hT_high(t + 2, u - 4)
                    if u < 7 or proj:
                        exps(t + (u + 1) // 8, (u + 1) % 8)

            rounds(act, body)

        @block.vector
        def _(dve):
            for s in dve_sems:
                dve.sem_inc(s, BASE)

            nc.vector.memset(gb_rows, 0.0).then_inc(prep_zero, 1)
            for n, kind in enumerate(["q"] * KT + ["k"] * KT + ["v"] * KT):
                if n == 0:
                    dve.wait_ge(const_loaded, 16 * 7)
                    dve.wait_ge(prep_zero, 2)
                    for b in range(KT):
                        ins = nc.vector.tensor_scalar(gb_rows[:, b], gb_rows[:, b], bcols[:, 3, b:b + 1], None, ALU.add)
                    ins.then_inc(prep_bias, 1)
                dve.wait_ge(prep_hi, n + 1)
                nc.vector.scalar_tensor_tensor(w_lo[kind][:, n % KT, :], ps_pj[n % 2][:],
                                               SCALE if kind == "q" else 1.0,
                                               w_hi[kind][:, n % KT, :].bitcast(F32), ALU.mult,
                                               ALU.subtract).then_inc(prep_lo, 1)
            dve.wait_ge(prep_hi, 3 * KT + 1)
            for kt in range(KT):
                nc.vector.tensor_tensor(w_lo["m"][:, kt], raw_mapT[:, kt], w_hi["m"][:, kt].bitcast(F32),
                                        ALU.subtract).then_inc(prep_lo, 1)
            dve.wait_ge(prep_mm, 3 * KT + 2)
            nc.vector.tensor_tensor(qb[:], ps_th[:, 0:KT], bcols[:, 1], ALU.add).then_inc(prep_bias, 1)
            nc.vector.tensor_tensor(kb[:], ps_th[:, KT:2 * KT], bcols[:, 2], ALU.add).then_inc(prep_bias, 1)
            dve.wait_ge(prep_bias, 3)
            nc.vector.tensor_scalar(qb[:], qb[:], SCALE, None, ALU.mult).then_inc(prep_bias, 1)
            nc.vector.tensor_copy(vb[:], ps_tn[:]).then_inc(prep_bias, 1)
            dve.wait_ge(prep_bias, 5)
            dve.wait_ge(prep_lo, 4 * KT)
            dve.sem_inc(prep_bias, 2)
            nc.vector.memset(k_bd[0:DH, :, :, 1, :], 0.0).then_inc(prep_done, 1)

            def stats(g, j):
                dve.wait_ge(x_loaded, 16 * (g + 1))
                row_stats(nc, dve, xg[:, j], ln_st[:, j], bn_done, count(2 * (QUAD * g + j)), passed_dve)

            def hT_low(g, j):
                dve.wait_ge(hhi_done, count(QUAD * g + j + 1))
                cols = slice(j * P, (j + 1) * P)
                nc.vector.tensor_tensor(hT_lo[:, :, cols], ps_th[:].rearrange("p (k n) -> p k n", k=KT),
                                        hT_hi[:, :, cols].bitcast(F32), ALU.subtract).then_inc(hlo_done, 1)

            def k_copy(g, par, b):
                dve.wait_ge(pj_ready, count(16 * g + 2 * b + 2))
                nc.vector.tensor_scalar(k_bd[DH:P, par, b, 1], ps_pj[1][DH:P, :], kb[DH:P, b:b + 1], None,
                                        ALU.add).then_inc(kb_done, 1)

            def m_copy(g, j):
                dve.wait_ge(pj_ready, count(16 * g + 8 + 2 * j + 1))
                nc.vector.tensor_tensor(m_sb[:, j], ps_pj[0][:], mb[:], ALU.add).then_inc(m_done, 1)

            def v_copy(g, par, j):
                dve.wait_ge(pj_ready, count(16 * g + 8 + 2 * j + 2))
                dst = v_sb[:, vslot(par, j), 0:H0 * VW].rearrange("p (h c) -> p h c", h=H0)[:, :, 0:DH]
                nc.vector.tensor_tensor(dst, ps_pj[1][:].rearrange("p (h c) -> p h c", h=H0),
                                        vb[:].rearrange("p (h c) -> p h c", h=H0), ALU.add).then_inc(v_done, 1)

            def head_sums(g, j):
                dve.wait_ge(sq_done, count(QUAD * g + j + 1))
                nc.vector.tensor_reduce(norm_st[:, 0], sq[:].rearrange("p (h c) -> p h c", h=H0), AX_X,
                                        ALU.add).then_inc(sum_done, 1)

            def normalise(g, j):
                heads = m_sb[:, j].rearrange("p (h c) -> p h c", h=H0)
                dve.wait_ge(norm_chain, count(NORM_OPS * (QUAD * g + j + 1)))
                nc.vector.tensor_tensor(heads, heads, norm_st[:, 1].unsqueeze(2).to_broadcast([P, H0, DH]),
                                        ALU.mult).then_inc(n_done, 1)

            def nT_blocks(g, j):
                dve.wait_ge(nT_done, count(QUAD * g + j + 1))
                nc.vector.tensor_copy(nT_bd[0:DH, j % 2, :, 0], nT[0:DH, j % 2])
                nc.vector.tensor_copy(nT_bd[DH:P, j % 2, :, 1], nT[DH:P, j % 2]).then_inc(nbd_done, 1)

            def row_max(t, u):
                dve.wait_ge(s_ready, count(8 * t + u + 1))
                nc.vector.tensor_reduce(negmax[:, u % 2], ps_s[:].rearrange("p (h n) -> p h n", h=HB), AX_X,
                                        ALU.max, negate=True).then_inc(negmax_done, 1)

            def select_similar(t, par, u):
                n, j = 8 * t + u, u // 2
                dve.wait_ge(exp_done, count(n + 1))
                dve.wait_ge(c_ready, count(n + 1))
                dve.wait_ge(pt_ready, count(n))
                nc.vector.scalar_tensor_tensor(cprobs[:], ps_c[:].rearrange("p (h n) -> p h n", h=HB), 
                                               bound[:, par, j:j + 1], probs[:], ALU.is_gt, ALU.mult).then_inc(cp_done, 1)

            def epilogue(t, u):
                n = 8 * t + u
                j, half = u // 2, u % 2
                first = count(EPI_OPS * n)
                av = ps_av[:].rearrange("p (h n) -> p h n", h=HB)
                den, rec = epi_st[:, 0], epi_st[:, 1]
                dve.wait_ge(av_ready, count(n + 1))
                nc.vector.tensor_tensor(den, av[:, :, DH], zsum[:, u % 2], ALU.add).then_inc(epi_chain, 1)
                dve.wait_ge(epi_chain, first + 1)
                nc.vector.reciprocal(rec, den).then_inc(epi_chain, 1)
                dve.wait_ge(epi_chain, first + 2)
                if half == 0:
                    dve.wait_ge(o_stored[j % 2], BASE + 16 * (2 * t + j // 2))
                dst = o_sb[:, j % 2, half * HB * DH:(half + 1) * HB * DH].rearrange("p (h c) -> p h c", h=HB)
                nc.vector.scalar_tensor_tensor(dst, av[:, :, 0:DH], 0.0, rec.unsqueeze(2).to_broadcast([P, HB, DH]),
                                               ALU.max, ALU.mult).then_inc(epi_chain, 1)

            for j in range(QUAD):
                stats(0, j)
                hT_low(0, j)
            for b in range(KT):
                k_copy(0, 0, b)
            for j in range(QUAD):
                m_copy(0, j)
                v_copy(0, 0, j)
                stats(1, j)
                hT_low(1, j)
            for j in range(3):
                head_sums(0, j)
                if j < 2:
                    normalise(0, j)
            nT_blocks(0, 0)
            row_max(0, 0)

            def body(pair, par, proj, ahead):
                t = 2 * pair + par
                dve.wait_ge(mask_ready, count(t + 1))
                for u in range(8):
                    select_similar(t, par, u)
                    if ahead and u in (1, 2, 4, 5):
                        stats(t + 2, (1, 2, 4, 5).index(u))
                    if u < 2:
                        normalise(t, 2 + u)
                    if proj and u in (6, 7):
                        normalise(t + 1, u - 6)
                    if proj and u >= 4:
                        m_copy(t + 1, u - 4)
                    if u == 0:
                        head_sums(t, 3)
                    if proj and u in (5, 6, 7):
                        head_sums(t + 1, u - 5)
                    if u in (1, 3, 5):
                        nT_blocks(t, (u + 1) // 2)
                    if proj and u == 7:
                        nT_blocks(t + 1, 0)
                    if proj and u < KT:
                        k_copy(t + 1, 1 - par, u)
                    if proj and u >= 4:
                        v_copy(t + 1, 1 - par, u - 4)
                    epilogue(t, u)
                    if ahead and u >= 4:
                        hT_low(t + 2, u - 4)
                    if u < 7 or proj:
                        row_max(t + (u + 1) // 8, (u + 1) % 8)

            rounds(dve, body)

        @block.tensor
        def _(pe):
            for s in pe_sems:
                pe.sem_inc(s, BASE)
            pe.wait_ge(raw_loaded, 16 * 5)
            pe.wait_ge(const_loaded, 16 * 7)
            for n in range(3 * KT):
                if n >= 2:
                    pe.wait_ge(prep_lo, n - 1)
                out = ps_pj[n % 2]
                rows = slice((n % KT) * P, (n % KT + 1) * P)
                if n < 2 * KT:
                    rhs = raw_q if n < KT else raw_k
                    for mk in range(KT):
                        mm = nc.tensor.matmul(out[:], raw_map[:, mk, rows], rhs[:, mk, :], start=(mk == 0), stop=(mk == KT - 1))
                else:
                    for pr in range(PAIRS0):
                        mm = nc.tensor.matmul(out[:, pr * P:(pr + 1) * P], raw_g[:, pr, rows], gw_bd, start=True, stop=True)
                mm.then_inc(prep_mm, 1)
            for n in range(2 * KT):
                rhs = raw_q if n < KT else raw_k
                cols = slice((n % KT) * P, (n % KT + 1) * P)
                for mk in range(KT):
                    mm = nc.tensor.matmul(ps_th[:, n:n + 1], rhs[:, mk, cols], bcols[:, 0, mk:mk + 1], start=(mk == 0), stop=(mk == KT - 1))
            mm.then_inc(prep_mm, 1)
            pe.wait_ge(prep_bias, 1)
            for pr in range(PAIRS0):
                mm = nc.tensor.matmul(ps_tn[:, pr * P:(pr + 1) * P], gb_rows[:, pr, :], gw_bd, start=True, stop=True)
            mm.then_inc(prep_mm, 1)
            pe.wait_ge(s_ident, 4)
            pe.wait_ge(prep_bias, 5)
            pe.wait_ge(prep_lo, 4 * KT)
            pe.wait_ge(prep_done, 2)

            def h_transpose(g, j):
                pe.wait_ge(relu_done, count(QUAD * g + j + 1))
                pe.wait_ge(hlo_done, count(QUAD * g + j))
                for kt in range(KT):
                    mm = nc.tensor.transpose(ps_th[:, kt * P:(kt + 1) * P], h[:, j % 2, kt * P:(kt + 1) * P], ident[:])
                mm.then_inc(th_ready, 1)

            def n_transpose(g, j):
                pe.wait_ge(n_done, count(QUAD * g + j + 1))
                pe.wait_ge(nT_done, count(QUAD * g + j))
                for kt in range(KT):
                    mm = nc.tensor.transpose(ps_tn[:, kt * P:(kt + 1) * P], m_sb[:, j, kt * P:(kt + 1) * P], ident[:])
                mm.then_inc(tn_ready, 1)

            def by_channel(kind, b, out):
                cols = slice(b * P, (b + 1) * P)
                split_products(nc.tensor, out, lambda k: w_hi[kind][:, k, cols], lambda k: w_lo[kind][:, k, cols],
                               lambda k: hT_hi[:, k, :], lambda k: hT_lo[:, k, :], KT).then_inc(pj_ready, 1)

            def by_node(kind, j, out):
                cols = slice(j * P, (j + 1) * P)
                split_products(nc.tensor, out, lambda k: hT_hi[:, k, cols], lambda k: hT_lo[:, k, cols],
                               lambda k: w_hi[kind][:, k, :], lambda k: w_lo[kind][:, k, :], KT).then_inc(pj_ready, 1)

            def project_q(g, b):
                if b == 0:
                    pe.wait_ge(hlo_done, count(QUAD * g + QUAD))
                    pe.wait_ge(m_done, count(QUAD * g))
                else:
                    pe.wait_ge(q_done, count(QUAD * g + b))
                by_channel("q", b, ps_pj[0][:])

            def project_k(g, b):
                if b == 0:
                    pe.wait_ge(v_done, count(QUAD * g))
                else:
                    pe.wait_ge(ka_done, count(QUAD * g + b))
                    pe.wait_ge(kb_done, count(QUAD * g + b))
                by_channel("k", b, ps_pj[1][:])

            def project_m(g, j):
                if j == 0:
                    pe.wait_ge(q_done, count(QUAD * g + QUAD))
                else:
                    pe.wait_ge(m_done, count(QUAD * g + j))
                by_node("m", j, ps_pj[0][:])

            def project_v(g, j):
                if j == 0:
                    pe.wait_ge(ka_done, count(QUAD * g + QUAD))
                    pe.wait_ge(kb_done, count(QUAD * g + QUAD))
                else:
                    pe.wait_ge(v_done, count(QUAD * g + j))
                by_node("v", j, ps_pj[1][:])

            def scores(t, par, u):
                n = 8 * t + u
                j, half = u // 2, u % 2
                cols = slice(j * P, (j + 1) * P)
                if u == 0:
                    pe.wait_ge(q_done, count(QUAD * t + QUAD))
                    pe.wait_ge(ka_done, count(QUAD * t + QUAD))
                    pe.wait_ge(kb_done, count(QUAD * t + QUAD))
                    pe.wait_ge(mask_ready, count(t + 1))
                pe.wait_ge(exp_done, count(n))
                nc.tensor.matmul(ps_s[:].rearrange("p (h n) -> p h n", h=HB), negi[:],
                                 mask[:, par, j:j + 1, :].to_broadcast([P, HB, P]), start=True, stop=False)
                for pl in range(2):
                    pr = 2 * half + pl
                    mm = nc.tensor.matmul(ps_s[:, 2 * pl * P:2 * (pl + 1) * P].rearrange("p (h n) -> p h n", h=2), q_sb[:, par, pr, cols], k_bd[:, par, pr, :, cols],
                                          start=False, stop=(pl == 1))
                mm.then_inc(s_ready, 1)
                pe.wait_ge(cp_done, count(n))
                if half == 0:
                    pe.wait_ge(nbd_done, count(QUAD * t + j + 1))
                for pl in range(2):
                    pr = 2 * half + pl
                    mm = nc.tensor.matmul(ps_c[:, 2 * pl * P:2 * (pl + 1) * P].rearrange("p (h n) -> p h n", h=2), nT[:, j % 2, pr, :], nT_bd[:, j % 2, pr],
                                          start=True, stop=True)
                mm.then_inc(c_ready, 1)

            def prob_transpose(t, u):
                n = 8 * t + u
                pe.wait_ge(cp_done, count(n + 1))
                pe.wait_ge(cpT_done, count(n))
                for hh in range(HB):
                    mm = nc.tensor.transpose(ps_pt[:, hh * P:(hh + 1) * P], cprobs[:, hh], ident[:])
                mm.then_inc(pt_ready, 1)

            def weigh_values(t, par, u):
                n = 8 * t + u
                j, half = u // 2, u % 2
                pe.wait_ge(cpT_done, count(n + 1))
                pe.wait_ge(epi_chain, count(EPI_OPS * n))
                pe.wait_ge(v_done, count(QUAD * t + j + 1))
                for hh in range(HB):
                    hd = HB * half + hh
                    mm = nc.tensor.matmul(ps_av[:, hh * P:hh * P + NV], cpT[:, hh],
                                          v_sb[:, vslot(par, j), hd * VW:hd * VW + NV], start=True, stop=True)
                mm.then_inc(av_ready, 1)

            for j in range(QUAD):
                h_transpose(0, j)
            for b in range(KT):
                project_q(0, b)
                project_k(0, b)
            for j in range(QUAD):
                project_m(0, j)
                project_v(0, j)
                h_transpose(1, j)
            n_transpose(0, 0)
            scores(0, 0, 0)

            def body(pair, par, proj, ahead):
                t = 2 * pair + par
                for u in range(8):
                    if proj and u < KT:
                        project_q(t + 1, u)
                    if proj and u >= KT:
                        project_m(t + 1, u - KT)
                    prob_transpose(t, u)
                    if u in (1, 3, 5):
                        n_transpose(t, (u + 1) // 2)
                    if proj and u == 7:
                        n_transpose(t + 1, 0)
                    if proj and u < KT:
                        project_k(t + 1, u)
                    if proj and u >= KT:
                        project_v(t + 1, u - KT)
                    weigh_values(t, par, u)
                    if ahead and u >= 4:
                        h_transpose(t + 2, u - 4)
                    if u < 7:
                        scores(t, par, u + 1)
                    elif proj:
                        scores(t + 1, 1 - par, 0)

            rounds(pe, body)


def layer1(nc, x1, adj, wq, wk, wv, wo, bo, out):
    with ExitStack() as ctx:
        def sb(name, shape, dt=F32):
            return ctx.enter_context(nc.sbuf_tensor("l1_" + name, shape, dt))

        def bank(name):
            return ctx.enter_context(nc.psum_tensor("l1_" + name, [P, 512], F32))

        def sem(name):
            return ctx.enter_context(nc.semaphore("l1_" + name))

        widths = {"q": (KT, INNER), "k": (KT, INNER), "v": (KT, INNER), "o": (PAIRS1, D)}
        w_hi = {k: sb(f"w{k}_hi", [P, *s], F32R) for k, s in widths.items()}
        w_lo = {k: sb(f"w{k}_lo", [P, *s], F32R) for k, s in widths.items()}
        raw = {k: sb(f"w{k}_raw", [P, *s]) for k, s in widths.items()}
        ident = sb("ident", [P, P])
        negi = sb("negi", [P, P], BF16)
        bo_rows = sb("bo_rows", [P, D])
        q_sb = sb("q_sb", [P, 2, PAIRS1, QUAD * P])
        k_bd = sb("k_bd", [P, 2, PAIRS1, 2, QUAD * P])
        v_sb = sb("v_sb", [P, 2, QUAD, INNER])
        hT_hi = sb("hT_hi", [P, 2, KT, QUAD * P], F32R)
        hT_lo = sb("hT_lo", [P, 2, KT, QUAD * P], F32R)
        xg = sb("xg", [P, QUAD, D])
        h = sb("h", [P, 2, D])
        ln_st = sb("ln_st", [P, QUAD, 12])
        consts = sb("consts", [P, 4, 1])
        mask_u8 = sb("mask_u8", [P, 2, QUAD, P], U8)
        mask = sb("mask", [P, 2, QUAD, P], BF16)
        negmax = sb("negmax", [P, 2, HB])
        zsum = sb("zsum", [P, 2, HB])
        rec = sb("rec", [P, HB])
        probs = sb("probs", [P, HB, P])
        nprobs = sb("nprobs", [P, HB, P])
        npT = sb("npT", [P, HB, P])
        aT_hi = sb("aT_hi", [P, PAIRS1, P], F32R)
        aT_lo = sb("aT_lo", [P, PAIRS1, P], F32R)
        xres = sb("xres", [P, 2, D])
        o_sb = sb("o_sb", [P, 2, D])

        ps_s, ps_pt, ps_av, ps_o, ps_th = bank("ps_s"), bank("ps_pt"), bank("ps_av"), bank("ps_o"), bank("ps_th")
        ps_pj = [bank("ps_pj0"), bank("ps_pj1")]

        raw_loaded, bo_loaded = sem("raw_loaded"), sem("bo_loaded")
        x_loaded = [sem(f"x_loaded{j}") for j in range(QUAD)]
        mask_loaded = [sem(f"mask_loaded{n}") for n in range(2)]
        xres_loaded = [sem(f"xres_loaded{n}") for n in range(2)]
        o_stored = [sem(f"o_stored{n}") for n in range(2)]
        s_ident, prep_hi, prep_lo, prep_zero = sem("s_ident"), sem("prep_hi"), sem("prep_lo"), sem("prep_zero")
        th_ready, qk_ready, vp_ready, s_ready, pt_ready, av_ready, o_ready = pe_sems = [
            sem(n) for n in ("th_ready", "qk_ready", "vp_ready", "s_ready", "pt_ready", "av_ready", "o_ready")]
        relu_done, hhi_done, q_done, ka_done, exp_done, npT_done, ahi_done = act_sems = [
            sem(n) for n in ("relu_done", "hhi_done", "q_done", "ka_done", "exp_done", "npT_done", "ahi_done")]
        bn_done, hlo_done, kb_done, v_done, negmax_done, rec_done, np_done, alo_done, out_done = dve_sems = [
            sem(n) for n in ("bn_done", "hlo_done", "kb_done", "v_done", "negmax_done", "rec_done", "np_done", "alo_done", "out_done")]
        passed_dve, passed_sp, passed_pool = sem("passed_dve"), sem("passed_sp"), sem("passed_pool")
        mask_ready, res_ready, ln_chain = pool_sems = [sem("mask_ready"), sem("res_ready"), sem("ln_chain")]

        xt = x1.rearrange("(g j) p d -> g j p d", j=QUAD)
        xrt = x1.rearrange("(g j) p d -> g j p d", j=QUAD)
        adjt = adj.rearrange("(g j) p d -> g p j d", j=QUAD)
        outt = out.rearrange("(g j) p d -> g j p d", j=QUAD)

        block = ctx.enter_context(nc.Block())

        @block.sync
        def _(sp):
            for j in range(QUAD):
                sp.dma_start(xg[:, j], xt[0, j]).then_inc(x_loaded[j], 16)
            for k, w in (("q", wq), ("k", wk), ("v", wv), ("o", wo)):
                sp.dma_start(raw[k][:], w.rearrange("(k p) n -> p k n", p=P)).then_inc(raw_loaded, 16)
            for n in range(2):
                sp.dma_start(mask_u8[:, n], adjt[n]).then_inc(mask_loaded[n], 16)
            sp.dma_start(bo_rows[:], bo.partition_broadcast(P)).then_inc(bo_loaded, 16)
            for g in (1, 2):
                for j in range(QUAD):
                    sp.wait_ge(relu_done, count(QUAD * (g - 1) + j + 1))
                    sp.dma_start(xg[:, j], xt[g, j]).then_inc(x_loaded[j], 16)

            def body(pair, par, proj, ahead):
                t = 2 * pair + par
                if ahead:
                    wait_apart(sp, mask_ready, count(t + 1), passed_sp)
                    sp.dma_start(mask_u8[:, par], adjt[t + 2]).then_inc(mask_loaded[par], 16)

                def load_residual(j):
                    wait_apart(sp, out_done, count(QUAD * t + j - 1), passed_sp)
                    sp.dma_start(xres[:, j % 2], xrt[t, j]).then_inc(xres_loaded[j % 2], 16)

                load_residual(0)
                for j in range(QUAD):
                    if ahead and exists(t + 3):
                        wait_apart(sp, relu_done, count(QUAD * (t + 2) + j + 1), passed_sp)
                        sp.dma_start(xg[:, j], xt[t + 3, j]).then_inc(x_loaded[j], 16)
                    if j + 1 < QUAD:
                        load_residual(j + 1)
                    wait_apart(sp, out_done, count(QUAD * t + j + 1), passed_sp)
                    sp.dma_start(outt[t, j], o_sb[:, j % 2]).then_inc(o_stored[j % 2], 16)

            rounds(sp, body, peeled=2)
            for n in range(2):
                sp.wait_ge(o_stored[n], BASE + 16 * (B // 2))

        @block.gpsimd
        def _(pool):
            for s in (*pool_sems, *o_stored):
                pool.sem_inc(s, BASE)
            identities(nc, pool, ident, negi, NEG1, s_ident)
            small_constants(nc, consts, s_ident)
            pool.wait_ge(s_ident, 3)
            nc.gpsimd.memset(k_bd[:], 0.0).then_inc(prep_zero, 1)
            pool.wait_ge(bo_loaded, 16)

            def convert_mask(pair, par):
                t = 2 * pair + par
                pool.wait_ge(mask_loaded[par], 16 * (pair + 1))
                wait_apart(pool, s_ready, count(QUAD * (t - 1)) if not isinstance(t, int) or t else BASE, passed_pool)
                nc.gpsimd.tensor_scalar(mask[:, par], mask_u8[:, par], -1.0, 1.0, ALU.mult, ALU.add).then_inc(mask_ready, 1)

            def factors(g, j):
                pool.wait_ge(bn_done, count(2 * (QUAD * g + j + 1)))
                layer_norm_factors(nc, pool, ln_chain, count(LN_OPS * (QUAD * g + j)), passed_pool, ln_st[:, j], consts)

            convert_mask(0, 0)
            for g in range(2):
                for j in range(QUAD):
                    factors(g, j)

            def body(pair, par, proj, ahead):
                t = 2 * pair + par
                for j in range(QUAD):
                    if ahead:
                        factors(t + 2, j)
                    if proj and j == 1:
                        convert_mask(pair + par, 1 - par)
                    pool.wait_ge(xres_loaded[j % 2], 16 * (2 * t + j // 2 + 1))
                    nc.gpsimd.tensor_tensor(xres[:, j % 2], xres[:, j % 2], bo_rows[:], ALU.add).then_inc(res_ready, 1)

            rounds(pool, body)

        @block.scalar
        def _(act):
            for s in act_sems:
                act.sem_inc(s, BASE)
            act.wait_ge(raw_loaded, 16 * 4)
            for k in "qkvo":
                nc.scalar.activation(w_hi[k][:], raw[k][:], ACT.Copy, scale=SCALE if k == "q" else 1.0).then_inc(prep_hi, 1)

            def relu(g, j):
                act.wait_ge(ln_chain, count(LN_OPS * (QUAD * g + j + 1)))
                act.wait_ge(th_ready, count(QUAD * g + j - 1))
                nc.scalar.activation(h[:, j % 2], xg[:, j], ACT.Relu, bias=ln_st[:, j, 11:12],
                                     scale=ln_st[:, j, 10:11]).then_inc(relu_done, 1)

            def hT_high(g, par, j):
                act.wait_ge(th_ready, count(QUAD * g + j + 1))
                nc.scalar.copy(hT_hi[:, par, :, j * P:(j + 1) * P],
                               ps_th[:].rearrange("p (k n) -> p k n", k=KT)).then_inc(hhi_done, 1)

            def qk_copy(g, par, c):
                act.wait_ge(qk_ready, count(QUAD * g + c + 1))
                if c % 2 == 0:
                    nc.scalar.copy(q_sb[:, par, c // 2], ps_pj[0][:]).then_inc(q_done, 1)
                else:
                    nc.scalar.copy(k_bd[0:DH, par, c // 2, 0], ps_pj[0][0:DH, :]).then_inc(ka_done, 1)

            def exps(t, u):
                n = QUAD * t + u
                act.wait_ge(negmax_done, count(n + 1))
                act.wait_ge(np_done, count(n))
                for hh in range(HB):
                    last = nc.scalar.activation(probs[:, hh], ps_s[:, hh * P:(hh + 1) * P], ACT.Exp,
                                                bias=negmax[:, u % 2, hh:hh + 1],
                                                accum_out=zsum[:, u % 2, hh:hh + 1])
                last.then_inc(exp_done, 1)

            def npT_copy(t, u):
                n = QUAD * t + u
                act.wait_ge(pt_ready, count(n + 1))
                act.wait_ge(av_ready, count(n))
                nc.scalar.copy(npT[:], ps_pt[:].rearrange("p (h n) -> p h n", h=HB)).then_inc(npT_done, 1)

            def aT_high(t, u):
                n = QUAD * t + u
                act.wait_ge(av_ready, count(n + 1))
                act.wait_ge(o_ready, count(n))
                nc.scalar.copy(aT_hi[:], ps_av[:, 0:PAIRS1 * P].rearrange("p (k n) -> p k n", k=PAIRS1)).then_inc(ahi_done, 1)

            for g in range(2):
                for j in range(QUAD):
                    relu(g, j)
                    hT_high(g, g, j)
            act.wait_ge(prep_zero, 1)
            for c in range(QUAD):
                qk_copy(0, 0, c)
            exps(0, 0)

            def body(pair, par, proj, ahead):
                t = 2 * pair + par
                for u in range(QUAD):
                    npT_copy(t, u)
                    if ahead:
                        relu(t + 2, u)
                    if proj:
                        qk_copy(t + 1, 1 - par, u)
                    aT_high(t, u)
                    if u < QUAD - 1 or proj:
                        exps(t + (u + 1) // QUAD, (u + 1) % QUAD)
                    if ahead:
                        hT_high(t + 2, par, u)

            rounds(act, body)

        @block.vector
        def _(dve):
            for s in dve_sems:
                dve.sem_inc(s, BASE)
            for n, k in enumerate("qkvo"):
                dve.wait_ge(prep_hi, n + 1)
                nc.vector.scalar_tensor_tensor(w_lo[k][:], raw[k][:], SCALE if k == "q" else 1.0,
                                               w_hi[k][:].bitcast(F32), ALU.mult, ALU.subtract).then_inc(prep_lo, 1)

            def stats(g, j):
                dve.wait_ge(x_loaded[j], 16 * (g + 1))
                row_stats(nc, dve, xg[:, j], ln_st[:, j], bn_done, count(2 * (QUAD * g + j)), passed_dve)

            def hT_low(g, par, j):
                dve.wait_ge(hhi_done, count(QUAD * g + j + 1))
                cols = slice(j * P, (j + 1) * P)
                nc.vector.tensor_tensor(hT_lo[:, par, :, cols], ps_th[:].rearrange("p (k n) -> p k n", k=KT),
                                        hT_hi[:, par, :, cols].bitcast(F32), ALU.subtract).then_inc(hlo_done, 1)

            def k_copy(g, par, c):
                dve.wait_ge(qk_ready, count(QUAD * g + c + 1))
                nc.vector.tensor_copy(k_bd[DH:P, par, c // 2, 1], ps_pj[0][DH:P, :]).then_inc(kb_done, 1)

            def v_copy(g, par, j):
                dve.wait_ge(vp_ready, count(QUAD * g + j + 1))
                nc.vector.tensor_copy(v_sb[:, par, j], ps_pj[1][:, 0:INNER]).then_inc(v_done, 1)

            def row_max(t, u):
                dve.wait_ge(s_ready, count(QUAD * t + u + 1))
                nc.vector.tensor_reduce(negmax[:, u % 2], ps_s[:].rearrange("p (h n) -> p h n", h=HB), AX_X,
                                        ALU.max, negate=True).then_inc(negmax_done, 1)

            def normalise(t, u):
                n = QUAD * t + u
                dve.wait_ge(exp_done, count(n + 1))
                nc.vector.reciprocal(rec[:], zsum[:, u % 2]).then_inc(rec_done, 1)
                dve.wait_ge(rec_done, count(n + 1))
                dve.wait_ge(pt_ready, count(n))
                nc.vector.tensor_tensor(nprobs[:], probs[:], rec[:].unsqueeze(2).to_broadcast([P, HB, P]),
                                        ALU.mult).then_inc(np_done, 1)

            def aT_low(t, u):
                n = QUAD * t + u
                dve.wait_ge(ahi_done, count(n + 1))
                nc.vector.tensor_tensor(aT_lo[:], ps_av[:, 0:PAIRS1 * P].rearrange("p (k n) -> p k n", k=PAIRS1),
                                        aT_hi[:].bitcast(F32), ALU.subtract).then_inc(alo_done, 1)

            def add_residual(t, u):
                dve.wait_ge(o_ready, count(QUAD * t + u + 1))
                dve.wait_ge(res_ready, count(QUAD * t + u + 1))
                dve.wait_ge(o_stored[u % 2], BASE + 16 * (2 * t + u // 2))
                nc.vector.tensor_tensor(o_sb[:, u % 2], ps_o[:], xres[:, u % 2], ALU.add).then_inc(out_done, 1)

            for g in range(2):
                for j in range(QUAD):
                    stats(g, j)
                    hT_low(g, g, j)
            dve.wait_ge(prep_zero, 1)
            for j in range(QUAD):
                if j % 2:
                    k_copy(0, 0, j)
                v_copy(0, 0, j)
            row_max(0, 0)
            stats(2, 0)
            normalise(0, 0)

            def body(pair, par, proj, ahead):
                t = 2 * pair + par
                for u in range(QUAD):
                    if proj:
                        v_copy(t + 1, 1 - par, u)
                    if proj and u % 2:
                        k_copy(t + 1, 1 - par, u)
                    aT_low(t, u)
                    following = (t + (u + 1) // QUAD, (u + 1) % QUAD)
                    if u < QUAD - 1 or proj:
                        row_max(*following)
                    if ahead and (u < QUAD - 1 or exists(t + 3)):
                        stats(following[0] + 2, following[1])
                    if u < QUAD - 1 or proj:
                        normalise(*following)
                    if ahead:
                        hT_low(t + 2, par, u)
                    add_residual(t, u)

            rounds(dve, body, peeled=2)

        @block.tensor
        def _(pe):
            for s in pe_sems:
                pe.sem_inc(s, BASE)
            pe.wait_ge(s_ident, 3)
            pe.wait_ge(prep_lo, 4)
            pe.wait_ge(prep_zero, 1)

            def h_transpose(g, j):
                pe.wait_ge(relu_done, count(QUAD * g + j + 1))
                pe.wait_ge(hlo_done, count(QUAD * g + j))
                for kt in range(KT):
                    mm = nc.tensor.transpose(ps_th[:, kt * P:(kt + 1) * P], h[:, j % 2, kt * P:(kt + 1) * P], ident[:])
                mm.then_inc(th_ready, 1)

            def project_qk(g, par, c):
                if c == 0:
                    pe.wait_ge(hlo_done, count(QUAD * g + QUAD))
                if c % 2 == 0:
                    pe.wait_ge(ka_done, count(2 * g + c // 2))
                    pe.wait_ge(kb_done, count(2 * g + c // 2))
                else:
                    pe.wait_ge(q_done, count(2 * g + c // 2 + 1))
                kind = "qk"[c % 2]
                cols = slice((c // 2) * P, (c // 2 + 1) * P)
                split_products(nc.tensor, ps_pj[0][:], lambda k: w_hi[kind][:, k, cols], lambda k: w_lo[kind][:, k, cols],
                               lambda k: hT_hi[:, par, k, :], lambda k: hT_lo[:, par, k, :], KT).then_inc(qk_ready, 1)

            def project_v(g, par, j):
                pe.wait_ge(hlo_done, count(QUAD * g + j + 1))
                pe.wait_ge(v_done, count(QUAD * g + j))
                cols = slice(j * P, (j + 1) * P)
                split_products(nc.tensor, ps_pj[1][:, 0:INNER], lambda k: hT_hi[:, par, k, cols], lambda k: hT_lo[:, par, k, cols],
                               lambda k: w_hi["v"][:, k, :], lambda k: w_lo["v"][:, k, :], KT).then_inc(vp_ready, 1)

            def scores(t, par, u):
                n = QUAD * t + u
                cols = slice(u * P, (u + 1) * P)
                if u == 0:
                    pe.wait_ge(q_done, count(2 * t + 2))
                    pe.wait_ge(ka_done, count(2 * t + 2))
                    pe.wait_ge(kb_done, count(2 * t + 2))
                    pe.wait_ge(mask_ready, count(t + 1))
                pe.wait_ge(exp_done, count(n))
                nc.tensor.matmul(ps_s[:].rearrange("p (h n) -> p h n", h=HB), negi[:],
                                 mask[:, par, u:u + 1, :].to_broadcast([P, HB, P]), start=True, stop=False)
                for pr in range(PAIRS1):
                    mm = nc.tensor.matmul(ps_s[:, 2 * pr * P:2 * (pr + 1) * P].rearrange("p (h n) -> p h n", h=2), q_sb[:, par, pr, cols], k_bd[:, par, pr, :, cols],
                                          start=False, stop=(pr == PAIRS1 - 1))
                mm.then_inc(s_ready, 1)

            def prob_transpose(t, u):
                n = QUAD * t + u
                pe.wait_ge(np_done, count(n + 1))
                pe.wait_ge(npT_done, count(n))
                for hh in range(HB):
                    mm = nc.tensor.transpose(ps_pt[:, hh * P:(hh + 1) * P], nprobs[:, hh], ident[:])
                mm.then_inc(pt_ready, 1)

            def weigh_values(t, par, u):
                n = QUAD * t + u
                pe.wait_ge(npT_done, count(n + 1))
                pe.wait_ge(alo_done, count(n))
                pe.wait_ge(v_done, count(n + 1))
                for hh in range(HB):
                    rows = slice(DH * (hh % 2), DH * (hh % 2) + DH)
                    mm = nc.tensor.matmul(ps_av[rows, (hh // 2) * P:(hh // 2 + 1) * P],
                                          v_sb[:, par, u, hh * DH:(hh + 1) * DH], npT[:, hh], start=True, stop=True)
                mm.then_inc(av_ready, 1)

            def project_out(t, u):
                n = QUAD * t + u
                pe.wait_ge(alo_done, count(n + 1))
                pe.wait_ge(out_done, count(n))
                split_products(nc.tensor, ps_o[:], lambda k: aT_hi[:, k, :], lambda k: aT_lo[:, k, :],
                               lambda k: w_hi["o"][:, k, :], lambda k: w_lo["o"][:, k, :], PAIRS1).then_inc(o_ready, 1)

            for g in range(2):
                for j in range(QUAD):
                    h_transpose(g, j)
            for c in range(QUAD):
                project_qk(0, 0, c)
                project_v(0, 0, c)
            scores(0, 0, 0)

            def body(pair, par, proj, ahead):
                t = 2 * pair + par
                for u in range(QUAD):
                    if proj:
                        project_v(t + 1, 1 - par, u)
                    prob_transpose(t, u)
                    if proj:
                        project_qk(t + 1, 1 - par, u)
                    weigh_values(t, par, u)
                    if u < QUAD - 1:
                        scores(t, par, u + 1)
                    elif proj:
                        scores(t + 1, 1 - par, 0)
                    if ahead:
                        h_transpose(t + 2, u)
                    project_out(t, u)

            rounds(pe, body)


def build(nc, ap):
    x1 = nc.dram_tensor("x1_scratch", (B, P, D), F32, kind="Internal").ap()
    layer0(nc, ap["x"], ap["adj"], ap["map_w"], ap["map_wT"], ap["map_b"], ap["q_wT"], ap["q_b"], ap["k_wT"], ap["k_b"],
           ap["gmap_w"], ap["gmap_b"], ap["gcn_WT"], x1)
    layer1(nc, x1, ap["adj"], ap["wq"], ap["wk"], ap["wv"], ap["wo"], ap["bo"], ap["out"])


def kernel(x, adj, L0_gnn_map_w, L0_gnn_map_b, L0_gnn_q_w, L0_gnn_q_b, L0_gnn_k_w, L0_gnn_k_b, L0_gnn_gcn_map_w,
           L0_gnn_gcn_map_b, L0_gnn_gcn_W, L1_gnn_Wq, L1_gnn_Wk, L1_gnn_Wv, L1_gnn_Wo, L1_gnn_bo):
    from concourse import bacc
    from concourse.bass_utils import run_bass_kernel_spmd

    arrays = {
        "x": x, "adj": adj, "map_w": L0_gnn_map_w, "map_wT": np.transpose(L0_gnn_map_w), "map_b": L0_gnn_map_b,
        "q_wT": np.transpose(L0_gnn_q_w), "q_b": L0_gnn_q_b, "k_wT": np.transpose(L0_gnn_k_w), "k_b": L0_gnn_k_b,
        "gmap_w": L0_gnn_gcn_map_w, "gmap_b": L0_gnn_gcn_map_b, "gcn_WT": np.transpose(L0_gnn_gcn_W),
        "wq": L1_gnn_Wq, "wk": L1_gnn_Wk, "wv": L1_gnn_Wv, "wo": L1_gnn_Wo, "bo": L1_gnn_bo,
    }
    arrays = {f"in_{k}": np.ascontiguousarray(a) for k, a in arrays.items()}
    nc = bacc.Bacc("TRN2", target_bir_lowering=False, num_devices=1)
    ap = {k[3:]: nc.dram_tensor(k, a.shape, mybir.dt.from_np(a.dtype), kind="ExternalInput").ap() for k, a in arrays.items()}
    ap["out"] = nc.dram_tensor("out", (B, P, D), F32, kind="ExternalOutput").ap()
    build(nc, ap)
    r = run_bass_kernel_spmd(nc, [arrays], core_ids=[0])
    return r.results[0]["out"]
```

```python
from contextlib import ExitStack

import numpy as np

import concourse.bass as bass
from concourse import mybir
from concourse.alu_op_type import AluOpType as ALU

ACT = mybir.ActivationFunctionType
AX_X = mybir.AxisListType.X
F32 = mybir.dt.float32
F32R = mybir.dt.float32r
BF16 = mybir.dt.bfloat16
F16 = mybir.dt.float16
I32 = mybir.dt.int32
U8 = mybir.dt.uint8

P = 128
B, D = 128, 512
KT = D // P
QUAD = 4
GROUPS = B // QUAD
DH = 64
H0, H1 = 8, 4
PAIRS0, PAIRS1 = H0 // 2, H1 // 2
INNER = H1 * DH
HB = 4
VW = DH + 2
F16_SCALE = 2.0 ** 14
H_NORM2 = float(D)
EXPONENT_BITS = 0x7F800000
THRESHOLD = 0.1
SCALE = DH ** -0.5
LN_EPS = 1e-5
NORM_EPS2 = 1e-16
NEG0 = -1e10 / SCALE
FLOAT_MAX = 3.4028234e38
NEG1 = -3.3895e38
RSQRT_SEED = 1597463007.0
NEWTON = 3
THRESHOLD_SCALED = float(np.float32(THRESHOLD)) * F16_SCALE ** 2
EXCLUDED = 3e38
LN_OPS = 5 + 4 * NEWTON
SCALE_OPS = 3 + 4 * NEWTON
NORM_OPS = 3 + 4 * NEWTON
BASE = 2


def count(n):
    return BASE + n


def wait_apart(eng, sem, n, passed):
    eng.wait_ge(sem, n)
    eng.sem_inc(passed, 1)


def exists(g):
    return not isinstance(g, int) or g < GROUPS


def upcoming(t, par, u, steps):
    later, j = divmod(u + steps, QUAD)
    return t + 2 + later, (par + later) % 2, j, exists(t + 2 + later)


def chained(pool, sem, first, total, passed):
    done = [0]

    def link(ins, plain=False):
        ins.then_inc(sem, 1)
        done[0] += 1
        assert done[0] <= total
        if done[0] < total:
            if plain:
                wait_apart(pool, sem, first + done[0], passed)
            else:
                pool.wait_ge(sem, first + done[0])

    return link


def rsqrt_steps(nc, link, y, v, vh, a, minus_half, three_halves):
    tt = nc.gpsimd.tensor_tensor
    link(tt(vh, v, minus_half, ALU.mult), plain=True)
    link(nc.gpsimd.tensor_scalar(y.bitcast(I32), v.bitcast(I32), -0.5, RSQRT_SEED, ALU.mult, ALU.add))
    for _ in range(NEWTON):
        link(tt(a, y, y, ALU.mult))
        link(tt(a, a, vh, ALU.mult))
        link(tt(a, a, three_halves, ALU.add))
        link(tt(y, a, y, ALU.mult))


def row_stats(nc, dve, x, st, bn_done, first, passed):
    nc.vector.bn_stats(st[:, 0:6], x).then_inc(bn_done, 1)
    wait_apart(dve, bn_done, first + 1, passed)
    nc.vector.bn_aggr(st[:, 6:8], st[:, 0:6]).then_inc(bn_done, 1)


def layer_norm_factors(nc, pool, ln_chain, first, passed, st, consts):
    link = chained(pool, ln_chain, first, LN_OPS, passed)
    mean, var, vh, a, rstd, nbias = (st[:, :, n] for n in range(6, 12))
    minus_half, three_halves, eps, minus_one = (consts[:, n, 0:st.shape[1]] for n in range(4))
    tt = nc.gpsimd.tensor_tensor
    link(tt(var, var, eps, ALU.add))
    rsqrt_steps(nc, link, rstd, var, vh, a, minus_half, three_halves)
    link(tt(nbias, mean, rstd, ALU.mult))
    link(tt(nbias, nbias, minus_one, ALU.mult))


def first_factors(nc, pool, bn_done, ln_chain, g, ln_st, consts, passed):
    pool.wait_ge(bn_done, count(2 * QUAD * (g + 1)))
    layer_norm_factors(nc, pool, ln_chain, count(LN_OPS * QUAD * g), passed, ln_st[:], consts)
    pool.wait_ge(ln_chain, count(LN_OPS * (QUAD * g + 1)))
    pool.sem_inc(ln_chain, LN_OPS * (QUAD - 1))


def mask_scores(nc, dve, s_ready, n, passed, masked, scores, mask, negmax):
    wait_apart(dve, s_ready, n, passed)
    for hh in range(HB):
        last = nc.vector.tensor_tensor_reduce(masked[:, hh], scores[:, hh * P:(hh + 1) * P], mask, -1.0, FLOAT_MAX,
                                              ALU.add, ALU.min, negmax[:, hh:hh + 1])
    return last


def small_constants(nc, consts, sem):
    for n, value in enumerate((-0.5, 1.5, LN_EPS, -1.0)):
        ins = nc.gpsimd.memset(consts[:, n], value)
    ins.then_inc(sem, 1)


def rounds(eng, body, peeled=1):
    pairs = GROUPS // 2
    with eng.Fori(0, pairs - peeled) as i:
        body(i, 0, True, True)
        body(i, 1, True, True)
    for pair in range(pairs - peeled, pairs):
        last = pair == pairs - 1
        body(pair, 0, True, not last)
        body(pair, 1, not last, not last)


def split_products(pe, out, lhs_hi, lhs_lo, rhs_hi, rhs_lo, kts):
    last = None
    n = 0
    for kt in range(kts):
        for a, b in ((lhs_hi, rhs_hi), (lhs_hi, rhs_lo), (lhs_lo, rhs_hi)):
            last = pe.matmul(out, a(kt), b(kt), start=(n == 0), stop=(n == 3 * kts - 1))
            n += 1
    return last


def identity(nc, pool, matrix, s_ident):
    nc.gpsimd.memset(matrix, 0.0).then_inc(s_ident, 1)
    pool.wait_ge(s_ident, 1)
    nc.gpsimd.affine_select(out=matrix, in_=matrix, compare_op=ALU.not_equal, fill=1.0, base=0,
                            pattern=[[-1, P]], channel_multiplier=1).then_inc(s_ident, 1)


def layer0(nc, next_layer, next_weights, x, adj, map_w, map_wT, map_b, q_wT, q_b, k_wT, k_b, gmap_w, gmap_b, gcn_WT, x1):
    with ExitStack() as ctx:
        def sb(name, shape, dt=F32):
            return ctx.enter_context(nc.sbuf_tensor(name, shape, dt))

        def bank(name):
            return ctx.enter_context(nc.psum_tensor(name, [P, 512], F32))

        def sem(name):
            return ctx.enter_context(nc.semaphore(name))

        w_hi = {k: sb(f"w{k}_hi", [P, KT, D], F32R) for k in "qkmv"}
        w_lo = {k: sb(f"w{k}_lo", [P, KT, D], F32R) for k in "qkmv"}
        ident = next_layer["ident"]
        mb = sb("mb", [P, D])
        vb = sb("vb", [P, D])
        qb = sb("qb", [P, KT])
        kb = sb("kb", [P, KT])
        bcols = sb("bcols", [P, 4, KT])
        qk = next_layer["room"]
        q_sb = qk[:, 0:2 * KT * D].rearrange("p (g b n) -> p g b n", g=2, b=KT)
        k_bd = qk[:, 2 * KT * D:].rearrange("p (g b s n) -> p g b s n", g=2, b=KT, s=2)
        raw = [qk[:, n * KT * D:(n + 1) * KT * D].rearrange("p (k n) -> p k n", k=KT) for n in range(5)]
        raw_mapT, raw_map, raw_q, raw_k, raw_g = raw
        gw_bd = qk[:, 5 * KT * D:5 * KT * D + P]
        gb_rows = qk[:, 5 * KT * D + P:5 * KT * D + P + KT * P].rearrange("p (k n) -> p k n", k=KT)
        hT_hi = sb("hT_hi", [P, KT, QUAD * P], F32R)
        hT_lo = sb("hT_lo", [P, KT, QUAD * P], F32R)
        xg = next_layer["xg"]
        h = sb("h", [P, 2, D])
        ln_st = next_layer["ln_st"]
        m_sb = sb("m_sb", [P, QUAD, D])
        bias_rows = m_sb[:, 0:2]
        sq = sb("sq", [P, D])
        norm_st = sb("norm_st", [P, 4, H0])
        consts = sb("consts", [P, 4, H0])
        ones_col = sb("ones_col", [P, 1])
        nT = sb("nT", [P, 2, 2, KT, P], F16)
        nT_bd = sb("nT_bd", [P, 2, 2, KT, 2, P], F16)
        v32 = sb("v32", [P, D])
        v_hi = sb("v_hi", [P, QUAD + 1, H0 * VW], F16)
        v_lo = sb("v_lo", [P, QUAD + 1, H0 * VW], F16)
        v_st = sb("v_st", [P, 4])
        v_scale = sb("v_scale", [P, 2])
        exponent = sb("exponent", [P, 1], I32)
        ones = sb("ones", [P, P], BF16)
        mask_u8 = sb("mask_u8", [P, 2, QUAD, P], U8)
        mask = sb("mask", [P, 2, QUAD, P], BF16)
        bound = sb("bound", [P, 2, QUAD])
        negmax = sb("negmax", [P, 2, HB])
        zsum = sb("zsum", [P, 4, HB])
        probs = sb("probs", [P, HB, P])
        cprobs = sb("cprobs", [P, HB, P])
        cpT_hi = sb("cpT_hi", [P, HB, P], F16)
        cpT_lo = sb("cpT_lo", [P, HB, P], F16)
        epi_st = sb("epi_st", [P, 2, HB])
        xres = sb("xres", [P, 2, D])
        o_sb = sb("o_sb", [P, 2, D])
        w_squares = o_sb[:].rearrange("p a n -> p (a n)").bitcast(BF16).rearrange("p (k n) -> p k n", k=KT)

        ps_s, ps_c, ps_pt, ps_av = bank("ps_s"), bank("ps_c"), bank("ps_pt"), bank("ps_av")
        ps_pj = [bank("ps_pj0"), bank("ps_pj1")]
        ps_th, ps_tn = bank("ps_th"), bank("ps_tn")

        const_loaded, x_loaded = sem("const_loaded"), sem("x_loaded")
        mapT_loaded, map_loaded, q_loaded, k_loaded, g_loaded = (sem(f"{n}_loaded") for n in ("mapT", "map", "q", "k", "g"))
        mask_loaded = [sem(f"mask_loaded{n}") for n in range(2)]
        xres_loaded = [sem(f"xres_loaded{n}") for n in range(2)]
        o_stored = [sem(f"o_stored{n}") for n in range(2)]
        s_ident, prep_zero, prep_mm, prep_hi, prep_lo, prep_bias, prep_done = (
            sem(n) for n in ("s_ident", "prep_zero", "prep_mm", "prep_hi", "prep_lo", "prep_bias", "prep_done"))
        th_ready, tn_ready, pj_ready, s_ready, c_ready, pt_ready, av_ready = pe_sems = [
            sem(n) for n in ("th_ready", "tn_ready", "pj_ready", "s_ready", "c_ready", "pt_ready", "av_ready")]
        relu_done, hhi_done, q_done, ka_done, sq_done, nT_done, exp_done, cph_done, vhi_done = act_sems = [
            sem(n) for n in ("relu_done", "hhi_done", "q_done", "ka_done", "sq_done", "nT_done", "exp_done", "cph_done",
                             "vhi_done")]
        bn_done, sum_done, n_done, epi_chain, hlo_done, kb_done, m_done, v_done, nlo_done, nbd_done, negmax_done, cp_done, cpl_done = dve_sems = [
            sem(n) for n in ("bn_done", "sum_done", "n_done", "epi_chain", "hlo_done", "kb_done", "m_done", "v_done",
                             "nlo_done", "nbd_done", "negmax_done", "cp_done", "cpl_done")]
        passed_dve, passed_sp, passed_pool = sem("passed_dve"), sem("passed_sp"), sem("passed_pool")
        mask_ready, res_done, ln_chain, norm_chain, vlo_done = pool_sems = [
            sem(n) for n in ("mask_ready", "res_done", "ln_chain", "norm_chain", "vlo_done")]
        v_bound, scale_chain, scale_done, sq_w_done = (sem(n) for n in ("v_bound", "scale_chain", "scale_done", "sq_w_done"))
        EPI_OPS = 4
        BIAS_STEPS = 1 + 2 * KT + 4

        xt = x.rearrange("(g j) p d -> g p j d", j=QUAD)
        adjt = adj.rearrange("(g j) p d -> g p j d", j=QUAD)
        x1t = x1.rearrange("(g j) p d -> g j p d", j=QUAD)
        xrt = x.rearrange("(g j) p d -> g j p d", j=QUAD)

        def vslot(par, j):
            return j if j < QUAD - 1 else j + par

        block = ctx.enter_context(nc.Block())

        @block.sync
        def _(sp):
            def load_weight(dst, src, loaded):
                sp.dma_start(dst, src.rearrange("(k p) n -> p k n", p=P)).then_inc(loaded, 16)

            sp.dma_start(xg[:], xt[0]).then_inc(x_loaded, 16)
            load_weight(raw_map, map_w, map_loaded)
            load_weight(raw_q, q_wT, q_loaded)
            load_weight(raw_k, k_wT, k_loaded)
            sp.dma_start(mb[:], map_b.partition_broadcast(P)).then_inc(const_loaded, 16)
            for n, b in enumerate((map_b, q_b, k_b, gmap_b)):
                with nc.allow_non_contiguous_dma("512 floats, once"):
                    sp.dma_start(bcols[:, n, :], b.rearrange("(k p) -> p k", p=P)).then_inc(const_loaded, 16)
            sp.wait_ge(prep_zero, 2)
            for n in range(2):
                sp.dma_start(gw_bd[DH * n:DH * n + DH, DH * n:DH * n + DH], gcn_WT).then_inc(const_loaded, 16)
            load_weight(raw_g, gmap_w, g_loaded)
            load_weight(raw_mapT, map_wT, mapT_loaded)
            for n in range(2):
                sp.dma_start(mask_u8[:, n], adjt[n]).then_inc(mask_loaded[n], 16)
            sp.wait_ge(relu_done, count(QUAD))
            sp.dma_start(xg[:], xt[1]).then_inc(x_loaded, 16)

            def load_residual(t, j):
                wait_apart(sp, res_done, count(QUAD * t + j - 1), passed_sp)
                sp.dma_start(xres[:, j % 2], xrt[t, j]).then_inc(xres_loaded[j % 2], 16)

            load_residual(0, 0)

            def body(pair, par, proj, ahead):
                t = 2 * pair + par
                if ahead:
                    wait_apart(sp, relu_done, count(QUAD * (t + 2)), passed_sp)
                    sp.dma_start(xg[:], xt[t + 2]).then_inc(x_loaded, 16)
                    wait_apart(sp, mask_ready, count(t + 1), passed_sp)
                    sp.dma_start(mask_u8[:, par], adjt[t + 2]).then_inc(mask_loaded[par], 16)

                for j in range(QUAD):
                    if j + 1 < QUAD:
                        load_residual(t, j + 1)
                    elif proj:
                        load_residual(t + 1, 0)
                    if not proj and j == 0:
                        for n in range(2):
                            sp.wait_ge(o_stored[n], BASE + 16 * (QUAD // 2))
                        sp.wait_ge(relu_done, count(QUAD * GROUPS))
                        for n in range(QUAD):
                            sp.dma_start(xg[:, n], x1t[0, n]).then_inc(next_layer["x_loaded"][n], 16)
                        sp.wait_ge(s_ready, count(8 * (GROUPS - 1)))
                        for (dst, loaded), w in zip(next_layer["weights"], next_weights):
                            sp.dma_start(dst, w.rearrange("(k p) n -> p k n", p=P)).then_inc(loaded, 16)
                    wait_apart(sp, res_done, count(QUAD * t + j + 1), passed_sp)
                    sp.dma_start(x1t[t, j], o_sb[:, j % 2]).then_inc(o_stored[j % 2], 16)

            rounds(sp, body)
            for n in range(2):
                sp.wait_ge(o_stored[n], BASE + 16 * (B // 2))

        @block.gpsimd
        def _(pool):
            for s in (*pool_sems, *o_stored, next_layer["ln_chain"]):
                pool.sem_inc(s, BASE)
            nc.gpsimd.memset(gw_bd, 0.0).then_inc(prep_zero, 1)
            identity(nc, pool, ident[:], s_ident)
            nc.gpsimd.memset(nT_bd[:], 0.0)
            nc.gpsimd.memset(v_hi[:], 1.0)
            nc.gpsimd.memset(v_lo[:], 0.0)
            nc.gpsimd.memset(ones[:], 1.0)
            nc.gpsimd.memset(exponent[:], EXPONENT_BITS).then_inc(s_ident, 1)
            nc.gpsimd.memset(ones_col[:], 1.0)
            small_constants(nc, consts, s_ident)
            pool.wait_ge(s_ident, 4)

            def convert_mask(pair, par):
                t = 2 * pair + par
                pool.wait_ge(mask_loaded[par], 16 * (pair + 1))
                pool.wait_ge(negmax_done, count(2 * QUAD * (t - 1)) if not isinstance(t, int) or t else BASE)
                wait_apart(pool, epi_chain, count(EPI_OPS * 2 * QUAD * (t - 1)) if not isinstance(t, int) or t else BASE, passed_pool)
                nc.gpsimd.tensor_scalar(bound[:, par, :], mask_u8[:, par, :, 0], EXCLUDED, THRESHOLD_SCALED, ALU.mult, ALU.add)
                nc.gpsimd.tensor_scalar(mask[:, par], mask_u8[:, par], NEG0, None, ALU.mult).then_inc(mask_ready, 1)

            def factors(g, j):
                pool.wait_ge(bn_done, count(2 * (QUAD * g + j + 1)))
                layer_norm_factors(nc, pool, ln_chain, count(LN_OPS * (QUAD * g + j)), passed_pool, ln_st[:, j:j + 1], consts)


            def head_norms(g, j):
                wait_apart(pool, sum_done, count(QUAD * g + j + 1), passed_pool)
                n2, r, a, vh = (norm_st[:, n] for n in range(4))
                link = chained(pool, norm_chain, count(NORM_OPS * (QUAD * g + j)), NORM_OPS, passed_pool)
                link(nc.gpsimd.tensor_scalar(n2, n2, NORM_EPS2, None, ALU.max))
                rsqrt_steps(nc, link, r, n2, vh, a, consts[:, 0], consts[:, 1])

            def v_low(g, par, j):
                dst, high = (v[:, vslot(par, j)].rearrange("p (h c) -> p h c", h=H0)[:, :, 0:DH] for v in (v_lo, v_hi))
                pool.wait_ge(vhi_done, count(QUAD * g + j + 1))
                nc.gpsimd.tensor_tensor(dst, v32[:].rearrange("p (h c) -> p h c", h=H0), high,
                                        ALU.subtract).then_inc(vlo_done, 1)

            def add_residual(t, j):
                pool.wait_ge(xres_loaded[j % 2], 16 * (2 * t + j // 2 + 1))
                pool.wait_ge(epi_chain, count(EPI_OPS * (8 * t + 2 * j + 2)))
                nc.gpsimd.tensor_tensor(o_sb[:, j % 2], o_sb[:, j % 2], xres[:, j % 2], ALU.add).then_inc(res_done, 1)

            first_factors(nc, pool, bn_done, ln_chain, 0, ln_st, consts, passed_pool)
            convert_mask(0, 0)
            pool.wait_ge(prep_mm, 3 * KT + 2)
            pool.wait_ge(prep_lo, 4 * KT)
            pool.wait_ge(mask_ready, count(1))
            nc.gpsimd.memset(k_bd[DH:P, :, :, 0, :], 0.0).then_inc(prep_done, 1)
            pool.wait_ge(prep_done, 2)
            wait_apart(pool, v_bound, 3, passed_pool)
            link = chained(pool, scale_chain, 0, SCALE_OPS, passed_pool)
            bound2, y, tmp, half = (v_st[:, n:n + 1] for n in range(4))
            link(nc.gpsimd.tensor_scalar(bound2, bound2, 1e-30, None, ALU.max))
            rsqrt_steps(nc, link, y, bound2, half, tmp, consts[:, 0, 0:1], consts[:, 1, 0:1])
            first_factors(nc, pool, bn_done, ln_chain, 1, ln_st, consts, passed_pool)
            for j in range(3):
                head_norms(0, j)
                v_low(0, 0, j)

            def body(pair, par, proj, ahead):
                t = 2 * pair + par
                for u in range(8):
                    if u == 0:
                        v_low(t, par, 3)
                        head_norms(t, 3)
                    if proj and u == 0:
                        convert_mask(pair + par, 1 - par)
                    if proj and u in (5, 6, 7):
                        v_low(t + 1, 1 - par, u - 5)
                        head_norms(t + 1, u - 5)
                    if ahead and 1 <= u < 5:
                        factors(t + 2, u - 1)
                    if u % 2:
                        add_residual(t, u // 2)
                    if not proj and u == 5:
                        first_factors(nc, pool, next_layer["bn_done"], next_layer["ln_chain"], 0, ln_st, consts, passed_pool)

            rounds(pool, body)

        @block.scalar
        def _(act):
            for s in act_sems:
                act.sem_inc(s, BASE)
            def relu(g, j):
                act.wait_ge(ln_chain, count(LN_OPS * (QUAD * g + j + 1)))
                act.wait_ge(th_ready, count(QUAD * g + j - 1))
                nc.scalar.activation(h[:, j % 2], xg[:, j], ACT.Relu, bias=ln_st[:, j, 11:12],
                                     scale=ln_st[:, j, 10:11]).then_inc(relu_done, 1)

            def hT_high(g, j):
                act.wait_ge(th_ready, count(QUAD * g + j + 1))
                nc.scalar.copy(hT_hi[:, :, j * P:(j + 1) * P],
                               ps_th[:].rearrange("p (k n) -> p k n", k=KT)).then_inc(hhi_done, 1)

            def q_copy(g, par, b):
                act.wait_ge(pj_ready, count(16 * g + 2 * b + 1))
                nc.scalar.activation(q_sb[:, par, b], ps_pj[0][:], ACT.Identity, bias=qb[:, b:b + 1]).then_inc(q_done, 1)

            def k_copy(g, par, b):
                act.wait_ge(pj_ready, count(16 * g + 2 * b + 2))
                nc.scalar.activation(k_bd[0:DH, par, b, 0], ps_pj[1][0:DH, :], ACT.Identity,
                                     bias=kb[0:DH, b:b + 1]).then_inc(ka_done, 1)

            def square(g, j):
                act.wait_ge(m_done, count(QUAD * g + j + 1))
                act.wait_ge(sum_done, count(QUAD * g + j))
                nc.scalar.activation(sq[:], m_sb[:, j], ACT.Square).then_inc(sq_done, 1)

            def nT_copy(g, j):
                act.wait_ge(tn_ready, count(QUAD * g + j + 1))
                nc.scalar.activation(nT[:, j % 2, 0], ps_tn[:].rearrange("p (k n) -> p k n", k=KT), ACT.Copy,
                                     scale=F16_SCALE).then_inc(nT_done, 1)

            def v_high(g, par, j):
                act.wait_ge(v_done, count(QUAD * g + j + 1))
                dst = v_hi[:, vslot(par, j)].rearrange("p (h c) -> p h c", h=H0)[:, :, 0:DH]
                nc.scalar.copy(dst, v32[:].rearrange("p (h c) -> p h c", h=H0)).then_inc(vhi_done, 1)

            def exps(t, u, epilogues_behind=1):
                n = 8 * t + u
                act.wait_ge(negmax_done, count(n + 1))
                act.wait_ge(cp_done, count(n))
                act.wait_ge(epi_chain, count(EPI_OPS * (n - epilogues_behind))
                            if not isinstance(n, int) or n else BASE)
                for hh in range(HB):
                    last = nc.scalar.activation(probs[:, hh], probs[:, hh], ACT.Exp, bias=negmax[:, u % 2, hh:hh + 1], scale=-1.0,
                                                accum_out=zsum[:, u % 4, hh:hh + 1])
                last.then_inc(exp_done, 1)

            def cpT_high(t, u):
                n = 8 * t + u
                act.wait_ge(pt_ready, count(n + 1))
                act.wait_ge(av_ready, count(n))
                nc.scalar.activation(cpT_hi[:], ps_pt[:].rearrange("p (h n) -> p h n", h=HB), ACT.Copy,
                                     scale=F16_SCALE).then_inc(cph_done, 1)

            for n, kind in enumerate(["q"] * KT + ["k"] * KT + ["v"] * KT):
                if n < QUAD:
                    relu(0, n)
                    hT_high(0, n)
                act.wait_ge(prep_mm, n + 1)
                nc.scalar.activation(w_hi[kind][:, n % KT, :], ps_pj[n % 2][:], ACT.Copy,
                                     scale=SCALE if kind == "q" else 1.0).then_inc(prep_hi, 1)
            act.wait_ge(mapT_loaded, 16)
            nc.scalar.copy(w_hi["m"][:], raw_mapT).then_inc(prep_hi, 1)
            act.wait_ge(prep_hi, 3 * KT)
            nc.scalar.activation(w_squares, w_hi["v"][:].bitcast(F32), ACT.Square).then_inc(sq_w_done, 1)
            act.wait_ge(prep_bias, BIAS_STEPS)
            act.wait_ge(prep_done, 2)
            for b in range(KT):
                q_copy(0, 0, b)
                k_copy(0, 0, b)
            for j in range(QUAD):
                if j < 3:
                    square(0, j)
                relu(1, j)
                hT_high(1, j)
                if j < 3:
                    v_high(0, 0, j)
                if j == 1:
                    nT_copy(0, 0)
            exps(0, 0)

            def last_group(t, par):
                square(t, 3)
                v_high(t, par, 3)
                for u in range(8):
                    if u < 7:
                        exps(t, u + 1, epilogues_behind=2)
                    cpT_high(t, u)
                    if u in (0, 1, 3):
                        nT_copy(t, (0, 1, 3).index(u) + 1)

            def body(pair, par, proj, ahead):
                t = 2 * pair + par
                if not proj:
                    last_group(t, par)
                    return
                for u in range(8):
                    if proj and u < KT:
                        q_copy(t + 1, 1 - par, u)
                    cpT_high(t, u)
                    if u == 0:
                        square(t, 3)
                        v_high(t, par, 3)
                    if proj and u in (5, 6, 7):
                        square(t + 1, u - 5)
                    if u in (1, 3, 5):
                        nT_copy(t, (u + 1) // 2)
                    if proj and u == 7:
                        nT_copy(t + 1, 0)
                    if proj and u in (5, 6, 7):
                        v_high(t + 1, 1 - par, u - 5)
                    if ahead and u in (2, 3, 5, 6):
                        relu(t + 2, (2, 3, 5, 6).index(u))
                    if proj and u < KT:
                        k_copy(t + 1, 1 - par, u)
                    if ahead and u == 7:
                        hT_high(t + 2, 3)
                    if u < 7 or proj:
                        exps(t + (u + 1) // 8, (u + 1) % 8)
                    if ahead and 4 <= u < 7:
                        hT_high(t + 2, u - 4)

            rounds(act, body)

        @block.vector
        def _(dve):
            for s in (*dve_sems, next_layer["bn_done"]):
                dve.sem_inc(s, BASE)

            nc.vector.memset(gb_rows, 0.0).then_inc(prep_zero, 1)

            def stats(g, j):
                dve.wait_ge(x_loaded, 16 * (g + 1))
                row_stats(nc, dve, xg[:, j], ln_st[:, j], bn_done, count(2 * (QUAD * g + j)), passed_dve)

            def hT_low(g, j):
                dve.wait_ge(hhi_done, count(QUAD * g + j + 1))
                cols = slice(j * P, (j + 1) * P)
                nc.vector.tensor_tensor(hT_lo[:, :, cols], ps_th[:].rearrange("p (k n) -> p k n", k=KT),
                                        hT_hi[:, :, cols].bitcast(F32), ALU.subtract).then_inc(hlo_done, 1)

            def k_copy(g, par, b):
                dve.wait_ge(pj_ready, count(16 * g + 2 * b + 2))
                nc.vector.tensor_scalar(k_bd[DH:P, par, b, 1], ps_pj[1][DH:P, :], kb[DH:P, b:b + 1], None,
                                        ALU.add).then_inc(kb_done, 1)

            def m_copy(g, j):
                dve.wait_ge(pj_ready, count(16 * g + 8 + 2 * j + 1))
                nc.vector.tensor_tensor(m_sb[:, j], ps_pj[0][:], mb[:], ALU.add).then_inc(m_done, 1)

            def v_copy(g, par, j):
                dve.wait_ge(pj_ready, count(16 * g + 8 + 2 * j + 2))
                dve.wait_ge(vlo_done, count(QUAD * g + j))
                nc.vector.scalar_tensor_tensor(v32[:], ps_pj[1][:], v_scale[:, 0:1], vb[:], ALU.mult,
                                               ALU.add).then_inc(v_done, 1)

            def head_sums(g, j):
                dve.wait_ge(sq_done, count(QUAD * g + j + 1))
                nc.vector.tensor_reduce(norm_st[:, 0], sq[:].rearrange("p (h c) -> p h c", h=H0), AX_X,
                                        ALU.add).then_inc(sum_done, 1)

            def normalise(g, j):
                heads = m_sb[:, j].rearrange("p (h c) -> p h c", h=H0)
                dve.wait_ge(norm_chain, count(NORM_OPS * (QUAD * g + j + 1)))
                nc.vector.tensor_tensor(heads, heads, norm_st[:, 1].unsqueeze(2).to_broadcast([P, H0, DH]),
                                        ALU.mult).then_inc(n_done, 1)

            def nT_blocks(g, j):
                dve.wait_ge(nT_done, count(QUAD * g + j + 1))
                nc.vector.scalar_tensor_tensor(nT[:, j % 2, 1], ps_tn[:].rearrange("p (k n) -> p k n", k=KT), F16_SCALE,
                                               nT[:, j % 2, 0], ALU.mult, ALU.subtract).then_inc(nlo_done, 1)
                dve.wait_ge(nlo_done, count(QUAD * g + j + 1))
                nc.vector.tensor_copy(nT_bd[0:DH, j % 2, :, :, 0], nT[0:DH, j % 2])
                nc.vector.tensor_copy(nT_bd[DH:P, j % 2, :, :, 1], nT[DH:P, j % 2]).then_inc(nbd_done, 1)

            def row_max(t, par, u):
                if u == 0:
                    dve.wait_ge(mask_ready, count(t + 1))
                dve.wait_ge(cp_done, count(8 * t + u))
                mask_scores(nc, dve, s_ready, count(8 * t + u + 1), passed_dve, probs, ps_s, mask[:, par, u // 2],
                            negmax[:, u % 2]).then_inc(negmax_done, 1)

            def select_similar(t, par, u):
                n, j = 8 * t + u, u // 2
                dve.wait_ge(exp_done, count(n + 1))
                dve.wait_ge(c_ready, count(n + 1))
                dve.wait_ge(pt_ready, count(n))
                nc.vector.scalar_tensor_tensor(cprobs[:], ps_c[:].rearrange("p (h n) -> p h n", h=HB), 
                                               bound[:, par, j:j + 1], probs[:], ALU.is_gt, ALU.mult).then_inc(cp_done, 1)

            def cpT_low(t, u):
                dve.wait_ge(cph_done, count(8 * t + u + 1))
                nc.vector.scalar_tensor_tensor(cpT_lo[:], ps_pt[:].rearrange("p (h n) -> p h n", h=HB), F16_SCALE,
                                               cpT_hi[:], ALU.mult, ALU.subtract).then_inc(cpl_done, 1)

            def epilogue(t, u):
                n = 8 * t + u
                j, half = u // 2, u % 2
                first = count(EPI_OPS * n)
                av = ps_av[:].rearrange("p (h n) -> p h n", h=HB)
                den, rec = epi_st[:, 0], epi_st[:, 1]
                dve.wait_ge(av_ready, count(n + 1))
                nc.vector.scalar_tensor_tensor(den, zsum[:, u % 4], F16_SCALE, av[:, :, DH], ALU.mult,
                                               ALU.add).then_inc(epi_chain, 1)
                dve.wait_ge(epi_chain, first + 1)
                nc.vector.reciprocal(rec, den).then_inc(epi_chain, 1)
                dve.wait_ge(epi_chain, first + 2)
                nc.vector.tensor_scalar(rec, rec, v_scale[:, 1:2], None, ALU.mult).then_inc(epi_chain, 1)
                dve.wait_ge(epi_chain, first + 3)
                if half == 0:
                    dve.wait_ge(o_stored[j % 2], BASE + 16 * (2 * t + j // 2))
                dst = o_sb[:, j % 2, half * HB * DH:(half + 1) * HB * DH].rearrange("p (h c) -> p h c", h=HB)
                nc.vector.scalar_tensor_tensor(dst, av[:, :, 0:DH], 0.0, rec.unsqueeze(2).to_broadcast([P, HB, DH]),
                                               ALU.max, ALU.mult).then_inc(epi_chain, 1)

            for j in range(QUAD):
                stats(0, j)

            def mapped_bias(row, raw_w, first):
                nc.vector.tensor_scalar(row, raw_w[:, 0], bcols[:, 0, 0:1], None, ALU.mult).then_inc(prep_bias, 1)
                for kt in range(1, KT):
                    dve.wait_ge(prep_bias, first + kt)
                    nc.vector.scalar_tensor_tensor(row, raw_w[:, kt], bcols[:, 0, kt:kt + 1], row, ALU.mult,
                                                   ALU.add).then_inc(prep_bias, 1)

            for n, kind in enumerate(["q"] * KT + ["k"] * KT + ["v"] * KT):
                if n < QUAD:
                    hT_low(0, n)
                dve.wait_ge(prep_hi, n + 1)
                nc.vector.scalar_tensor_tensor(w_lo[kind][:, n % KT, :], ps_pj[n % 2][:],
                                               SCALE if kind == "q" else 1.0,
                                               w_hi[kind][:, n % KT, :].bitcast(F32), ALU.mult,
                                               ALU.subtract).then_inc(prep_lo, 1)
                if n == KT:
                    dve.wait_ge(const_loaded, 16 * 7)
                    dve.wait_ge(prep_zero, 2)
                    for b in range(KT):
                        ins = nc.vector.tensor_scalar(gb_rows[:, b], gb_rows[:, b], bcols[:, 3, b:b + 1], None, ALU.add)
                    ins.then_inc(prep_bias, 1)
                    mapped_bias(bias_rows[:, 0], raw_q, 1)
                if n == KT + 1:
                    mapped_bias(bias_rows[:, 1], raw_k, 1 + KT)
            dve.wait_ge(prep_hi, 3 * KT + 1)
            for kt in range(KT):
                nc.vector.tensor_tensor(w_lo["m"][:, kt], raw_mapT[:, kt], w_hi["m"][:, kt].bitcast(F32),
                                        ALU.subtract).then_inc(prep_lo, 1)
            dve.wait_ge(prep_mm, 3 * KT + 2)
            nc.vector.tensor_tensor(qb[:], ps_s[:, 0:KT], bcols[:, 1], ALU.add).then_inc(prep_bias, 1)
            nc.vector.tensor_tensor(kb[:], ps_s[:, KT:2 * KT], bcols[:, 2], ALU.add).then_inc(prep_bias, 1)
            dve.wait_ge(prep_bias, BIAS_STEPS - 2)
            nc.vector.tensor_scalar(qb[:], qb[:], SCALE, None, ALU.mult).then_inc(prep_bias, 1)
            nc.vector.tensor_copy(vb[:], ps_c[:]).then_inc(prep_bias, 1)
            dve.wait_ge(prep_bias, BIAS_STEPS)
            dve.wait_ge(prep_lo, 4 * KT)
            nc.vector.memset(k_bd[0:DH, :, :, 1, :], 0.0).then_inc(prep_done, 1)
            nc.vector.scalar_tensor_tensor(sq[:], vb[:], 4.0, vb[:], ALU.mult, ALU.mult).then_inc(v_bound, 1)
            dve.wait_ge(v_bound, 1)
            dve.wait_ge(prep_mm, 3 * KT + 3)
            nc.vector.scalar_tensor_tensor(sq[:], ps_pt[:], 4.0 * H_NORM2, sq[:], ALU.mult, ALU.add).then_inc(v_bound, 1)
            dve.wait_ge(v_bound, 2)
            nc.vector.tensor_reduce(v_st[:, 0:1], sq[:], AX_X, ALU.max).then_inc(v_bound, 1)
            for b in range(KT):
                k_copy(0, 0, b)
                if b == 1:
                    for j in range(QUAD):
                        stats(1, j)
            dve.wait_ge(scale_chain, SCALE_OPS)
            nc.vector.tensor_scalar(v_st[:, 1:2], v_st[:, 1:2], F16_SCALE, None, ALU.mult).then_inc(scale_done, 1)
            dve.wait_ge(scale_done, 1)
            nc.vector.tensor_tensor(v_scale[:, 0:1].bitcast(I32), v_st[:, 1:2].bitcast(I32), exponent[:],
                                    ALU.bitwise_and).then_inc(scale_done, 1)
            dve.wait_ge(scale_done, 2)
            nc.vector.reciprocal(v_scale[:, 1:2], v_scale[:, 0:1])
            nc.vector.tensor_scalar(vb[:], vb[:], v_scale[:, 0:1], None, ALU.mult).then_inc(scale_done, 1)
            dve.wait_ge(scale_done, 3)
            for j in range(QUAD):
                if 0 < j < 3:
                    normalise(0, j - 1)
                m_copy(0, j)
                if j < 3:
                    head_sums(0, j)
                v_copy(0, 0, j)
                hT_low(1, j)
                if j == 2:
                    nT_blocks(0, 0)
            row_max(0, 0, 0)

            def last_group(t, par):
                for u in range(8):
                    select_similar(t, par, u)
                    if u > 0:
                        cpT_low(t, u - 1)
                    if u < 7:
                        row_max(t, par, u + 1)
                    if u < 2:
                        normalise(t, 2 + u)
                    if u == 0:
                        head_sums(t, 3)
                    if u in (1, 2, 4):
                        nT_blocks(t, (1, 2, 4).index(u) + 1)
                    if u > 0:
                        epilogue(t, u - 1)
                    if 2 <= u < 2 + QUAD:
                        j = u - 2
                        dve.wait_ge(next_layer["x_loaded"][j], 16)
                        row_stats(nc, dve, xg[:, j], ln_st[:, j], next_layer["bn_done"], count(2 * j), passed_dve)
                cpT_low(t, 7)
                epilogue(t, 7)

            def body(pair, par, proj, ahead):
                t = 2 * pair + par
                dve.wait_ge(mask_ready, count(t + 1))
                if not proj:
                    last_group(t, par)
                    return
                for u in range(8):
                    select_similar(t, par, u)
                    if ahead and 1 <= u < 5:
                        stats(t + 2, u - 1)
                    if ahead and u >= 5:
                        hT_low(t + 2, u - 5)
                    if u < 2:
                        normalise(t, 2 + u)
                    if proj and u in (6, 7):
                        normalise(t + 1, u - 6)
                    if proj and u >= 4:
                        m_copy(t + 1, u - 4)
                    cpT_low(t, u)
                    if u == 0:
                        head_sums(t, 3)
                    if proj and u in (5, 6, 7):
                        head_sums(t + 1, u - 5)
                    if u in (1, 3, 5):
                        nT_blocks(t, (u + 1) // 2)
                    if proj and u == 7:
                        nT_blocks(t + 1, 0)
                    if proj and u < KT:
                        k_copy(t + 1, 1 - par, u)
                    if proj and u >= 4:
                        v_copy(t + 1, 1 - par, u - 4)
                    if ahead and u == 7:
                        hT_low(t + 2, 3)
                    if u < 7 or proj:
                        row_max(t + (u + 1) // 8, par if u < 7 else 1 - par, (u + 1) % 8)
                    epilogue(t, u)

            rounds(dve, body)

        @block.tensor
        def _(pe):
            for s in pe_sems:
                pe.sem_inc(s, BASE)
            def h_transpose(g, j):
                pe.wait_ge(relu_done, count(QUAD * g + j + 1))
                pe.wait_ge(hlo_done, count(QUAD * g + j))
                for kt in range(KT):
                    mm = nc.tensor.transpose(ps_th[:, kt * P:(kt + 1) * P], h[:, j % 2, kt * P:(kt + 1) * P], ident[:])
                mm.then_inc(th_ready, 1)

            def n_transpose(g, j):
                pe.wait_ge(n_done, count(QUAD * g + j + 1))
                pe.wait_ge(nlo_done, count(QUAD * g + j))
                for kt in range(KT):
                    mm = nc.tensor.transpose(ps_tn[:, kt * P:(kt + 1) * P], m_sb[:, j, kt * P:(kt + 1) * P], ident[:])
                mm.then_inc(tn_ready, 1)

            def by_channel(kind, b, out):
                cols = slice(b * P, (b + 1) * P)
                split_products(nc.tensor, out, lambda k: w_hi[kind][:, k, cols], lambda k: w_lo[kind][:, k, cols],
                               lambda k: hT_hi[:, k, :], lambda k: hT_lo[:, k, :], KT).then_inc(pj_ready, 1)

            def by_node(kind, j, out):
                cols = slice(j * P, (j + 1) * P)
                split_products(nc.tensor, out, lambda k: hT_hi[:, k, cols], lambda k: hT_lo[:, k, cols],
                               lambda k: w_hi[kind][:, k, :], lambda k: w_lo[kind][:, k, :], KT).then_inc(pj_ready, 1)

            def project_q(g, b):
                if b == 0:
                    pe.wait_ge(hlo_done, count(QUAD * g + QUAD))
                    pe.wait_ge(m_done, count(QUAD * g))
                else:
                    pe.wait_ge(q_done, count(QUAD * g + b))
                by_channel("q", b, ps_pj[0][:])

            def project_k(g, b):
                if b == 0:
                    pe.wait_ge(v_done, count(QUAD * g))
                else:
                    pe.wait_ge(ka_done, count(QUAD * g + b))
                    pe.wait_ge(kb_done, count(QUAD * g + b))
                by_channel("k", b, ps_pj[1][:])

            def project_m(g, j):
                if j == 0:
                    pe.wait_ge(q_done, count(QUAD * g + QUAD))
                else:
                    pe.wait_ge(m_done, count(QUAD * g + j))
                by_node("m", j, ps_pj[0][:])

            def project_v(g, j):
                if j == 0:
                    pe.wait_ge(ka_done, count(QUAD * g + QUAD))
                    pe.wait_ge(kb_done, count(QUAD * g + QUAD))
                else:
                    pe.wait_ge(v_done, count(QUAD * g + j))
                by_node("v", j, ps_pj[1][:])

            def scores(t, par, u):
                n = 8 * t + u
                j, half = u // 2, u % 2
                cols = slice(j * P, (j + 1) * P)
                if u == 0:
                    pe.wait_ge(q_done, count(QUAD * t + QUAD))
                    pe.wait_ge(ka_done, count(QUAD * t + QUAD))
                    pe.wait_ge(kb_done, count(QUAD * t + QUAD))
                pe.wait_ge(negmax_done, count(n))
                for pl in range(2):
                    pr = 2 * half + pl
                    mm = nc.tensor.matmul(ps_s[:, 2 * pl * P:2 * (pl + 1) * P].rearrange("p (h n) -> p h n", h=2), q_sb[:, par, pr, cols], k_bd[:, par, pr, :, cols],
                                          start=True, stop=True)
                mm.then_inc(s_ready, 1)
                pe.wait_ge(cp_done, count(n))
                if half == 0:
                    pe.wait_ge(nbd_done, count(QUAD * t + j + 1))
                for pl in range(2):
                    pr = 2 * half + pl
                    for n, (x_part, y_part) in enumerate(((0, 0), (0, 1), (1, 0))):
                        mm = nc.tensor.matmul(ps_c[:, 2 * pl * P:2 * (pl + 1) * P].rearrange("p (h n) -> p h n", h=2),
                                              nT[:, j % 2, x_part, pr, :], nT_bd[:, j % 2, y_part, pr],
                                              start=(n == 0), stop=(n == 2))
                mm.then_inc(c_ready, 1)

            def prob_transpose(t, u):
                n = 8 * t + u
                pe.wait_ge(cp_done, count(n + 1))
                pe.wait_ge(cpl_done, count(n))
                for hh in range(HB):
                    mm = nc.tensor.transpose(ps_pt[:, hh * P:(hh + 1) * P], cprobs[:, hh], ident[:])
                mm.then_inc(pt_ready, 1)

            def weigh_values(t, par, u):
                n = 8 * t + u
                j, half = u // 2, u % 2
                pe.wait_ge(cpl_done, count(n + 1))
                pe.wait_ge(epi_chain, count(EPI_OPS * n))
                pe.wait_ge(vlo_done, count(QUAD * t + j + 1))
                for hh in range(HB):
                    hd = HB * half + hh
                    for n, (probs_part, v_part) in enumerate(((cpT_hi, v_hi), (cpT_hi, v_lo), (cpT_lo, v_hi))):
                        mm = nc.tensor.matmul(ps_av[:, hh * P:hh * P + VW], probs_part[:, hh],
                                              v_part[:, vslot(par, j), hd * VW:(hd + 1) * VW], start=(n == 0), stop=(n == 2))
                mm.then_inc(av_ready, 1)

            pe.wait_ge(s_ident, 4)
            for n in range(3 * KT):
                if n < QUAD:
                    h_transpose(0, n)
                if n == 0:
                    pe.wait_ge(map_loaded, 16)
                    pe.wait_ge(q_loaded, 16)
                if n == KT:
                    pe.wait_ge(k_loaded, 16)
                if n == 2 * KT:
                    pe.wait_ge(g_loaded, 16)
                    pe.wait_ge(const_loaded, 16 * 7)
                if n >= 2:
                    pe.wait_ge(prep_lo, n - 1)
                out = ps_pj[n % 2]
                rows = slice((n % KT) * P, (n % KT + 1) * P)
                if n < 2 * KT:
                    rhs = raw_q if n < KT else raw_k
                    for mk in range(KT):
                        mm = nc.tensor.matmul(out[:], raw_map[:, mk, rows], rhs[:, mk, :], start=(mk == 0), stop=(mk == KT - 1))
                else:
                    for pr in range(PAIRS0):
                        mm = nc.tensor.matmul(out[:, pr * P:(pr + 1) * P], raw_g[:, pr, rows], gw_bd, start=True, stop=True)
                mm.then_inc(prep_mm, 1)
            pe.wait_ge(prep_bias, 1 + 2 * KT)
            for n in range(2 * KT):
                cols = slice((n % KT) * P, (n % KT + 1) * P)
                mm = nc.tensor.matmul(ps_s[:, n:n + 1], bias_rows[:, n // KT, cols], ones_col[:], start=True, stop=True)
            mm.then_inc(prep_mm, 1)
            for pr in range(PAIRS0):
                mm = nc.tensor.matmul(ps_c[:, pr * P:(pr + 1) * P], gb_rows[:, pr, :], gw_bd, start=True, stop=True)
            mm.then_inc(prep_mm, 1)
            pe.wait_ge(prep_lo, 3 * KT)
            for b in range(KT):
                project_q(0, b)
                project_k(0, b)
                if b == 0:
                    pe.wait_ge(sq_w_done, 1)
                    for kt in range(KT):
                        mm = nc.tensor.matmul(ps_pt[:], ones[:], w_squares[:, kt, :], start=(kt == 0), stop=(kt == KT - 1))
                    mm.then_inc(prep_mm, 1)
            pe.wait_ge(prep_lo, 4 * KT)
            for j in range(QUAD):
                project_m(0, j)
                project_v(0, j)
                if j == 1:
                    n_transpose(0, 0)
                h_transpose(1, j)
            scores(0, 0, 0)

            def last_group(t, par):
                for u in range(8):
                    if u < 7:
                        scores(t, par, u + 1)
                    prob_transpose(t, u)
                    if u in (0, 1, 3):
                        n_transpose(t, (0, 1, 3).index(u) + 1)
                    if u > 0:
                        weigh_values(t, par, u - 1)
                weigh_values(t, par, 7)

            def body(pair, par, proj, ahead):
                t = 2 * pair + par
                if not proj:
                    last_group(t, par)
                    return
                for u in range(8):
                    if proj and u < KT:
                        project_q(t + 1, u)
                    if proj and u >= KT:
                        project_m(t + 1, u - KT)
                    prob_transpose(t, u)
                    if u in (1, 3, 5):
                        n_transpose(t, (u + 1) // 2)
                    if proj and u == 7:
                        n_transpose(t + 1, 0)
                    if proj and u < KT:
                        project_k(t + 1, u)
                    if proj and u >= KT:
                        project_v(t + 1, u - KT)
                    if ahead and u == 7:
                        h_transpose(t + 2, 3)
                    if u < 7:
                        scores(t, par, u + 1)
                    elif proj:
                        scores(t + 1, 1 - par, 0)
                    weigh_values(t, par, u)
                    if ahead and 4 <= u < 7:
                        h_transpose(t + 2, u - 4)

            rounds(pe, body)


def layer1(nc, prepared, x1, adj, bo, out):
    with ExitStack() as ctx:
        def sb(name, shape, dt=F32):
            return ctx.enter_context(nc.sbuf_tensor("l1_" + name, shape, dt))

        def bank(name):
            return ctx.enter_context(nc.psum_tensor("l1_" + name, [P, 512], F32))

        def sem(name):
            return ctx.enter_context(nc.semaphore("l1_" + name))

        widths = {"q": (KT, INNER), "k": (KT, INNER), "v": (KT, INNER), "o": (PAIRS1, D)}
        w_hi = {k: sb(f"w{k}_hi", [P, *s], F32R) for k, s in widths.items()}
        w_lo = {k: sb(f"w{k}_lo", [P, *s], F32R) for k, s in widths.items()}
        raw = {k: dst for k, (dst, _) in zip("qkvo", prepared["weights"])}
        ident = prepared["ident"]
        bo_rows = sb("bo_rows", [P, D])
        q_sb = sb("q_sb", [P, 2, PAIRS1, QUAD * P])
        k_bd = sb("k_bd", [P, 2, PAIRS1, 2, QUAD * P])
        v_sb = sb("v_sb", [P, 2, QUAD, INNER])
        hT_hi = sb("hT_hi", [P, 2, KT, QUAD * P], F32R)
        hT_lo = sb("hT_lo", [P, 2, KT, QUAD * P], F32R)
        xg = prepared["xg"]
        h = sb("h", [P, 2, D])
        ln_st = prepared["ln_st"]
        consts = sb("consts", [P, 4, QUAD])
        mask_u8 = sb("mask_u8", [P, 2, QUAD, P], U8)
        mask = sb("mask", [P, 2, QUAD, P], BF16)
        negmax = sb("negmax", [P, 2, HB])
        zsum = sb("zsum", [P, 2, HB])
        rec = sb("rec", [P, HB])
        probs = sb("probs", [P, HB, P])
        nprobs = sb("nprobs", [P, HB, P])
        npT = sb("npT", [P, HB, P])
        aT_hi = sb("aT_hi", [P, PAIRS1, P], F32R)
        aT_lo = sb("aT_lo", [P, PAIRS1, P], F32R)
        xres = sb("xres", [P, 2, D])
        o_sb = sb("o_sb", [P, 2, D])

        ps_s, ps_pt, ps_av, ps_o, ps_th = bank("ps_s"), bank("ps_pt"), bank("ps_av"), bank("ps_o"), bank("ps_th")
        ps_pj = [bank("ps_pj0"), bank("ps_pj1")]

        raw_loaded = {k: loaded for k, (_, loaded) in zip("qkvo", prepared["weights"])}
        bo_loaded = sem("bo_loaded")
        x_loaded, bn_done, ln_chain = prepared["x_loaded"], prepared["bn_done"], prepared["ln_chain"]
        mask_loaded = [sem(f"mask_loaded{n}") for n in range(2)]
        xres_loaded = [sem(f"xres_loaded{n}") for n in range(2)]
        o_stored = [sem(f"o_stored{n}") for n in range(2)]
        s_consts, prep_hi, prep_lo, prep_zero = sem("s_consts"), sem("prep_hi"), sem("prep_lo"), sem("prep_zero")
        th_ready, qk_ready, vp_ready, s_ready, pt_ready, av_ready, o_ready = pe_sems = [
            sem(n) for n in ("th_ready", "qk_ready", "vp_ready", "s_ready", "pt_ready", "av_ready", "o_ready")]
        relu_done, hhi_done, q_done, ka_done, exp_done, npT_done, ahi_done = act_sems = [
            sem(n) for n in ("relu_done", "hhi_done", "q_done", "ka_done", "exp_done", "npT_done", "ahi_done")]
        hlo_done, kb_done, v_done, negmax_done, rec_done, np_done, alo_done, out_done = dve_sems = [
            sem(n) for n in ("hlo_done", "kb_done", "v_done", "negmax_done", "rec_done", "np_done", "alo_done", "out_done")]
        passed_dve, passed_sp, passed_pool = sem("passed_dve"), sem("passed_sp"), sem("passed_pool")
        mask_ready, res_ready = pool_sems = [sem("mask_ready"), sem("res_ready")]

        xt = x1.rearrange("(g j) p d -> g j p d", j=QUAD)
        xrt = x1.rearrange("(g j) p d -> g j p d", j=QUAD)
        adjt = adj.rearrange("(g j) p d -> g p j d", j=QUAD)
        outt = out.rearrange("(g j) p d -> g j p d", j=QUAD)

        block = ctx.enter_context(nc.Block())

        @block.sync
        def _(sp):
            for n in range(2):
                sp.dma_start(mask_u8[:, n], adjt[n]).then_inc(mask_loaded[n], 16)
            sp.dma_start(bo_rows[:], bo.partition_broadcast(P)).then_inc(bo_loaded, 16)
            for g in (1, 2):
                for j in range(QUAD):
                    sp.wait_ge(relu_done, count(QUAD * (g - 1) + j + 1))
                    sp.dma_start(xg[:, j], xt[g, j]).then_inc(x_loaded[j], 16)

            def load_residual(t, j):
                wait_apart(sp, out_done, count(QUAD * t + j - 1), passed_sp)
                sp.dma_start(xres[:, j % 2], xrt[t, j]).then_inc(xres_loaded[j % 2], 16)

            load_residual(0, 0)

            def body(pair, par, proj, ahead):
                t = 2 * pair + par
                if ahead:
                    wait_apart(sp, mask_ready, count(t + 1), passed_sp)
                    sp.dma_start(mask_u8[:, par], adjt[t + 2]).then_inc(mask_loaded[par], 16)

                for j in range(QUAD):
                    if ahead and exists(t + 3):
                        wait_apart(sp, relu_done, count(QUAD * (t + 2) + j + 1), passed_sp)
                        sp.dma_start(xg[:, j], xt[t + 3, j]).then_inc(x_loaded[j], 16)
                    if j + 1 < QUAD:
                        load_residual(t, j + 1)
                    elif proj:
                        load_residual(t + 1, 0)
                    wait_apart(sp, out_done, count(QUAD * t + j + 1), passed_sp)
                    sp.dma_start(outt[t, j], o_sb[:, j % 2]).then_inc(o_stored[j % 2], 16)

            rounds(sp, body, peeled=2)
            for n in range(2):
                sp.wait_ge(o_stored[n], BASE + 16 * (B // 2))

        @block.gpsimd
        def _(pool):
            for s in (*pool_sems, *o_stored):
                pool.sem_inc(s, BASE)
            small_constants(nc, consts, s_consts)
            pool.wait_ge(s_consts, 1)

            def convert_mask(pair, par):
                t = 2 * pair + par
                pool.wait_ge(mask_loaded[par], 16 * (pair + 1))
                wait_apart(pool, negmax_done, count(QUAD * (t - 1)) if not isinstance(t, int) or t else BASE, passed_pool)
                nc.gpsimd.tensor_scalar(mask[:, par], mask_u8[:, par], -NEG1, NEG1, ALU.mult, ALU.add).then_inc(mask_ready, 1)

            def factors(g, j):
                pool.wait_ge(bn_done, count(2 * (QUAD * g + j + 1)))
                layer_norm_factors(nc, pool, ln_chain, count(LN_OPS * (QUAD * g + j)), passed_pool, ln_st[:, j:j + 1], consts)


            convert_mask(0, 0)
            first_factors(nc, pool, bn_done, ln_chain, 1, ln_st, consts, passed_pool)
            factors(2, 0)
            pool.wait_ge(bo_loaded, 16)

            def body(pair, par, proj, ahead):
                t = 2 * pair + par
                for j in range(QUAD):
                    g, _, graph, there = upcoming(t, par, j, 1)
                    if there:
                        factors(g, graph)
                    if proj and j == 1:
                        convert_mask(pair + par, 1 - par)
                    pool.wait_ge(xres_loaded[j % 2], 16 * (2 * t + j // 2 + 1))
                    nc.gpsimd.tensor_tensor(xres[:, j % 2], xres[:, j % 2], bo_rows[:], ALU.add).then_inc(res_ready, 1)

            rounds(pool, body, peeled=2)

        @block.scalar
        def _(act):
            for s in act_sems:
                act.sem_inc(s, BASE)

            def relu(g, j):
                act.wait_ge(ln_chain, count(LN_OPS * (QUAD * g + j + 1)))
                act.wait_ge(th_ready, count(QUAD * g + j - 1))
                nc.scalar.activation(h[:, j % 2], xg[:, j], ACT.Relu, bias=ln_st[:, j, 11:12],
                                     scale=ln_st[:, j, 10:11]).then_inc(relu_done, 1)

            def hT_high(g, par, j):
                act.wait_ge(th_ready, count(QUAD * g + j + 1))
                nc.scalar.copy(hT_hi[:, par, :, j * P:(j + 1) * P],
                               ps_th[:].rearrange("p (k n) -> p k n", k=KT)).then_inc(hhi_done, 1)

            def qk_copy(g, par, c):
                act.wait_ge(qk_ready, count(QUAD * g + c + 1))
                if c % 2 == 0:
                    nc.scalar.copy(q_sb[:, par, c // 2], ps_pj[0][:]).then_inc(q_done, 1)
                else:
                    nc.scalar.copy(k_bd[0:DH, par, c // 2, 0], ps_pj[0][0:DH, :]).then_inc(ka_done, 1)

            def exps(t, u):
                n = QUAD * t + u
                act.wait_ge(negmax_done, count(n + 1))
                act.wait_ge(np_done, count(n))
                for hh in range(HB):
                    last = nc.scalar.activation(probs[:, hh], probs[:, hh], ACT.Exp, bias=negmax[:, u % 2, hh:hh + 1], scale=-1.0,
                                                accum_out=zsum[:, u % 2, hh:hh + 1])
                last.then_inc(exp_done, 1)

            def npT_copy(t, u):
                n = QUAD * t + u
                act.wait_ge(pt_ready, count(n + 1))
                act.wait_ge(av_ready, count(n))
                nc.scalar.copy(npT[:], ps_pt[:].rearrange("p (h n) -> p h n", h=HB)).then_inc(npT_done, 1)

            def aT_high(t, u):
                n = QUAD * t + u
                act.wait_ge(av_ready, count(n + 1))
                act.wait_ge(o_ready, count(n))
                nc.scalar.copy(aT_hi[:], ps_av[:, 0:PAIRS1 * P].rearrange("p (k n) -> p k n", k=PAIRS1)).then_inc(ahi_done, 1)

            for j, k in enumerate("qkvo"):
                relu(0, j)
                act.wait_ge(raw_loaded[k], 16)
                nc.scalar.activation(w_hi[k][:], raw[k], ACT.Copy, scale=SCALE if k == "q" else 1.0).then_inc(prep_hi, 1)
                hT_high(0, 0, j)
            for c in range(QUAD):
                qk_copy(0, 0, c)
                relu(1, c)
                hT_high(1, 1, c)
            relu(2, 0)
            exps(0, 0)
            hT_high(2, 0, 0)

            def body(pair, par, proj, ahead):
                t = 2 * pair + par
                for u in range(QUAD):
                    g, parity, j, there = upcoming(t, par, u, 1)
                    if proj:
                        qk_copy(t + 1, 1 - par, u)
                    npT_copy(t, u)
                    if there:
                        relu(g, j)
                    if proj:
                        aT_high(t, u)
                    if u < QUAD - 1 or proj:
                        exps(t + (u + 1) // QUAD, (u + 1) % QUAD)
                    if not proj:
                        aT_high(t, u)
                    if there:
                        hT_high(g, parity, j)

            rounds(act, body, peeled=2)

        @block.vector
        def _(dve):
            for s in dve_sems:
                dve.sem_inc(s, BASE)
            def stats(g, j):
                dve.wait_ge(x_loaded[j], 16 * (g + 1))
                row_stats(nc, dve, xg[:, j], ln_st[:, j], bn_done, count(2 * (QUAD * g + j)), passed_dve)

            def hT_low(g, par, j):
                dve.wait_ge(hhi_done, count(QUAD * g + j + 1))
                cols = slice(j * P, (j + 1) * P)
                nc.vector.tensor_tensor(hT_lo[:, par, :, cols], ps_th[:].rearrange("p (k n) -> p k n", k=KT),
                                        hT_hi[:, par, :, cols].bitcast(F32), ALU.subtract).then_inc(hlo_done, 1)

            def k_copy(g, par, c):
                dve.wait_ge(qk_ready, count(QUAD * g + c + 1))
                nc.vector.tensor_copy(k_bd[DH:P, par, c // 2, 1], ps_pj[0][DH:P, :]).then_inc(kb_done, 1)

            def v_copy(g, par, j):
                dve.wait_ge(vp_ready, count(QUAD * g + j + 1))
                nc.vector.tensor_copy(v_sb[:, par, j], ps_pj[1][:, 0:INNER]).then_inc(v_done, 1)

            def row_max(t, par, u):
                if u == 0:
                    dve.wait_ge(mask_ready, count(t + 1))
                dve.wait_ge(np_done, count(QUAD * t + u))
                mask_scores(nc, dve, s_ready, count(QUAD * t + u + 1), passed_dve, probs, ps_s, mask[:, par, u],
                            negmax[:, u % 2]).then_inc(negmax_done, 1)

            def normalise(t, u):
                n = QUAD * t + u
                dve.wait_ge(exp_done, count(n + 1))
                nc.vector.reciprocal(rec[:], zsum[:, u % 2]).then_inc(rec_done, 1)
                dve.wait_ge(rec_done, count(n + 1))
                dve.wait_ge(pt_ready, count(n))
                nc.vector.tensor_tensor(nprobs[:], probs[:], rec[:].unsqueeze(2).to_broadcast([P, HB, P]),
                                        ALU.mult).then_inc(np_done, 1)

            def aT_low(t, u):
                n = QUAD * t + u
                dve.wait_ge(ahi_done, count(n + 1))
                nc.vector.tensor_tensor(aT_lo[:], ps_av[:, 0:PAIRS1 * P].rearrange("p (k n) -> p k n", k=PAIRS1),
                                        aT_hi[:].bitcast(F32), ALU.subtract).then_inc(alo_done, 1)

            def add_residual(t, u):
                dve.wait_ge(o_ready, count(QUAD * t + u + 1))
                dve.wait_ge(res_ready, count(QUAD * t + u + 1))
                dve.wait_ge(o_stored[u % 2], BASE + 16 * (2 * t + u // 2))
                nc.vector.tensor_tensor(o_sb[:, u % 2], ps_o[:], xres[:, u % 2], ALU.add).then_inc(out_done, 1)

            for n, k in enumerate("qkvo"):
                dve.wait_ge(prep_hi, n + 1)
                nc.vector.scalar_tensor_tensor(w_lo[k][:], raw[k], SCALE if k == "q" else 1.0,
                                               w_hi[k][:].bitcast(F32), ALU.mult, ALU.subtract).then_inc(prep_lo, 1)
                hT_low(0, 0, n)
            for j in range(QUAD):
                stats(1, j)
            nc.vector.memset(k_bd[0:DH, :, :, 1], 0.0)
            nc.vector.memset(k_bd[DH:P, :, :, 0], 0.0).then_inc(prep_zero, 2)
            for j in range(QUAD):
                if j % 2:
                    k_copy(0, 0, j)
                v_copy(0, 0, j)
                hT_low(1, 1, j)
                if j == 2:
                    stats(2, 0)
            row_max(0, 0, 0)
            stats(2, 1)
            normalise(0, 0)
            hT_low(2, 0, 0)

            def body(pair, par, proj, ahead):
                t = 2 * pair + par
                for u in range(QUAD):
                    if proj and u % 2:
                        k_copy(t + 1, 1 - par, u)
                    if proj:
                        v_copy(t + 1, 1 - par, u)
                    following = (t + (u + 1) // QUAD, (u + 1) % QUAD)
                    if proj:
                        aT_low(t, u)
                    if u < QUAD - 1 or proj:
                        row_max(following[0], par if u < QUAD - 1 else 1 - par, following[1])
                    if not proj:
                        aT_low(t, u)
                    g, _, j, there = upcoming(t, par, u, 2)
                    if there:
                        stats(g, j)
                    if u < QUAD - 1 or proj:
                        normalise(*following)
                    g, parity, j, there = upcoming(t, par, u, 1)
                    if there:
                        hT_low(g, parity, j)
                    add_residual(t, u)

            rounds(dve, body, peeled=2)

        @block.tensor
        def _(pe):
            for s in pe_sems:
                pe.sem_inc(s, BASE)

            def h_transpose(g, j):
                pe.wait_ge(relu_done, count(QUAD * g + j + 1))
                pe.wait_ge(hlo_done, count(QUAD * g + j))
                for kt in range(KT):
                    mm = nc.tensor.transpose(ps_th[:, kt * P:(kt + 1) * P], h[:, j % 2, kt * P:(kt + 1) * P], ident[:])
                mm.then_inc(th_ready, 1)

            def project_qk(g, par, c):
                if c == 0:
                    pe.wait_ge(hlo_done, count(QUAD * g + QUAD))
                if c % 2 == 0:
                    pe.wait_ge(ka_done, count(2 * g + c // 2))
                    pe.wait_ge(kb_done, count(2 * g + c // 2))
                else:
                    pe.wait_ge(q_done, count(2 * g + c // 2 + 1))
                kind = "qk"[c % 2]
                cols = slice((c // 2) * P, (c // 2 + 1) * P)
                split_products(nc.tensor, ps_pj[0][:], lambda k: w_hi[kind][:, k, cols], lambda k: w_lo[kind][:, k, cols],
                               lambda k: hT_hi[:, par, k, :], lambda k: hT_lo[:, par, k, :], KT).then_inc(qk_ready, 1)

            def project_v(g, par, j):
                pe.wait_ge(hlo_done, count(QUAD * g + j + 1))
                pe.wait_ge(v_done, count(QUAD * g + j))
                cols = slice(j * P, (j + 1) * P)
                split_products(nc.tensor, ps_pj[1][:, 0:INNER], lambda k: hT_hi[:, par, k, cols], lambda k: hT_lo[:, par, k, cols],
                               lambda k: w_hi["v"][:, k, :], lambda k: w_lo["v"][:, k, :], KT).then_inc(vp_ready, 1)

            def scores(t, par, u):
                n = QUAD * t + u
                cols = slice(u * P, (u + 1) * P)
                if u == 0:
                    pe.wait_ge(q_done, count(2 * t + 2))
                    pe.wait_ge(ka_done, count(2 * t + 2))
                    pe.wait_ge(kb_done, count(2 * t + 2))
                pe.wait_ge(negmax_done, count(n))
                for pr in range(PAIRS1):
                    mm = nc.tensor.matmul(ps_s[:, 2 * pr * P:2 * (pr + 1) * P].rearrange("p (h n) -> p h n", h=2), q_sb[:, par, pr, cols], k_bd[:, par, pr, :, cols],
                                          start=True, stop=True)
                mm.then_inc(s_ready, 1)

            def prob_transpose(t, u):
                n = QUAD * t + u
                pe.wait_ge(np_done, count(n + 1))
                pe.wait_ge(npT_done, count(n))
                for hh in range(HB):
                    mm = nc.tensor.transpose(ps_pt[:, hh * P:(hh + 1) * P], nprobs[:, hh], ident[:])
                mm.then_inc(pt_ready, 1)

            def weigh_values(t, par, u):
                n = QUAD * t + u
                pe.wait_ge(npT_done, count(n + 1))
                pe.wait_ge(alo_done, count(n))
                pe.wait_ge(v_done, count(n + 1))
                for hh in range(HB):
                    rows = slice(DH * (hh % 2), DH * (hh % 2) + DH)
                    mm = nc.tensor.matmul(ps_av[rows, (hh // 2) * P:(hh // 2 + 1) * P],
                                          v_sb[:, par, u, hh * DH:(hh + 1) * DH], npT[:, hh], start=True, stop=True)
                mm.then_inc(av_ready, 1)

            def project_out(t, u):
                n = QUAD * t + u
                pe.wait_ge(alo_done, count(n + 1))
                pe.wait_ge(out_done, count(n))
                split_products(nc.tensor, ps_o[:], lambda k: aT_hi[:, k, :], lambda k: aT_lo[:, k, :],
                               lambda k: w_hi["o"][:, k, :], lambda k: w_lo["o"][:, k, :], PAIRS1).then_inc(o_ready, 1)

            for j in range(QUAD):
                h_transpose(0, j)
            for c in range(QUAD):
                if c < 2:
                    pe.wait_ge(prep_lo, c + 1)
                project_qk(0, 0, c)
                if c == 0:
                    pe.wait_ge(prep_lo, 3)
                project_v(0, 0, c)
                h_transpose(1, c)
            pe.wait_ge(prep_zero, 2)
            scores(0, 0, 0)
            h_transpose(2, 0)
            pe.wait_ge(prep_lo, 4)

            def body(pair, par, proj, ahead):
                t = 2 * pair + par
                for u in range(QUAD):
                    if proj:
                        project_qk(t + 1, 1 - par, u)
                    if not proj and u < QUAD - 1:
                        scores(t, par, u + 1)
                    prob_transpose(t, u)
                    if proj:
                        project_v(t + 1, 1 - par, u)
                    weigh_values(t, par, u)
                    if proj and u < QUAD - 1:
                        scores(t, par, u + 1)
                    elif proj:
                        scores(t + 1, 1 - par, 0)
                    g, _, j, there = upcoming(t, par, u, 1)
                    if there:
                        h_transpose(g, j)
                    project_out(t, u)

            rounds(pe, body, peeled=2)


def build(nc, ap):
    x1 = nc.dram_tensor("x1_scratch", (B, P, D), F32, kind="Internal").ap()
    with ExitStack() as ctx:
        room = ctx.enter_context(nc.sbuf_tensor("room", [P, 2 * KT * D + 2 * KT * 2 * D], F32))
        keys = 2 * KT * D
        spaces = [room[:, keys + n * KT * INNER:keys + (n + 1) * KT * INNER] for n in range(4)]
        prepared = {
            "room": room,
            "weights": [(spaces[n].rearrange("p (k n) -> p k n", k=k), ctx.enter_context(nc.semaphore(f"l1_w{n}_loaded")))
                        for n, k in enumerate((KT, KT, KT, PAIRS1))],
            "ident": ctx.enter_context(nc.sbuf_tensor("ident", [P, P], F32)),
            "xg": ctx.enter_context(nc.sbuf_tensor("xg", [P, QUAD, D], F32)),
            "ln_st": ctx.enter_context(nc.sbuf_tensor("ln_st", [P, QUAD, 12], F32)),
            "x_loaded": [ctx.enter_context(nc.semaphore(f"l1_x_loaded{j}")) for j in range(QUAD)],
            "bn_done": ctx.enter_context(nc.semaphore("l1_bn_done")),
            "ln_chain": ctx.enter_context(nc.semaphore("l1_ln_chain")),
        }
        layer0(nc, prepared, [ap["wq"], ap["wk"], ap["wv"], ap["wo"]], ap["x"], ap["adj"], ap["map_w"], ap["map_wT"], ap["map_b"], ap["q_wT"], ap["q_b"], ap["k_wT"], ap["k_b"],
               ap["gmap_w"], ap["gmap_b"], ap["gcn_WT"], x1)
        layer1(nc, prepared, x1, ap["adj"], ap["bo"], ap["out"])


def kernel(x, adj, L0_gnn_map_w, L0_gnn_map_b, L0_gnn_q_w, L0_gnn_q_b, L0_gnn_k_w, L0_gnn_k_b, L0_gnn_gcn_map_w,
           L0_gnn_gcn_map_b, L0_gnn_gcn_W, L1_gnn_Wq, L1_gnn_Wk, L1_gnn_Wv, L1_gnn_Wo, L1_gnn_bo):
    from concourse import bacc
    from concourse.bass_utils import run_bass_kernel_spmd

    arrays = {
        "x": x, "adj": adj, "map_w": L0_gnn_map_w, "map_wT": np.transpose(L0_gnn_map_w), "map_b": L0_gnn_map_b,
        "q_wT": np.transpose(L0_gnn_q_w), "q_b": L0_gnn_q_b, "k_wT": np.transpose(L0_gnn_k_w), "k_b": L0_gnn_k_b,
        "gmap_w": L0_gnn_gcn_map_w, "gmap_b": L0_gnn_gcn_map_b, "gcn_WT": np.transpose(L0_gnn_gcn_W),
        "wq": L1_gnn_Wq, "wk": L1_gnn_Wk, "wv": L1_gnn_Wv, "wo": L1_gnn_Wo, "bo": L1_gnn_bo,
    }
    arrays = {f"in_{k}": np.ascontiguousarray(a) for k, a in arrays.items()}
    nc = bacc.Bacc("TRN2", target_bir_lowering=False, num_devices=1)
    ap = {k[3:]: nc.dram_tensor(k, a.shape, mybir.dt.from_np(a.dtype), kind="ExternalInput").ap() for k, a in arrays.items()}
    ap["out"] = nc.dram_tensor("out", (B, P, D), F32, kind="ExternalOutput").ap()
    build(nc, ap)
    r = run_bass_kernel_spmd(nc, [arrays], core_ids=[0])
    return r.results[0]["out"]
```
